# Optimizing a Trainium2 kernel written in Bass

```python
import numpy as np
import jax
import jax.numpy as jnp

def _softmax(x, axis=-1):
    return jax.nn.softmax(x, axis=axis)

def _gelu(x):
    return jax.nn.gelu(x, approximate=True)

def _silu(x):
    return jax.nn.silu(x)

def _sigmoid(x):
    return jax.nn.sigmoid(x)

def _layernorm(x, axis=-1, eps=1e-05):
    m = jnp.mean(x, axis=axis, keepdims=True)
    v = jnp.var(x, axis=axis, keepdims=True)
    return (x - m) / jnp.sqrt(v + eps)

def _scatter_add(tgt, idx, src, axis=0):
    return tgt.at[idx].add(src)

def _segment_sum(src, seg, n):
    return jax.ops.segment_sum(src, seg, n)
kernel_name = 'mk_gnn_ffn_d2_gnn_r8_69eaba'

def setup_inputs(seed: int=0):
    np.random.seed(seed)
    _w = jnp.asarray

    def _rec_inputs():
        import jax
        import jax.numpy as jnp
        _gk = jax.random.key(seed)
        x = -0.0002117 + 1 * jax.random.normal(jax.random.fold_in(_gk, 1), (1250, 512), jnp.float32)
        src = jax.random.randint(jax.random.fold_in(_gk, 2), (40000,), 0, 1250, jnp.int32)
        dst = jnp.minimum((1250 * jax.random.uniform(jax.random.fold_in(_gk, 3), (40000,)) ** 2.0).astype(jnp.int32), 9999)
        _o = jnp.argsort(dst, stable=True)
        src = src[_o]
        dst = dst[_o]
        return (x, src, dst)
    x, src, dst = _rec_inputs()

    def _L0_gnn_setup():
        import jax, jax.numpy as jnp
        import numpy as np
        N_NODES = 6250
        N_EDGES = 100000
        D_IN = 512
        D_OUT = 512
        key = jax.random.key(seed)
        k1, k2, k3, k4, k5 = jax.random.split(key, 5)
        local_feats = jax.random.normal(k1, (N_NODES, D_IN), dtype=jnp.float32)
        src = jax.random.randint(k2, (N_EDGES,), 0, N_NODES, dtype=jnp.int64)
        dst = jax.random.randint(k3, (N_EDGES,), 0, N_NODES, dtype=jnp.int64)
        lim = (6.0 / (D_IN + D_OUT)) ** 0.5
        W_self = jax.random.uniform(k4, (D_OUT, D_IN), minval=-lim, maxval=lim, dtype=jnp.float32)
        W_neigh = jax.random.uniform(k5, (D_OUT, D_IN), minval=-lim, maxval=lim, dtype=jnp.float32)
        b = jnp.zeros((D_OUT,), dtype=jnp.float32)
        return {'local_feats': local_feats, 'src': src, 'dst': dst, 'layer': 0, 'W_self': W_self, 'W_neigh': W_neigh, 'b': b}
    _L0_gnn_all = _L0_gnn_setup()
    _L0_gnn_in = {k: v for k, v in _L0_gnn_all.items() if k in ('W_self', 'W_neigh', 'b')}
    del _L0_gnn_all

    def _L0_ffn_setup():
        import math
        import jax, jax.numpy as jnp
        import numpy as np
        B, T, D, FF, E = (32, 1024, 512, 256, 8)
        CAPACITY_FACTOR = 1.25
        CAP = int(math.ceil(CAPACITY_FACTOR * B * T / E))

        def _bank_residual(x2, Wr, br, W1, b1, W2, b2):
            N, d = x2.shape
            e = Wr.shape[1]
            logits = x2 @ Wr + br
            probs = jax.nn.softmax(logits, axis=-1)
            expert = jnp.argmax(probs, axis=-1)
            gate = jnp.take_along_axis(probs, expert[:, None], axis=-1)[:, 0]
            oneh = jax.nn.one_hot(expert, e, dtype=x2.dtype)
            pos = (jnp.cumsum(oneh, axis=0) * oneh).sum(-1).astype(jnp.int32) - 1
            keep = pos < CAP
            slot = expert.astype(jnp.int32) * CAP + jnp.minimum(pos, CAP - 1)
            xd = jnp.where(keep[:, None], x2, 0.0)
            buf = jnp.zeros((e * CAP, d), x2.dtype).at[slot].add(xd)
            buf = buf.reshape(e, CAP, d)
            h = jax.nn.gelu(jnp.einsum('ecd,edf->ecf', buf, W1) + b1[:, None, :], approximate=False)
            out = jnp.einsum('ecf,efd->ecd', h, W2) + b2[:, None, :]
            y = out.reshape(e * CAP, d)[slot]
            return y * (gate * keep.astype(x2.dtype))[:, None]
        key = jax.random.key(seed)
        ks = jax.random.split(key, 18)
        s = 0.02
        inp = {'x': jax.random.normal(ks[0], (B, T, D), dtype=jnp.float32), 'Wr_sp': jax.random.normal(ks[1], (D, E)) * s, 'br_sp': jnp.zeros((E,), jnp.float32), 'Wr_fq': jax.random.normal(ks[2], (D, E)) * s, 'br_fq': jnp.zeros((E,), jnp.float32), 'Ws1': jax.random.normal(ks[3], (D, FF)) * s, 'bs1': jnp.zeros((FF,), jnp.float32), 'Ws2': jax.random.normal(ks[4], (FF, D)) * s, 'bs2': jnp.zeros((D,), jnp.float32), 'W1_sp': jax.random.normal(ks[5], (E, D, FF)) * s, 'b1_sp': jnp.zeros((E, FF), jnp.float32), 'W2_sp': jax.random.normal(ks[6], (E, FF, D)) * s, 'b2_sp': jnp.zeros((E, D), jnp.float32), 'W1_fq': jax.random.normal(ks[7], (E, D, FF)) * s, 'b1_fq': jnp.zeros((E, FF), jnp.float32), 'W2_fq': jax.random.normal(ks[8], (E, FF, D)) * s, 'b2_fq': jnp.zeros((E, D), jnp.float32)}
        return inp
    _L0_ffn_all = _L0_ffn_setup()
    _L0_ffn_in = {k: v for k, v in _L0_ffn_all.items() if k in ('Wr_sp', 'br_sp', 'Wr_fq', 'br_fq', 'Ws1', 'bs1', 'Ws2', 'bs2', 'W1_sp', 'b1_sp', 'W2_sp', 'b2_sp', 'W1_fq', 'b1_fq', 'W2_fq', 'b2_fq')}
    del _L0_ffn_all

    def _L1_gnn_setup():
        import jax, jax.numpy as jnp
        import numpy as np
        from math import sqrt
        N_NODES = 6250
        N_EDGES = 50000
        D_EMB = 512
        HEADS = 8
        DK = 32
        DV = 32
        key = jax.random.key(seed)
        ks = jax.random.split(key, 8)
        x = jax.random.normal(ks[0], (N_NODES, D_EMB), dtype=jnp.float32)
        edge_index = jax.random.randint(ks[1], (2, N_EDGES), 0, N_NODES, dtype=jnp.int64)

        def lin(k, fan_in, fan_out):
            bound = 1.0 / sqrt(fan_in)
            kw, kb = jax.random.split(k)
            W = jax.random.uniform(kw, (fan_in, fan_out), minval=-bound, maxval=bound, dtype=jnp.float32)
            b = jax.random.uniform(kb, (fan_out,), minval=-bound, maxval=bound, dtype=jnp.float32)
            return (W, b)
        Wk, bk = lin(ks[2], D_EMB, HEADS * DK)
        Wq, bq = lin(ks[3], D_EMB, HEADS * DK)
        Wv, bv = lin(ks[4], D_EMB, HEADS * DV)
        Wa, ba = lin(ks[5], HEADS * DV, D_EMB)
        Wf, bf = lin(ks[6], D_EMB, D_EMB)
        return {'x': x, 'edge_index': edge_index, 'Wk': Wk, 'bk': bk, 'Wq': Wq, 'bq': bq, 'Wv': Wv, 'bv': bv, 'Wa': Wa, 'ba': ba, 'Wf': Wf, 'bf': bf}
    _L1_gnn_all = _L1_gnn_setup()
    _L1_gnn_in = {k: v for k, v in _L1_gnn_all.items() if k in ('Wk', 'bk', 'Wq', 'bq', 'Wv', 'bv', 'Wa', 'ba', 'Wf', 'bf')}
    del _L1_gnn_all

    def _L1_ffn_setup():
        import jax, jax.numpy as jnp
        import numpy as np
        MAX_THRESHOLD = 0.25
        B, S, D, E = (8, 512, 512, 8)
        key = jax.random.key(seed)
        ks = jax.random.split(key, 5)
        scale = 1.0 / np.sqrt(D)
        return {'inputs': jax.random.normal(ks[0], (B, S, D), dtype=jnp.float32), 'W_gate': jax.random.normal(ks[1], (D, E), dtype=jnp.float32) * scale, 'b_gate': jnp.zeros((E,), dtype=jnp.float32), 'W_thr': jax.random.normal(ks[2], (D, 1), dtype=jnp.float32) * scale, 'b_thr': jnp.zeros((1,), dtype=jnp.float32), 'W_exp': jax.random.normal(ks[3], (E, D, D), dtype=jnp.float32) * scale, 'b_exp': jnp.zeros((E, D), dtype=jnp.float32)}
    _L1_ffn_all = _L1_ffn_setup()
    _L1_ffn_in = {k: v for k, v in _L1_ffn_all.items() if k in ('W_gate', 'b_gate', 'W_thr', 'b_thr', 'W_exp', 'b_exp')}
    del _L1_ffn_all
    return {'x': x, 'src': src, 'dst': dst, 'L0_gnn_W_self': _L0_gnn_in['W_self'], 'L0_gnn_W_neigh': _L0_gnn_in['W_neigh'], 'L0_gnn_b': _L0_gnn_in['b'], 'L0_ffn_Wr_sp': _L0_ffn_in['Wr_sp'], 'L0_ffn_br_sp': _L0_ffn_in['br_sp'], 'L0_ffn_Wr_fq': _L0_ffn_in['Wr_fq'], 'L0_ffn_br_fq': _L0_ffn_in['br_fq'], 'L0_ffn_Ws1': _L0_ffn_in['Ws1'], 'L0_ffn_bs1': _L0_ffn_in['bs1'], 'L0_ffn_Ws2': _L0_ffn_in['Ws2'], 'L0_ffn_bs2': _L0_ffn_in['bs2'], 'L0_ffn_W1_sp': _L0_ffn_in['W1_sp'], 'L0_ffn_b1_sp': _L0_ffn_in['b1_sp'], 'L0_ffn_W2_sp': _L0_ffn_in['W2_sp'], 'L0_ffn_b2_sp': _L0_ffn_in['b2_sp'], 'L0_ffn_W1_fq': _L0_ffn_in['W1_fq'], 'L0_ffn_b1_fq': _L0_ffn_in['b1_fq'], 'L0_ffn_W2_fq': _L0_ffn_in['W2_fq'], 'L0_ffn_b2_fq': _L0_ffn_in['b2_fq'], 'L1_gnn_Wk': _L1_gnn_in['Wk'], 'L1_gnn_bk': _L1_gnn_in['bk'], 'L1_gnn_Wq': _L1_gnn_in['Wq'], 'L1_gnn_bq': _L1_gnn_in['bq'], 'L1_gnn_Wv': _L1_gnn_in['Wv'], 'L1_gnn_bv': _L1_gnn_in['bv'], 'L1_gnn_Wa': _L1_gnn_in['Wa'], 'L1_gnn_ba': _L1_gnn_in['ba'], 'L1_gnn_Wf': _L1_gnn_in['Wf'], 'L1_gnn_bf': _L1_gnn_in['bf'], 'L1_ffn_W_gate': _L1_ffn_in['W_gate'], 'L1_ffn_b_gate': _L1_ffn_in['b_gate'], 'L1_ffn_W_thr': _L1_ffn_in['W_thr'], 'L1_ffn_b_thr': _L1_ffn_in['b_thr'], 'L1_ffn_W_exp': _L1_ffn_in['W_exp'], 'L1_ffn_b_exp': _L1_ffn_in['b_exp']}

def reference(x, src, dst, L0_gnn_W_self, L0_gnn_W_neigh, L0_gnn_b, L0_ffn_Wr_sp, L0_ffn_br_sp, L0_ffn_Wr_fq, L0_ffn_br_fq, L0_ffn_Ws1, L0_ffn_bs1, L0_ffn_Ws2, L0_ffn_bs2, L0_ffn_W1_sp, L0_ffn_b1_sp, L0_ffn_W2_sp, L0_ffn_b2_sp, L0_ffn_W1_fq, L0_ffn_b1_fq, L0_ffn_W2_fq, L0_ffn_b2_fq, L1_gnn_Wk, L1_gnn_bk, L1_gnn_Wq, L1_gnn_bq, L1_gnn_Wv, L1_gnn_bv, L1_gnn_Wa, L1_gnn_ba, L1_gnn_Wf, L1_gnn_bf, L1_ffn_W_gate, L1_ffn_b_gate, L1_ffn_W_thr, L1_ffn_b_thr, L1_ffn_W_exp, L1_ffn_b_exp):
    import jax
    import jax.numpy as jnp

    def _L0_gnn_ref(local_feats, src, dst, layer, W_self, W_neigh, b):
        import jax, jax.numpy as jnp
        import numpy as np
        N_NODES = 6250
        N_EDGES = 100000
        D_IN = 512
        D_OUT = 512
        'DistSAGEConv forward: mean neighbor aggregation + fc_self + fc_neigh + bias + ReLU.\n            `layer` only selects which hop in the distributed impl; aggregation math is identical.\n            '
        n = local_feats.shape[0]
        msg = local_feats[src]
        agg = jax.ops.segment_sum(msg, dst, num_segments=n)
        deg = jax.ops.segment_sum(jnp.ones((src.shape[0],), local_feats.dtype), dst, num_segments=n)
        h_neigh = agg / jnp.maximum(deg, 1.0)[:, None]
        rst = local_feats @ W_self.T + h_neigh @ W_neigh.T + b
        return jax.nn.relu(rst)

    def _L0_ffn_ref(x, Wr_sp, br_sp, Wr_fq, br_fq, Ws1, bs1, Ws2, bs2, W1_sp, b1_sp, W2_sp, b2_sp, W1_fq, b1_fq, W2_fq, b2_fq):
        import math
        import jax, jax.numpy as jnp
        import numpy as np
        B, T, D, FF, E = (32, 1024, 512, 256, 8)
        CAPACITY_FACTOR = 1.25
        CAP = int(math.ceil(CAPACITY_FACTOR * B * T / E))

        def _bank_residual(x2, Wr, br, W1, b1, W2, b2):
            N, d = x2.shape
            e = Wr.shape[1]
            logits = x2 @ Wr + br
            probs = jax.nn.softmax(logits, axis=-1)
            expert = jnp.argmax(probs, axis=-1)
            gate = jnp.take_along_axis(probs, expert[:, None], axis=-1)[:, 0]
            oneh = jax.nn.one_hot(expert, e, dtype=x2.dtype)
            pos = (jnp.cumsum(oneh, axis=0) * oneh).sum(-1).astype(jnp.int32) - 1
            keep = pos < CAP
            slot = expert.astype(jnp.int32) * CAP + jnp.minimum(pos, CAP - 1)
            xd = jnp.where(keep[:, None], x2, 0.0)
            buf = jnp.zeros((e * CAP, d), x2.dtype).at[slot].add(xd)
            buf = buf.reshape(e, CAP, d)
            h = jax.nn.gelu(jnp.einsum('ecd,edf->ecf', buf, W1) + b1[:, None, :], approximate=False)
            out = jnp.einsum('ecf,efd->ecd', h, W2) + b2[:, None, :]
            y = out.reshape(e * CAP, d)[slot]
            return y * (gate * keep.astype(x2.dtype))[:, None]
        b, t, d = x.shape
        x2 = x.reshape(b * t, d)
        shared = jax.nn.gelu(x2 @ Ws1 + bs1, approximate=False) @ Ws2 + bs2
        y = shared
        y = y + _bank_residual(x2, Wr_sp, br_sp, W1_sp, b1_sp, W2_sp, b2_sp)
        y = y + _bank_residual(x2, Wr_fq, br_fq, W1_fq, b1_fq, W2_fq, b2_fq)
        return y.reshape(b, t, d)

    def _L1_gnn_ref(x, edge_index, Wk, bk, Wq, bq, Wv, bv, Wa, ba, Wf, bf):
        import jax, jax.numpy as jnp
        import numpy as np
        from math import sqrt
        N_NODES = 6250
        N_EDGES = 50000
        D_EMB = 512
        HEADS = 8
        DK = 32
        DV = 32
        N = x.shape[0]
        receivers, senders = (edge_index[0], edge_index[1])
        K = (x @ Wk + bk).reshape(N, HEADS, DK)
        Q = (x @ Wq + bq).reshape(N, HEADS, DK)
        V = (x @ Wv + bv).reshape(N, HEADS, DV)
        att = jnp.exp(jnp.einsum('ehd,ehd->eh', Q[receivers], K[senders]) / sqrt(DK))
        denom = jax.ops.segment_sum(att, receivers, num_segments=N)
        att = att / denom[receivers]
        msg = att[:, :, None] * V[senders]
        agg = jnp.zeros((N, HEADS, DV), dtype=V.dtype).at[receivers].add(msg)
        out = jax.nn.relu(agg).reshape(N, HEADS * DV)
        out = jax.nn.relu(out @ Wa + ba)
        out = jax.nn.relu(out @ Wf + bf)
        return x + out

    def _L1_ffn_ref(inputs, W_gate, b_gate, W_thr, b_thr, W_exp, b_exp):
        import jax, jax.numpy as jnp
        import numpy as np
        MAX_THRESHOLD = 0.25
        B, S, D, E = (8, 512, 512, 8)
        d = inputs.shape[-1]
        x = inputs.reshape(-1, d)
        gate_logits = jax.nn.softmax(x @ W_gate + b_gate, axis=-1)
        thresholds = jax.nn.sigmoid(x @ W_thr + b_thr) * MAX_THRESHOLD
        adapted = gate_logits - thresholds
        selected = (adapted >= 0).astype(x.dtype)
        weights = adapted * selected
        wsum = jnp.sum(weights, axis=-1, keepdims=True)
        wsum = jnp.where(wsum == 0, jnp.ones_like(wsum), wsum)
        weights = weights / wsum
        ex_out = jnp.einsum('td,edf->etf', x, W_exp) + b_exp[:, None, :]
        results = jnp.einsum('etf,te->tf', ex_out, weights)
        return results.reshape(inputs.shape[:-1] + (results.shape[-1],))
    edge_index = jnp.stack([src, dst])
    x = x + _L0_gnn_ref(_layernorm(x, axis=-1), src, dst, 0, L0_gnn_W_self, L0_gnn_W_neigh, L0_gnn_b)
    x = x + _L0_ffn_ref(_layernorm(x, axis=-1)[None], L0_ffn_Wr_sp, L0_ffn_br_sp, L0_ffn_Wr_fq, L0_ffn_br_fq, L0_ffn_Ws1, L0_ffn_bs1, L0_ffn_Ws2, L0_ffn_bs2, L0_ffn_W1_sp, L0_ffn_b1_sp, L0_ffn_W2_sp, L0_ffn_b2_sp, L0_ffn_W1_fq, L0_ffn_b1_fq, L0_ffn_W2_fq, L0_ffn_b2_fq)[0]
    x = x + _L1_gnn_ref(_layernorm(x, axis=-1), edge_index, L1_gnn_Wk, L1_gnn_bk, L1_gnn_Wq, L1_gnn_bq, L1_gnn_Wv, L1_gnn_bv, L1_gnn_Wa, L1_gnn_ba, L1_gnn_Wf, L1_gnn_bf)
    x = x + _L1_ffn_ref(_layernorm(x, axis=-1)[None], L1_ffn_W_gate, L1_ffn_b_gate, L1_ffn_W_thr, L1_ffn_b_thr, L1_ffn_W_exp, L1_ffn_b_exp)[0]
    return x

_drawn_inputs = setup_inputs


def setup_inputs(seed=0):
    import zlib

    import numpy as np

    out = dict(_drawn_inputs(seed))
    spreads = {'L0_gnn_b': (0.0, 0.1),
     'L0_ffn_br_sp': (0.0, 0.1),
     'L0_ffn_br_fq': (0.0, 0.1),
     'L0_ffn_bs1': (0.0, 0.1),
     'L0_ffn_bs2': (0.0, 0.1),
     'L0_ffn_b1_sp': (0.0, 0.1),
     'L0_ffn_b2_sp': (0.0, 0.1),
     'L0_ffn_b1_fq': (0.0, 0.1),
     'L0_ffn_b2_fq': (0.0, 0.1),
     'L1_ffn_b_gate': (0.0, 0.1),
     'L1_ffn_b_exp': (0.0, 0.1)}
    factors = {}
    for name, (base, spread) in spreads.items():
        noise = np.random.default_rng([zlib.crc32(name.encode()), seed]).standard_normal(out[name].shape)
        drawn = base * np.exp(spread * noise) if base else spread * noise
        out[name] = jnp.asarray(drawn.astype(out[name].dtype))
    for name, factor in factors.items():
        out[name] = (out[name] * factor).astype(out[name].dtype)
    return out
```

```python
from contextlib import ExitStack

import concourse.bass as bass
from concourse import mybir

F32 = mybir.dt.float32
F32R = mybir.dt.float32r
F16 = mybir.dt.float16
I32 = mybir.dt.int32
ALU = mybir.AluOpType
ACT = mybir.ActivationFunctionType
AX = mybir.AxisListType

N = 1250
D = 512
E = 40000
DUMPS = []
PT = 125
NT = N // PT
KD = D // 128
CHUNKS = [(0, 512), (512, 1024), (1024, N)]

WIN = 25
NWIN = N // WIN
CELLS = NT * WIN
EB = 512
NEB = (E + EB - 1) // EB
EC = EB // 128
TAIL = E - (NEB - 1) * EB
ROUND = 12582912.0
EPS = 1e-5


def chained(eng, sem):
    count = [0]

    def link(ins):
        count[0] += 1
        ins.then_inc(sem, 1)
        eng.wait_ge(sem, count[0])

    return link


class Semaphores:

    def __init__(self, nc):
        self.nc, self.used, self.stale = nc, [], []

    def new(self, ctx, name):
        handle = ctx.enter_context(self.nc.semaphore(name))
        self.used.append(handle)
        return handle

    def next_phase(self):
        self.used, self.stale = [], self.used

    def clear(self, pool):
        for handle in self.stale:
            pool.sem_clear(handle)


class Norm:

    def __init__(self, nc, sems, ctx, tag, X, H, hT_hi, hT_lo, ps, ident, eps_col):
        self.nc, self.X, self.H, self.hi, self.lo, self.ps, self.ident = nc, X, H, hT_hi, hT_lo, ps, ident
        self.eps_col = eps_col

        def sb(name, shape):
            return ctx.enter_context(nc.sbuf_tensor(f"{tag}_{name}", shape, F32))

        def sem(name):
            return sems.new(ctx, f"{tag}_{name}")

        self.stats = sb("stats", [PT, NT, 6])
        self.mv = sb("mv", [PT, NT, 2])
        self.sd = sb("sd", [PT, NT])
        self.rs = sb("rs", [PT, NT])
        self.t0 = sb("t0", [PT, NT])
        self.nmr = sb("nmr", [PT, NT])
        self.var_ready = sem("var_ready")
        self.sd_ready = sem("sd_ready")
        self.h_ready = sem("h_ready")
        self.turned = sem("turned")
        self.hi_ready = sem("hi_ready")
        self.lo_ready = sem("lo_ready")

    def vector(self, dve, link):
        nc = self.nc
        for t in range(NT):
            last = nc.vector.bn_stats(self.stats[:, t, :], self.X[:, t, :])
        link(last)
        for t in range(NT):
            last = nc.vector.bn_aggr(self.mv[:, t, :], self.stats[:, t, :])
        last.then_inc(self.var_ready, 1)
        dve.wait_ge(self.var_ready, 1)
        link(nc.vector.tensor_scalar(self.t0[:, :], self.mv[:, :, 1], EPS, -0.5, ALU.add, ALU.mult))
        dve.wait_ge(self.sd_ready, 1)
        link(nc.vector.reciprocal(self.rs[:, :], self.sd[:, :]))
        link(nc.vector.tensor_tensor(self.nmr[:, :], self.rs[:, :], self.rs[:, :], ALU.mult))
        link(nc.vector.tensor_tensor(self.nmr[:, :], self.nmr[:, :], self.t0[:, :], ALU.mult))
        link(nc.vector.scalar_tensor_tensor(self.rs[:, :], self.nmr[:, :], 1.5, self.rs[:, :], ALU.add, ALU.mult))
        link(nc.vector.scalar_tensor_tensor(self.nmr[:, :], self.mv[:, :, 0], -1.0, self.rs[:, :], ALU.mult, ALU.mult))
        for t in range(NT):
            nc.vector.tensor_scalar(self.H[:, t, :], self.X[:, t, :], self.rs[:, t:t + 1], self.nmr[:, t:t + 1],
                                    ALU.mult, ALU.add).then_inc(self.h_ready, 1)
        for t in range(NT):
            dve.wait_ge(self.hi_ready, t + 1)
            cols = slice(t * PT, (t + 1) * PT)
            nc.vector.tensor_tensor(self.lo[:, :, cols], self.ps[t % 2][:, :, 0:PT],
                                    self.hi[:, :, cols].bitcast(F32), ALU.subtract).then_inc(self.lo_ready, 1)

    def scalar(self, act):
        nc = self.nc
        act.wait_ge(self.var_ready, 1)
        nc.scalar.activation(self.sd[:, :], self.mv[:, :, 1], ACT.Sqrt, bias=self.eps_col[0:PT, :]).then_inc(self.sd_ready, 1)
        for t in range(NT):
            act.wait_ge(self.turned, t + 1)
            nc.scalar.activation(self.hi[:, :, t * PT:(t + 1) * PT], self.ps[t % 2][:, :, 0:PT],
                                 ACT.Copy).then_inc(self.hi_ready, 1)

    def tensor(self, pe):
        nc = self.nc
        for t in range(NT):
            pe.wait_ge(self.h_ready, t + 1)
            if t >= 2:
                pe.wait_ge(self.lo_ready, t - 1)
                pe.wait_ge(self.hi_ready, t - 1)
            for k in range(KD):
                last = nc.tensor.transpose(self.ps[t % 2][:, k, 0:PT], self.H[:, t, k * 128:(k + 1) * 128],
                                           self.ident[0:PT, 0:PT])
            last.then_inc(self.turned, 1)


def count_matrix_and_first_norm(nc, sems, a, X, H, hT_hi, hT_lo, ident, eps_col, CT):
    sems.next_phase()
    with ExitStack() as ctx:
        def sb(name, shape, dt=F32):
            return ctx.enter_context(nc.sbuf_tensor(name, shape, dt))

        def pb(name, shape, dt=F32):
            return ctx.enter_context(nc.psum_tensor(name, shape, dt))

        def sem(name):
            return sems.new(ctx, name)

        edges_i = sb("edges_i", [NEB, 2, EB], I32)
        edges_f = sb("edges_f", [NEB, 2, EB])
        reach = sb("reach", [NEB, 2])
        reach_b = sb("reach_b", [NEB, 2, NWIN])
        sender_tile = sb("sender_tile", [128, EC, NEB])
        sender_row = sb("sender_row", [128, EC, NEB])
        window = sb("window", [128, EC, NEB])
        cell = sb("cell", [128, EC, NEB])
        iota_b = sb("iota_b", [NWIN, NEB])
        win_first = sb("win_first", [NWIN, 1])
        meets = sb("meets", [NWIN, NEB])
        cand = sb("cand", [NWIN, 2, NEB])
        span = sb("span", [NWIN, 2])
        span_row = sb("span_row", [1, 2 * NWIN], I32)
        iota_c = sb("iota_c", [128, CELLS], F16)
        minus_first = sb("minus_first", [128, NWIN])
        rows1h = sb("rows1h", [128, EC, PT], F16)
        cells1h = sb("cells1h", [128, EC, CELLS], F16)
        zeros = sb("zeros", [128, CELLS], F16)
        ps_turn = [pb(f"ps_turn{i}", [128, 4, 128]) for i in range(2)]
        ps_span = pb("ps_span", [128, 512])
        ps_count = [pb(f"ps_count{i}", [PT, NT, WIN]) for i in range(2)]

        made = sem("made")
        edges_loaded = sem("edges_loaded")
        edges_ready = sem("edges_ready")
        reach_ready = sem("reach_ready")
        edges_turned = sem("edges_turned")
        edges_taken = sem("edges_taken")
        reach_spread = sem("reach_spread")
        span_ready = sem("span_ready")
        span_turned = sem("span_turned")
        span_known = sem("span_known")
        onehot_ready = sem("onehot_ready")
        onehot_used = sem("onehot_used")
        counted = sem("counted")
        copied = sem("copied")
        x_loaded = sem("x_loaded")
        dve_step = sem("dve_step")
        ln = Norm(nc, sems, ctx, "ln1", X, H, hT_hi, hT_lo, ps_turn, ident, eps_col)
        block = ctx.enter_context(nc.Block())

        @block.sync
        def _(sp):
            full = (NEB - 1) * EB
            for i, name in enumerate(("dst", "src")):
                sp.dma_start(edges_i[0:NEB - 1, i, :], a[name][0:full].rearrange("(b q) -> b q", q=EB)).then_inc(edges_loaded, 16)
                for j in range(EB // TAIL):
                    sp.dma_start(edges_i[NEB - 1:NEB, i, j * TAIL:(j + 1) * TAIL],
                                 a[name][full:E].rearrange("(b q) -> b q", b=1)).then_inc(edges_loaded, 16)
            for t in range(NT):
                sp.dma_start(X[:, t, :], a["x"][t * PT:(t + 1) * PT, :]).then_inc(x_loaded, 16)

        @block.gpsimd
        def _(pool):
            sems.clear(pool)
            nc.gpsimd.memset(ident[:, :], 0.0).then_inc(made, 1)
            nc.gpsimd.memset(eps_col[:, :], EPS).then_inc(made, 1)
            nc.gpsimd.memset(zeros[:, :], 0.0).then_inc(made, 1)
            nc.gpsimd.iota(iota_c[:, :], [[1, CELLS]], base=0, channel_multiplier=0,
                           allow_small_or_imprecise_dtypes=True).then_inc(made, 1)
            nc.gpsimd.iota(minus_first[:, :], [[-CELLS, NWIN]], base=0, channel_multiplier=0,
                           allow_small_or_imprecise_dtypes=True).then_inc(made, 1)
            nc.gpsimd.iota(iota_b[:, :], [[1, NEB]], base=0, channel_multiplier=0,
                           allow_small_or_imprecise_dtypes=True).then_inc(made, 1)
            nc.gpsimd.iota(win_first[:, :], [[1, 1]], base=0, channel_multiplier=WIN,
                           allow_small_or_imprecise_dtypes=True).then_inc(made, 1)
            pool.wait_ge(made, 1)
            nc.gpsimd.affine_select(out=ident[:, :], in_=ident[:, :], compare_op=ALU.not_equal, fill=1.0,
                                    base=0, pattern=[[-1, 128]], channel_multiplier=1).then_inc(made, 1)

        @block.vector
        def _(dve):
            link = chained(dve, dve_step)
            dve.wait_ge(edges_loaded, 32 * (1 + EB // TAIL))
            nc.vector.tensor_copy(edges_f[:, :, :], edges_i[:, :, :]).then_inc(edges_ready, 1)
            dve.wait_ge(edges_ready, 1)
            nc.vector.tensor_reduce(reach[:, 0:1], edges_f[:, 0, :], AX.X, ALU.min)
            link(nc.vector.tensor_reduce(reach[:, 1:2], edges_f[:, 0, :], AX.X, ALU.max))
            for i in range(2):
                last = nc.vector.tensor_scalar(reach_b[:, i, :], edges_f[:, 0, 0:NWIN], 0.0, reach[:, i:i + 1],
                                               ALU.mult, ALU.add)
            last.then_inc(reach_ready, 1)
            dve.wait_ge(edges_turned, 2)
            dst_t, src_t = (ps_turn[i][:, :, 0:NEB] for i in range(2))
            link(nc.vector.tensor_scalar(sender_tile[:, :, :], src_t, 1.0 / PT, -(PT // 2) / PT, ALU.mult, ALU.add))
            link(nc.vector.tensor_scalar(sender_tile[:, :, :], sender_tile[:, :, :], ROUND, -ROUND, ALU.add, ALU.add))
            link(nc.vector.scalar_tensor_tensor(sender_row[:, :, :], sender_tile[:, :, :], -float(PT), src_t, ALU.mult, ALU.add))
            link(nc.vector.tensor_scalar(window[:, :, :], dst_t, 1.0 / WIN, -(WIN // 2) / WIN, ALU.mult, ALU.add))
            link(nc.vector.tensor_scalar(window[:, :, :], window[:, :, :], ROUND, -ROUND, ALU.add, ALU.add))
            link(nc.vector.scalar_tensor_tensor(cell[:, :, :], window[:, :, :], float(CELLS - WIN), dst_t, ALU.mult, ALU.add))
            link(nc.vector.scalar_tensor_tensor(cell[:, :, :], sender_tile[:, :, :], float(WIN), cell[:, :, :], ALU.mult, ALU.add))
            first, used = TAIL // 128, TAIL % 128
            nc.vector.memset(cell[used:128, first, NEB - 1:NEB], -1.0e6)
            link(nc.vector.memset(cell[:, first + 1:EC, NEB - 1:NEB], -1.0e6))
            nc.vector.tensor_copy(window[0:1, 0, 0:1], cell[0:1, 0, 0:1]).then_inc(edges_taken, 1)
            dve.wait_ge(made, 8)
            dve.wait_ge(reach_spread, 1)
            low, high = ps_span[0:NWIN, 0:NEB], ps_span[0:NWIN, 128:128 + NEB]
            link(nc.vector.tensor_scalar(meets[:, :], high, win_first[:, :], None, ALU.is_ge))
            link(nc.vector.tensor_scalar(cand[:, 0, :], low, win_first[:, :], float(WIN - 1), ALU.subtract, ALU.is_le))
            link(nc.vector.tensor_tensor(meets[:, :], meets[:, :], cand[:, 0, :], ALU.mult))
            nc.vector.scalar_tensor_tensor(cand[:, 1, :], iota_b[:, :], 1.0, meets[:, :], ALU.add, ALU.mult)
            link(nc.vector.scalar_tensor_tensor(cand[:, 0, :], iota_b[:, :], -float(NEB), meets[:, :], ALU.add, ALU.mult))
            nc.vector.tensor_reduce(span[:, 1:2], cand[:, 1, :], AX.X, ALU.max)
            link(nc.vector.tensor_reduce(span[:, 0:1], cand[:, 0, :], AX.X, ALU.min))
            link(nc.vector.tensor_scalar(span[:, 0:1], span[:, 0:1], float(NEB), float(NEB - 1), ALU.add, ALU.min))
            nc.vector.scalar_tensor_tensor(span[:, 1:2], span[:, 0:1], 1.0, span[:, 1:2], ALU.add, ALU.max).then_inc(span_ready, 1)
            dve.wait_ge(span_turned, 1)
            nc.vector.tensor_copy(span_row[:, :], ps_span[0:1, 256:256 + 2 * NWIN]).then_inc(span_known, 1)
            dve.wait_ge(span_known, 1)
            dve.wait_ge(x_loaded, 16 * NT)
            ln.vector(dve, link)
            done = dve.alloc_register("dve_chunks")
            dve.reg_mov(done, 0)
            with dve.Fori(0, NWIN) as w:
                lo_b = dve.value_load(span_row[0:1, bass.DynSlice(w, 1)], min_val=0, max_val=NEB - 1)
                hi_b = dve.value_load(span_row[0:1, bass.DynSlice(w + NWIN, 1)], min_val=1, max_val=NEB)
                with dve.Fori(lo_b, hi_b) as b:
                    n = dve.snap(done, min_val=0, max_val=NWIN * NEB * EC)
                    for j in range(EC):
                        dve.wait_ge(onehot_used, n + (j + 1))
                        nc.vector.tensor_scalar(rows1h[:, j, :], iota_c[:, 0:PT], sender_row[:, j, bass.DynSlice(b, 1)],
                                                None, ALU.is_equal)
                        nc.vector.tensor_scalar(cells1h[:, j, :], iota_c[:, :], cell[:, j, bass.DynSlice(b, 1)],
                                                minus_first[:, bass.DynSlice(w, 1)],
                                                ALU.subtract, ALU.is_equal).then_inc(onehot_ready, 1)
                    dve.reg_add(done, done, EC)

        @block.tensor
        def _(pe):
            pe.wait_ge(made, 8)
            pe.wait_ge(edges_ready, 1)
            for i in range(2):
                for j in range(EC):
                    last = nc.tensor.transpose(ps_turn[i][:, j, 0:NEB], edges_f[:, i, j * 128:(j + 1) * 128],
                                               ident[0:NEB, 0:NEB])
                last.then_inc(edges_turned, 1)
            pe.wait_ge(reach_ready, 1)
            for i in range(2):
                last = nc.tensor.matmul(ps_span[0:NWIN, i * 128:i * 128 + NEB], reach_b[:, i, :], ident[0:NEB, 0:NEB],
                                        start=True, stop=True)
            last.then_inc(reach_spread, 1)
            pe.wait_ge(span_ready, 1)
            for i in range(2):
                last = nc.tensor.matmul(ps_span[0:1, 256 + i * NWIN:256 + (i + 1) * NWIN], span[:, i:i + 1],
                                        ident[0:NWIN, 0:NWIN], start=True, stop=True)
            last.then_inc(span_turned, 1)
            pe.wait_ge(edges_taken, 1)
            ln.tensor(pe)
            pe.wait_ge(span_known, 1)
            pe.sem_inc(onehot_used, EC)
            done = pe.alloc_register("pe_chunks")
            pe.reg_mov(done, 0)
            with pe.Fori(0, NWIN // 2) as pair:
                for half in range(2):
                    w = pair * 2 + half
                    ps = ps_count[half]
                    lo_b = pe.value_load(span_row[0:1, bass.DynSlice(w, 1)], min_val=0, max_val=NEB - 1)
                    hi_b = pe.value_load(span_row[0:1, bass.DynSlice(w + NWIN, 1)], min_val=1, max_val=NEB)
                    pe.wait_ge(copied, w + 1)
                    nc.tensor.matmul(ps[:, :, :], zeros[:, 0:PT], zeros[:, :], start=True, stop=False, skip_group_check=True)
                    with pe.Fori(lo_b, hi_b) as b:
                        n = pe.snap(done, min_val=0, max_val=NWIN * NEB * EC)
                        for j in range(EC):
                            pe.wait_ge(onehot_ready, n + (j + 1))
                            nc.tensor.matmul(ps[:, :, :], rows1h[:, j, :], cells1h[:, j, :], start=False, stop=False,
                                             skip_group_check=True).then_inc(onehot_used, 1)
                        pe.reg_add(done, done, EC)
                    nc.tensor.matmul(ps[:, 0, 0:2], zeros[:, 0:PT], zeros[:, 0:2], start=False, stop=True,
                                     skip_group_check=True).then_inc(counted, 1)

        @block.scalar
        def _(act):
            act.wait_ge(made, 8)
            ln.scalar(act)
            act.sem_inc(copied, 2)
            with act.Fori(0, NWIN // 2) as pair:
                for half in range(2):
                    w = pair * 2 + half
                    act.wait_ge(counted, w + 1)
                    nc.scalar.activation(CT[:, :, bass.DynSlice(w * WIN, WIN)], ps_count[half][:, :, :],
                                         ACT.Copy).then_inc(copied, 1)



def three(nc, out, a_hi, a_lo, b_hi, b_lo, start, stop):
    nc.tensor.matmul(out, a_lo, b_hi, start=start, stop=False)
    nc.tensor.matmul(out, a_hi, b_lo, start=False, stop=False)
    return nc.tensor.matmul(out, a_hi, b_hi, start=False, stop=stop)


def mean_aggregation(nc, sems, a, X, H, hT_hi, hT_lo, CT):
    GROUPS = [(0, 4), (4, 8), (8, NT)]
    sems.next_phase()
    with ExitStack() as ctx:
        def sb(name, shape, dt=F32):
            return ctx.enter_context(nc.sbuf_tensor(name, shape, dt))

        def pb(name, shape, dt=F32):
            return ctx.enter_context(nc.psum_tensor(name, shape, dt))

        def sem(name):
            return sems.new(ctx, name)

        w_raw = [sb(f"w_raw{i}", [128, KD, D]) for i in range(2)]
        w_hi = [sb(f"w_hi{i}", [128, KD, D], F32R) for i in range(2)]
        w_lo = [sb(f"w_lo{i}", [128, KD, D], F32R) for i in range(2)]
        agg_hi = sb("agg_hi", [128, KD, 4 * PT], F32R)
        agg_lo = sb("agg_lo", [128, KD, 4 * PT], F32R)
        bias = sb("bias", [PT, D])
        ones = sb("ones", [PT, 2])
        rdeg = sb("rdeg", [PT, NT])
        mean = [sb(f"mean{i}", [PT, D]) for i in range(2)]
        ps_agg = [pb(f"ps_agg{i}", [128, 512]) for i in range(2)]
        ps_self = [pb(f"ps_self{i}", [PT, D]) for i in range(2)]
        ps_neigh = [pb(f"ps_neigh{i}", [PT, D]) for i in range(2)]
        ps_deg = pb("ps_deg", [PT, 512])
        w_loaded = [sem(f"g_w_loaded{i}") for i in range(2)]
        bias_loaded = sem("g_bias_loaded")
        whi_ready = sem("g_whi_ready")
        wlo_ready = sem("g_wlo_ready")
        made = sem("g_made")
        deg_done = sem("deg_done")
        rdeg_ready = sem("rdeg_ready")
        agg_done = sem("agg_done")
        agghi_ready = sem("agghi_ready")
        agglo_ready = sem("agglo_ready")
        self_done = sem("self_done")
        neigh_done = sem("neigh_done")
        mean_ready = sem("mean_ready")
        summed = sem("g_summed")
        x_done = sem("g_x_done")
        step = sem("g_step")
        block = ctx.enter_context(nc.Block())

        @block.sync
        def _(sp):
            for i, name in enumerate(("L0_gnn_W_self", "L0_gnn_W_neigh")):
                sp.dma_start(w_raw[i][:, :, :], a[name].rearrange("(k p) n -> p k n", p=128)).then_inc(w_loaded[i], 16)
            sp.dma_start(bias[:, :], a["L0_gnn_b"].partition_broadcast(PT)).then_inc(bias_loaded, 16)

        @block.gpsimd
        def _(pool):
            sems.clear(pool)
            nc.gpsimd.memset(ones[:, :], 1.0).then_inc(made, 1)

        @block.scalar
        def _(act):
            for i in range(2):
                act.wait_ge(w_loaded[i], 16)
                nc.scalar.activation(w_hi[i][:, :, :], w_raw[i][:, :, :], ACT.Copy).then_inc(whi_ready, 1)
            act.wait_ge(rdeg_ready, 1)
            for g, (t0, t1) in enumerate(GROUPS):
                if t0:
                    act.wait_ge(neigh_done, t0)
                for f in range(KD):
                    act.wait_ge(agg_done, g * KD + f + 1)
                    nc.scalar.activation(agg_hi[:, f, 0:(t1 - t0) * PT], ps_agg[f % 2][:, 0:(t1 - t0) * PT],
                                         ACT.Copy).then_inc(agghi_ready, 1)
                for t in range(t0, t1):
                    act.wait_ge(neigh_done, t + 1)
                    if t >= 2:
                        act.wait_ge(summed, t - 1)
                    nc.scalar.activation(mean[t % 2][:, :], ps_neigh[t % 2][:, :], ACT.Copy,
                                         scale=rdeg[:, t:t + 1]).then_inc(mean_ready, 1)

        @block.vector
        def _(dve):
            link = chained(dve, step)
            for i in range(2):
                dve.wait_ge(w_loaded[i], 16)
                dve.wait_ge(whi_ready, i + 1)
                nc.vector.tensor_tensor(w_lo[i][:, :, :], w_raw[i][:, :, :], w_hi[i][:, :, :].bitcast(F32),
                                        ALU.subtract).then_inc(wlo_ready, 1)
            dve.wait_ge(deg_done, 1)
            link(nc.vector.tensor_scalar(rdeg[:, :], ps_deg[:, 0:NT], 1.0, None, ALU.max))
            nc.vector.reciprocal(rdeg[:, :], rdeg[:, :]).then_inc(rdeg_ready, 1)
            dve.wait_ge(bias_loaded, 16)
            for g, (t0, t1) in enumerate(GROUPS):
                for f in range(KD):
                    dve.wait_ge(agghi_ready, g * KD + f + 1)
                    nc.vector.tensor_tensor(agg_lo[:, f, 0:(t1 - t0) * PT], ps_agg[f % 2][:, 0:(t1 - t0) * PT],
                                            agg_hi[:, f, 0:(t1 - t0) * PT].bitcast(F32),
                                            ALU.subtract).then_inc(agglo_ready, 1)
                for t in range(t0, t1):
                    m = mean[t % 2]
                    dve.wait_ge(self_done, t + 1)
                    dve.wait_ge(mean_ready, t + 1)
                    link(nc.vector.tensor_tensor(m[:, :], m[:, :], ps_self[t % 2][:, :], ALU.add))
                    link(nc.vector.tensor_tensor(m[:, :], m[:, :], bias[:, :], ALU.add))
                    nc.vector.scalar_tensor_tensor(X[:, t, :], m[:, :], 0.0, X[:, t, :], ALU.max,
                                                   ALU.add).then_inc(summed, 1)

        @block.tensor
        def _(pe):
            pe.wait_ge(made, 1)
            for d in range(NT):
                for s in range(NT):
                    last = nc.tensor.matmul(ps_deg[:, d:d + 1], CT[:, s, d * PT:(d + 1) * PT], ones[:, 0:1],
                                            start=(s == 0), stop=(s == NT - 1))
            last.then_inc(deg_done, 1)
            for g, (t0, t1) in enumerate(GROUPS):
                for f in range(KD):
                    i = g * KD + f
                    if i >= 2:
                        pe.wait_ge(agglo_ready, i - 1)
                    for s in range(NT):
                        last = nc.tensor.matmul(ps_agg[f % 2][:, 0:(t1 - t0) * PT], H[:, s, f * 128:(f + 1) * 128],
                                                CT[:, s, t0 * PT:t1 * PT], start=(s == 0), stop=(s == NT - 1))
                    last.then_inc(agg_done, 1)
                for t in range(t0, t1):
                    if t == 0:
                        pe.wait_ge(wlo_ready, 1)
                    if t >= 2:
                        pe.wait_ge(summed, t - 1)
                    for k in range(KD):
                        tok = slice(t * PT, (t + 1) * PT)
                        last = three(nc, ps_self[t % 2][:, :], hT_hi[:, k, tok], hT_lo[:, k, tok],
                                     w_hi[0][:, k, :], w_lo[0][:, k, :], k == 0, k == KD - 1)
                    last.then_inc(self_done, 1)
                    if t == 0:
                        pe.wait_ge(wlo_ready, 2)
                    if t == t0:
                        pe.wait_ge(agglo_ready, (g + 1) * KD)
                    for k in range(KD):
                        tok = slice((t - t0) * PT, (t - t0 + 1) * PT)
                        last = three(nc, ps_neigh[t % 2][:, :], agg_hi[:, k, tok], agg_lo[:, k, tok],
                                     w_hi[1][:, k, :], w_lo[1][:, k, :], k == 0, k == KD - 1)
                    last.then_inc(neigh_done, 1)


NB = 2
NE = 8
NX = NB * NE
FF = 256
KF = FF // 128
FIRST_ROWS = 256
MORE_ROWS = 128
ROUNDS = (N - FIRST_ROWS + MORE_ROWS - 1) // MORE_ROWS
MORE_FROM = NX * FIRST_ROWS
ROWS = MORE_FROM + NB * ROUNDS * MORE_ROWS
BANKS = ("sp", "fq")


class Route:
    pass


def route_tensors(nc, ctx):
    r = Route()

    def sb(name, shape, dt=F32):
        return ctx.enter_context(nc.sbuf_tensor(name, shape, dt))

    r.gate = sb("gate", [PT, NT, NB])
    r.slot = sb("slot", [PT, NT, NB], I32)
    r.rounds = sb("rounds", [1, NX], I32)
    r.h_rows = nc.dram_tensor("h_rows", (N, D), F32).ap()
    r.y_rows = nc.dram_tensor("y_rows", (ROWS, D), F32).ap()
    r.token_of = nc.dram_tensor("token_of", (ROWS, 1), I32).ap()
    r.qk = nc.dram_tensor("qk_rows", (4, FF, N), F32).ap()
    return r


def route_and_shared_expert(nc, sems, a, X, H, hT_hi, hT_lo, ident, eps_col, r):
    UNITS = [(m, c) for m in range(KF) for c in range(len(CHUNKS))]
    sems.next_phase()
    with ExitStack() as ctx:
        def sb(name, shape, dt=F32):
            return ctx.enter_context(nc.sbuf_tensor(name, shape, dt))

        def pb(name, shape, dt=F32):
            return ctx.enter_context(nc.psum_tensor(name, shape, dt))

        def sem(name):
            return sems.new(ctx, "r_" + name)

        wr_raw = sb("wr_raw", [128, KD, NX])
        wr_hi = sb("wr_hi", [128, KD, NX], F32R)
        wr_lo = sb("wr_lo", [128, KD, NX], F32R)
        br = sb("br", [PT, NX])
        s_raw = sb("s_raw", [128, 2048])
        s_hi = sb("s_hi", [128, 2048], F32R)
        s_lo = sb("s_lo", [128, 2048], F32R)
        bs1 = sb("bs1", [128, KF])
        bs2 = sb("bs2", [PT, D])
        act1 = [sb(f"act1_{i}", [128, 512]) for i in range(2)]
        gT_hi = sb("gT_hi", [128, KF, N], F32R)
        gT_lo = sb("gT_lo", [128, KF, N], F32R)
        y = [sb(f"ys{i}", [PT, D]) for i in range(2)]
        logit = sb("logit", [PT, NT, NX])
        work = sb("work", [PT, NT, NX])
        prob = sb("prob", [PT, NT, NX])
        peak = sb("peak", [PT, NT * NB])
        onehot = sb("onehot", [PT, NT, NX])
        onehot16 = sb("onehot16", [PT, NT, NX], F16)
        slot_f = sb("slot_f", [PT, NT * NB])
        falling = sb("falling", [PT, NT * NB, NE])
        row0 = sb("row0", [PT, NT, NX])
        before = sb("before", [PT, NX])
        ones16 = sb("ones16", [PT, NX])
        jump = sb("jump", [PT, NX])
        zero_f = sb("zero_f", [128, D])
        upto = sb("upto", [PT, PT], F16)
        every = sb("every", [PT, PT], F16)
        zero_i = sb("zero_i", [128, ROWS // 128], I32)
        token = sb("token", [PT, NT], I32)
        more = sb("more", [PT, NX])
        kth = sb("kth", [PT, NX])
        ps_turn = [pb(f"r_turn{i}", [128, 4, 128]) for i in range(2)]
        ps_logit = pb("ps_logit", [PT, NT, NX])
        ps_rank = pb("ps_rank", [PT, 512])
        ps_up = [pb(f"ps_up{i}", [128, 512]) for i in range(2)]
        ps_down = [pb(f"ps_down{i}", [PT, D]) for i in range(2)]

        w_loaded, b_loaded = sem("w_loaded"), sem("b_loaded")
        whi_ready, wlo_ready = sem("whi_ready"), sem("wlo_ready")
        made, saved = sem("made"), sem("saved")
        logits_done, shifted, exped = sem("logits_done"), sem("shifted"), sem("exped")
        onehot_ready, ranked = sem("onehot_ready"), sem("ranked")
        slot_ready, cleared, scattered = sem("slot_ready"), sem("cleared"), sem("scattered")
        up_done, act_ready, ghi_ready, glo_ready = sem("up_done"), sem("act_ready"), sem("ghi_ready"), sem("glo_ready")
        down_done, y_ready, step = sem("down_done"), sem("y_ready"), sem("step")
        ln = Norm(nc, sems, ctx, "ln2", X, H, hT_hi, hT_lo, ps_turn, ident, eps_col)
        block = ctx.enter_context(nc.Block())
        w1 = (s_hi[:, 0:1024].rearrange("p (k f) -> p k f", k=KD), s_lo[:, 0:1024].rearrange("p (k f) -> p k f", k=KD))
        w2 = (s_hi[:, 1024:2048].rearrange("p (k f) -> p k f", k=KF), s_lo[:, 1024:2048].rearrange("p (k f) -> p k f", k=KF))

        @block.sync
        def _(sp):
            for b, bank in enumerate(BANKS):
                sp.dma_start(wr_raw[:, :, b * NE:(b + 1) * NE],
                             a[f"L0_ffn_Wr_{bank}"].rearrange("(k p) e -> p k e", p=128)).then_inc(w_loaded, 16)
                sp.dma_start(br[:, b * NE:(b + 1) * NE], a[f"L0_ffn_br_{bank}"].partition_broadcast(PT)).then_inc(b_loaded, 16)
            sp.dma_start(s_raw[:, 0:1024].rearrange("p (k f) -> p k f", k=KD),
                         a["L0_ffn_Ws1"].rearrange("(k p) f -> p k f", p=128)).then_inc(w_loaded, 16)
            sp.dma_start(s_raw[:, 1024:2048].rearrange("p (k f) -> p k f", k=KF),
                         a["L0_ffn_Ws2"].rearrange("(k p) f -> p k f", p=128)).then_inc(w_loaded, 16)
            sp.dma_start(bs1[:, :], a["L0_ffn_bs1"]).then_inc(b_loaded, 16)
            sp.dma_start(bs2[:, :], a["L0_ffn_bs2"].partition_broadcast(PT)).then_inc(b_loaded, 16)
            sp.wait_ge(made, 4)
            sp.dma_start(r.token_of.rearrange("(p f) o -> p (f o)", p=128), zero_i[:, :]).then_inc(cleared, 16)
            sp.dma_start(r.y_rows[MORE_FROM:ROWS, :].rearrange("(p i) d -> p i d", p=128),
                         zero_f[:, :].unsqueeze(1).to_broadcast([128, (ROWS - MORE_FROM) // 128, D])).then_inc(saved, 16)
            for t in range(NT):
                sp.wait_ge(ln.h_ready, t + 1)
                sp.dma_start(r.h_rows[t * PT:(t + 1) * PT, :], H[:, t, :]).then_inc(saved, 16)
            sp.wait_ge(saved, 16 * (NT + 1))

        @block.gpsimd
        def _(pool):
            sems.clear(pool)
            small = dict(allow_small_or_imprecise_dtypes=True)
            nc.gpsimd.memset(every[:, :], 1.0).then_inc(made, 1)
            nc.gpsimd.memset(zero_i[:, :], 0).then_inc(made, 1)
            nc.gpsimd.memset(zero_f[:, :], 0.0).then_inc(made, 1)
            nc.gpsimd.memset(ones16[:, :], 1.0).then_inc(made, 1)
            nc.gpsimd.iota(token[:, :], [[PT, NT]], base=0, channel_multiplier=1).then_inc(made, 1)
            nc.gpsimd.iota(falling[:, :, :], [[0, NT * NB], [-1, NE]], base=NE, channel_multiplier=0, **small).then_inc(made, 1)
            nc.gpsimd.iota(row0[:, :, :], [[0, NT], [FIRST_ROWS, NX]], base=-1, channel_multiplier=0, **small).then_inc(made, 1)
            pool.wait_ge(made, 2)
            nc.gpsimd.affine_select(out=upto[:, :], in_=every[:, :], compare_op=ALU.is_ge, fill=0.0,
                                    base=0, pattern=[[1, PT]], channel_multiplier=-1).then_inc(made, 1)
            pool.wait_ge(cleared, 16)
            pool.wait_ge(slot_ready, 1)
            pool.wait_ge(made, 8)
            for t in range(NT):
                for b in range(NB):
                    nc.gpsimd.indirect_dma_start(
                        out=r.token_of, out_offset=bass.IndirectOffsetOnAxis(ap=r.slot[:, t, b:b + 1], axis=0),
                        in_=token[:, t:t + 1], in_offset=None).then_inc(scattered, 16)
            pool.wait_ge(scattered, 16 * NT * NB)

        @block.scalar
        def _(act):
            ln.scalar(act)
            act.wait_ge(w_loaded, 64)
            nc.scalar.activation(wr_hi[:, :, :], wr_raw[:, :, :], ACT.Copy).then_inc(whi_ready, 1)
            nc.scalar.activation(s_hi[:, :], s_raw[:, :], ACT.Copy).then_inc(whi_ready, 1)
            act.wait_ge(shifted, 1)
            nc.scalar.activation(prob[:, :, :], logit[:, :, :], ACT.Exp).then_inc(exped, 1)
            act.wait_ge(b_loaded, 64)
            for u, (m, c) in enumerate(UNITS):
                c0, c1 = CHUNKS[c]
                act.wait_ge(up_done, u + 1)
                if u >= 2:
                    act.wait_ge(glo_ready, u - 1)
                nc.scalar.activation(act1[u % 2][:, 0:c1 - c0], ps_up[u % 2][:, 0:c1 - c0], ACT.Gelu,
                                     bias=bs1[:, m:m + 1]).then_inc(act_ready, 1)
                act.wait_ge(act_ready, u + 1)
                nc.scalar.activation(gT_hi[:, m, c0:c1], act1[u % 2][:, 0:c1 - c0], ACT.Copy).then_inc(ghi_ready, 1)

        @block.vector
        def _(dve):
            link = chained(dve, step)
            ln.vector(dve, link)
            dve.wait_ge(whi_ready, 2)
            nc.vector.tensor_tensor(wr_lo[:, :, :], wr_raw[:, :, :], wr_hi[:, :, :].bitcast(F32), ALU.subtract).then_inc(wlo_ready, 1)
            nc.vector.tensor_tensor(s_lo[:, :], s_raw[:, :], s_hi[:, :].bitcast(F32), ALU.subtract).then_inc(wlo_ready, 1)

            def banked(t):
                return t[:, :, :].rearrange("p t (b e) -> p (t b) e", b=NB)

            def spread(t):
                return t[:, :].unsqueeze(2).to_broadcast([PT, NT * NB, NE])

            dve.wait_ge(logits_done, 1)
            dve.wait_ge(b_loaded, 64)
            dve.wait_ge(made, 8)
            link(nc.vector.tensor_tensor(logit[:, :, :], ps_logit[:, :, :],
                                         br[:, :].unsqueeze(1).to_broadcast([PT, NT, NX]), ALU.add))
            link(nc.vector.tensor_reduce(peak[:, :], banked(logit), AX.X, ALU.max))
            nc.vector.tensor_tensor(banked(logit), banked(logit), spread(peak), ALU.subtract).then_inc(shifted, 1)
            dve.wait_ge(shifted, 1)
            link(nc.vector.scalar_tensor_tensor(banked(work), banked(logit), 0.0, falling[:, :, :], ALU.is_ge, ALU.mult))
            link(nc.vector.tensor_reduce(peak[:, :], banked(work), AX.X, ALU.max))
            link(nc.vector.tensor_tensor(banked(onehot), banked(work), spread(peak), ALU.is_equal))
            nc.vector.tensor_copy(onehot16[:, :, :], onehot[:, :, :]).then_inc(onehot_ready, 1)
            dve.wait_ge(exped, 1)
            link(nc.vector.tensor_reduce(peak[:, :], banked(prob), AX.X, ALU.add))
            link(nc.vector.reciprocal(r.gate[:, :, :].rearrange("p t b -> p (t b)"), peak[:, :]))
            dve.wait_ge(ranked, 1)
            total = ps_rank[:, NT * NX:(NT + 1) * NX]
            link(nc.vector.tensor_scalar(more[:, :], total, float(FIRST_ROWS), None, ALU.is_gt))
            for k in range(1, ROUNDS):
                link(nc.vector.tensor_scalar(kth[:, :], total, float(FIRST_ROWS + k * MORE_ROWS), None, ALU.is_gt))
                link(nc.vector.tensor_tensor(more[:, :], more[:, :], kth[:, :], ALU.add))
            nc.vector.tensor_copy(r.rounds[:, :], more[0:1, :])
            link(nc.vector.tensor_tensor_scan(before[:, :], ones16[:, :], more[:, :], 0.0, ALU.mult, ALU.add))
            link(nc.vector.tensor_tensor(before[:, :], before[:, :], more[:, :], ALU.subtract))
            link(nc.vector.tensor_scalar(before[:, :], before[:, :], float(MORE_ROWS), float(MORE_FROM - FIRST_ROWS - 1),
                                         ALU.mult, ALU.add))
            link(nc.vector.tensor_tensor(jump[:, :], before[:, :], row0[:, 0, :], ALU.subtract))
            upto_now = ps_rank[:, 0:NT * NX].rearrange("p (t e) -> p t e", e=NX)
            link(nc.vector.tensor_scalar(work[:, :, :], upto_now, float(FIRST_ROWS), None, ALU.is_gt))
            link(nc.vector.tensor_tensor(work[:, :, :], work[:, :, :], jump[:, :].unsqueeze(1).to_broadcast([PT, NT, NX]), ALU.mult))
            link(nc.vector.tensor_tensor(work[:, :, :], work[:, :, :], upto_now, ALU.add))
            link(nc.vector.tensor_tensor(work[:, :, :], work[:, :, :], row0[:, :, :], ALU.add))
            link(nc.vector.tensor_tensor(work[:, :, :], work[:, :, :], onehot[:, :, :], ALU.mult))
            link(nc.vector.tensor_reduce(slot_f[:, :], banked(work), AX.X, ALU.add))
            nc.vector.tensor_copy(r.slot[:, :, :].rearrange("p t b -> p (t b)"), slot_f[:, :]).then_inc(slot_ready, 1)
            for u, (m, c) in enumerate(UNITS):
                c0, c1 = CHUNKS[c]
                dve.wait_ge(ghi_ready, u + 1)
                nc.vector.tensor_tensor(gT_lo[:, m, c0:c1], act1[u % 2][:, 0:c1 - c0], gT_hi[:, m, c0:c1].bitcast(F32),
                                        ALU.subtract).then_inc(glo_ready, 1)
            for t in range(NT):
                dve.wait_ge(down_done, t + 1)
                nc.vector.tensor_tensor(y[t % 2][:, :], ps_down[t % 2][:, :], bs2[:, :], ALU.add).then_inc(y_ready, 1)
                dve.wait_ge(y_ready, t + 1)
                link(nc.vector.tensor_tensor(X[:, t, :], X[:, t, :], y[t % 2][:, :], ALU.add))

        @block.tensor
        def _(pe):
            ln.tensor(pe)
            pe.wait_ge(wlo_ready, 2)
            pe.wait_ge(ln.lo_ready, NT)
            for t in range(NT):
                tok = slice(t * PT, (t + 1) * PT)
                for k in range(KD):
                    last = three(nc, ps_logit[:, t, :], hT_hi[:, k, tok], hT_lo[:, k, tok], wr_hi[:, k, :], wr_lo[:, k, :],
                                 k == 0, k == KD - 1)
            last.then_inc(logits_done, 1)
            for u, (m, c) in enumerate(UNITS):
                c0, c1 = CHUNKS[c]
                if u >= 2:
                    pe.wait_ge(act_ready, u - 1)
                for k in range(KD):
                    ms = slice(m * 128, (m + 1) * 128)
                    last = three(nc, ps_up[u % 2][:, 0:c1 - c0], w1[0][:, k, ms], w1[1][:, k, ms],
                                 hT_hi[:, k, c0:c1], hT_lo[:, k, c0:c1], k == 0, k == KD - 1)
                last.then_inc(up_done, 1)
                if u == 1:
                    pe.wait_ge(onehot_ready, 1)
                    pe.wait_ge(made, 8)
                    for t in range(NT + 1):
                        for q in range(min(t + 1, NT)):
                            lhs = upto if q == t else every
                            last = nc.tensor.matmul(ps_rank[:, t * NX:(t + 1) * NX], lhs[:, :], onehot16[:, q, :],
                                                    start=(q == 0), stop=(q == min(t, NT - 1)))
                    last.then_inc(ranked, 1)
            pe.wait_ge(glo_ready, len(UNITS))
            for t in range(NT):
                tok = slice(t * PT, (t + 1) * PT)
                if t >= 2:
                    pe.wait_ge(y_ready, t - 1)
                for k in range(KF):
                    last = three(nc, ps_down[t % 2][:, :], gT_hi[:, k, tok], gT_lo[:, k, tok], w2[0][:, k, :], w2[1][:, k, :],
                                 k == 0, k == KF - 1)
                last.then_inc(down_done, 1)


def expert_weights(a, x):
    bank, e = BANKS[x // NE], x % NE
    return (a[f"L0_ffn_W1_{bank}"][e].rearrange("(k p) f -> p k f", p=128),
            a[f"L0_ffn_W2_{bank}"][e].rearrange("(k p) f -> p k f", p=128), a[f"L0_ffn_b2_{bank}"][e])


def routed_experts(nc, sems, a, ident, r):
    ST = FIRST_ROWS // 128
    sems.next_phase()
    with ExitStack() as ctx:
        def sb(name, shape, dt=F32):
            return ctx.enter_context(nc.sbuf_tensor(name, shape, dt))

        def pb(name, shape, dt=F32):
            return ctx.enter_context(nc.psum_tensor(name, shape, dt))

        def sem(name):
            return sems.new(ctx, "e_" + name)

        raw = [sb(f"e_raw{i}", [128, 2048]) for i in range(2)]
        whi = [sb(f"e_whi{i}", [128, 2048], F32R) for i in range(2)]
        wlo = [sb(f"e_wlo{i}", [128, 2048], F32R) for i in range(2)]
        b1 = sb("e_b1", [128, NX, KF])
        b2 = [sb(f"e_b2_{i}", [128, D]) for i in range(2)]
        idx_rows = sb("e_idx_rows", [ST * NX, 128], I32)
        idx_f = sb("e_idx_f", [ST * NX, 128])
        idx = sb("e_idx", [128, ST * NX], I32)
        rows = [sb(f"e_rows{i}", [128, ST, D]) for i in range(2)]
        xT_hi = sb("e_xT_hi", [128, KD, FIRST_ROWS], F32R)
        xT_lo = sb("e_xT_lo", [128, KD, FIRST_ROWS], F32R)
        g = sb("e_g", [128, KF, FIRST_ROWS])
        g_hi = sb("e_g_hi", [128, KF, FIRST_ROWS], F32R)
        g_lo = sb("e_g_lo", [128, KF, FIRST_ROWS], F32R)
        y = [sb(f"e_y{i}", [128, D]) for i in range(ST)]
        ps_turn = [pb(f"e_turn{s}", [128, KD, 128]) for s in range(ST)]
        ps_up = [pb(f"e_up{i}", [128, KF, FIRST_ROWS]) for i in range(2)]
        ps_down = [pb(f"e_down{s}", [128, D]) for s in range(ST)]
        b1_loaded, idx_loaded = sem("b1_loaded"), sem("idx_loaded")
        idx_float, idx_turned, idx_ready = sem("idx_float"), sem("idx_turned"), sem("idx_ready")
        w_loaded = [sem(f"w_loaded{i}") for i in range(2)]
        gathered = [sem(f"gathered{i}") for i in range(2 * ST)]
        whi_ready, wlo_ready = sem("whi_ready"), sem("wlo_ready")
        turned, xhi_ready, xlo_ready = sem("turned"), sem("xhi_ready"), sem("xlo_ready")
        up_done, g_ready, ghi_ready, glo_ready = sem("up_done"), sem("g_ready"), sem("ghi_ready"), sem("glo_ready")
        down_done, y_ready = sem("down_done"), sem("y_ready")
        y_stored = [sem(f"y_stored{s}") for s in range(ST)]
        block = ctx.enter_context(nc.Block())

        def parts(t, i):
            return (t[i][:, 0:1024].rearrange("p (k f) -> p k f", k=KD), t[i][:, 1024:2048].rearrange("p (k f) -> p k f", k=KF))

        @block.sync
        def _(sp):
            def load(x):
                if x >= 2:
                    sp.wait_ge(whi_ready, x - 1)
                    sp.wait_ge(wlo_ready, x - 1)
                    sp.wait_ge(y_ready, ST * (x - 1))
                w1, w2, bias2 = expert_weights(a, x)
                up, down = parts(raw, x % 2)
                sp.dma_start(up, w1).then_inc(w_loaded[x % 2], 16)
                sp.dma_start(down, w2).then_inc(w_loaded[x % 2], 16)
                sp.dma_start(b2[x % 2][:, :], bias2.partition_broadcast(128)).then_inc(w_loaded[x % 2], 16)

            tok = r.token_of[0:MORE_FROM, :].rearrange("(x s p) o -> s x (p o)", x=NX, p=128)
            for s in range(ST):
                sp.dma_start(idx_rows[s * NX:(s + 1) * NX, :], tok[s]).then_inc(idx_loaded, 16)
            for b, bank in enumerate(BANKS):
                sp.dma_start(b1[:, b * NE:(b + 1) * NE, :], a[f"L0_ffn_b1_{bank}"]).then_inc(b1_loaded, 16)
            load(0)
            for x in range(NX):
                if x + 1 < NX:
                    load(x + 1)
                for s in range(ST):
                    sp.wait_ge(y_ready, x * ST + s + 1)
                    row = x * FIRST_ROWS + s * 128
                    sp.dma_start(r.y_rows[row:row + 128, :], y[s][:, :]).then_inc(y_stored[s], 16)
            for s in range(ST):
                sp.wait_ge(y_stored[s], 16 * NX)

        @block.gpsimd
        def _(pool):
            sems.clear(pool)
            pool.wait_ge(idx_ready, 1)
            for x in range(NX):
                for s in range(ST):
                    if x >= 2:
                        pool.wait_ge(turned, ST * (x - 2) + s + 1)
                    nc.gpsimd.indirect_dma_start(
                        out=rows[x % 2][:, s, :], out_offset=None, in_=r.h_rows,
                        in_offset=bass.IndirectOffsetOnAxis(ap=idx[:, s * NX + x:s * NX + x + 1], axis=0)).then_inc(gathered[(x % 2) * ST + s], 16)

        @block.scalar
        def _(act):
            act.wait_ge(b1_loaded, 16 * NB)

            def split_w(x):
                act.wait_ge(w_loaded[x % 2], 48 * (x // 2 + 1))
                if x >= 2:
                    act.wait_ge(down_done, ST * (x - 1))
                nc.scalar.activation(whi[x % 2][:, :], raw[x % 2][:, :], ACT.Copy).then_inc(whi_ready, 1)

            def split_x(x):
                for s in range(ST):
                    act.wait_ge(turned, ST * x + s + 1)
                    if x:
                        act.wait_ge(up_done, x)
                    nc.scalar.activation(xT_hi[:, :, s * 128:(s + 1) * 128], ps_turn[s][:, :, :], ACT.Copy).then_inc(xhi_ready, 1)

            split_w(0)
            split_x(0)
            for x in range(NX):
                act.wait_ge(up_done, x + 1)
                if x:
                    act.wait_ge(glo_ready, x)
                for m in range(KF):
                    nc.scalar.activation(g[:, m, :], ps_up[x % 2][:, m, :], ACT.Gelu, bias=b1[:, x, m:m + 1]).then_inc(g_ready, 1)
                act.wait_ge(g_ready, KF * (x + 1))
                if x:
                    act.wait_ge(down_done, ST * x)
                nc.scalar.activation(g_hi[:, :, :], g[:, :, :], ACT.Copy).then_inc(ghi_ready, 1)
                if x + 1 < NX:
                    split_x(x + 1)
                    split_w(x + 1)

        @block.vector
        def _(dve):
            def split_w(x):
                dve.wait_ge(whi_ready, x + 1)
                nc.vector.tensor_tensor(wlo[x % 2][:, :], raw[x % 2][:, :], whi[x % 2][:, :].bitcast(F32),
                                        ALU.subtract).then_inc(wlo_ready, 1)

            def split_x(x):
                for s in range(ST):
                    dve.wait_ge(xhi_ready, ST * x + s + 1)
                    cols = slice(s * 128, (s + 1) * 128)
                    nc.vector.tensor_tensor(xT_lo[:, :, cols], ps_turn[s][:, :, :], xT_hi[:, :, cols].bitcast(F32),
                                            ALU.subtract).then_inc(xlo_ready, 1)

            dve.wait_ge(idx_loaded, 16 * ST)
            nc.vector.tensor_copy(idx_f[:, :], idx_rows[:, :]).then_inc(idx_float, 1)
            dve.wait_ge(idx_turned, 1)
            nc.vector.tensor_copy(idx[:, :], ps_down[0][:, 0:ST * NX]).then_inc(idx_ready, 1)
            split_w(0)
            split_x(0)
            for x in range(NX):
                dve.wait_ge(ghi_ready, x + 1)
                nc.vector.tensor_tensor(g_lo[:, :, :], g[:, :, :], g_hi[:, :, :].bitcast(F32), ALU.subtract).then_inc(glo_ready, 1)
                if x + 1 < NX:
                    split_x(x + 1)
                    split_w(x + 1)
                for s in range(ST):
                    dve.wait_ge(down_done, ST * x + s + 1)
                    if x:
                        dve.wait_ge(y_stored[s], 16 * x)
                    nc.vector.tensor_tensor(y[s][:, :], ps_down[s][:, :], b2[x % 2][:, :], ALU.add).then_inc(y_ready, 1)

        @block.tensor
        def _(pe):
            def turn(x):
                for s in range(ST):
                    pe.wait_ge(gathered[(x % 2) * ST + s], 16 * (x // 2 + 1))
                    if x:
                        pe.wait_ge(xlo_ready, ST * (x - 1) + s + 1)
                    for k in range(KD):
                        last = nc.tensor.transpose(ps_turn[s][:, k, :], rows[x % 2][:, s, k * 128:(k + 1) * 128], ident[:, :])
                    last.then_inc(turned, 1)

            pe.wait_ge(idx_float, 1)
            nc.tensor.transpose(ps_down[0][:, 0:ST * NX], idx_f[:, :], ident[0:ST * NX, 0:ST * NX]).then_inc(idx_turned, 1)
            turn(0)
            pe.wait_ge(idx_ready, 1)
            for x in range(NX):
                (u_hi, d_hi), (u_lo, d_lo) = parts(whi, x % 2), parts(wlo, x % 2)
                pe.wait_ge(xlo_ready, ST * (x + 1))
                pe.wait_ge(wlo_ready, x + 1)
                for m in range(KF):
                    for k in range(KD):
                        ms = slice(m * 128, (m + 1) * 128)
                        last = three(nc, ps_up[x % 2][:, m, :], u_hi[:, k, ms], u_lo[:, k, ms], xT_hi[:, k, :], xT_lo[:, k, :],
                                     k == 0, k == KD - 1)
                last.then_inc(up_done, 1)
                if x + 1 < NX:
                    turn(x + 1)
                pe.wait_ge(glo_ready, x + 1)
                for s in range(ST):
                    if x:
                        pe.wait_ge(y_ready, ST * (x - 1) + s + 1)
                    for k in range(KF):
                        cols = slice(s * 128, (s + 1) * 128)
                        last = three(nc, ps_down[s][:, :], g_hi[:, k, cols], g_lo[:, k, cols], d_hi[:, k, :], d_lo[:, k, :],
                                     k == 0, k == KF - 1)
                    last.then_inc(down_done, 1)


def overfull_experts(nc, sems, a, ident, r):
    sems.next_phase()
    with ExitStack() as ctx:
        def sb(name, shape, dt=F32):
            return ctx.enter_context(nc.sbuf_tensor(name, shape, dt))

        def pb(name, shape, dt=F32):
            return ctx.enter_context(nc.psum_tensor(name, shape, dt))

        def sem(name):
            return sems.new(ctx, "o_" + name)

        raw = sb("o_raw", [128, 2048])
        whi = sb("o_whi", [128, 2048], F32R)
        wlo = sb("o_wlo", [128, 2048], F32R)
        b1 = sb("o_b1", [128, KF])
        b2 = sb("o_b2", [128, D])
        idx = sb("o_idx", [128, 1], I32)
        rows = sb("o_rows", [128, D])
        xT_hi = sb("o_xT_hi", [128, KD, MORE_ROWS], F32R)
        xT_lo = sb("o_xT_lo", [128, KD, MORE_ROWS], F32R)
        g = sb("o_g", [128, KF, MORE_ROWS])
        g_hi = sb("o_g_hi", [128, KF, MORE_ROWS], F32R)
        g_lo = sb("o_g_lo", [128, KF, MORE_ROWS], F32R)
        y = sb("o_y", [128, D])
        ps_turn = pb("o_turn", [128, KD, 128])
        ps_up = pb("o_up", [128, KF, 256])
        ps_down = pb("o_down", [128, D])
        w_loaded, whi_ready, w_ready = sem("w_loaded"), sem("whi_ready"), sem("w_ready")
        begun = sem("begun")
        expert_over = sem("expert_over")
        idx_loaded, gathered, turned = sem("idx_loaded"), sem("gathered"), sem("turned")
        xhi_ready, x_ready, up_done, g_made = sem("xhi_ready"), sem("x_ready"), sem("up_done"), sem("g_made")
        ghi_ready, g_ready, down_done, y_ready, y_stored, round_over = (
            sem("ghi_ready"), sem("g_ready"), sem("down_done"), sem("y_ready"), sem("y_stored"), sem("round_over"))
        block = ctx.enter_context(nc.Block())
        up_hi, down_hi = (whi[:, 0:1024].rearrange("p (k f) -> p k f", k=KD), whi[:, 1024:2048].rearrange("p (k f) -> p k f", k=KF))
        up_lo, down_lo = (wlo[:, 0:1024].rearrange("p (k f) -> p k f", k=KD), wlo[:, 1024:2048].rearrange("p (k f) -> p k f", k=KF))

        def overfull(eng, tag, at_expert, at_round):
            experts = eng.alloc_register(f"{tag}_experts")
            rounds = eng.alloc_register(f"{tag}_rounds")
            eng.reg_mov(experts, 1)
            eng.reg_mov(rounds, 1)
            for b in range(NB):
                with eng.Fori(0, NE) as e:
                    count = eng.value_load(r.rounds[0:1, bass.DynSlice(e + b * NE, 1)], min_val=0, max_val=ROUNDS)
                    with eng.If(count > 0):
                        nth = eng.snap(experts, min_val=1, max_val=NX)
                        at_expert(nth, b, e)
                        with eng.Fori(0, count) as k:
                            at_round(eng.snap(rounds, min_val=1, max_val=NB * ROUNDS), b, e, k)
                            eng.reg_add(rounds, rounds, 1)
                        eng.reg_add(experts, experts, 1)

        @block.sync
        def _(sp):
            sp.sem_inc(round_over, 1)
            sp.sem_inc(expert_over, 1)

            def at_expert(nth, b, e):
                sp.wait_ge(expert_over, nth)
                bank, one = BANKS[b], bass.DynSlice(e, 1)
                sp.dma_start(raw[:, 0:1024].rearrange("p (k f) -> p k f", k=KD),
                             a[f"L0_ffn_W1_{bank}"][one].rearrange("o (k p) f -> p (o k) f", p=128)).then_inc(w_loaded, 16)
                sp.dma_start(raw[:, 1024:2048].rearrange("p (k f) -> p k f", k=KF),
                             a[f"L0_ffn_W2_{bank}"][one].rearrange("o (k p) f -> p (o k) f", p=128)).then_inc(w_loaded, 16)
                sp.dma_start(b1[:, :], a[f"L0_ffn_b1_{bank}"][:, one, :].rearrange("p o m -> p (o m)")).then_inc(w_loaded, 16)
                sp.dma_start(b2[:, :], a[f"L0_ffn_b2_{bank}"][one].rearrange("o d -> (o d)").partition_broadcast(128)).then_inc(w_loaded, 16)

            def at_round(nth, b, e, k):
                row = nth * MORE_ROWS + (MORE_FROM - MORE_ROWS)
                sp.wait_ge(round_over, nth)
                sp.dma_start(idx[:, :], r.token_of[bass.DynSlice(row, MORE_ROWS), :]).then_inc(idx_loaded, 16)
                sp.wait_ge(y_ready, nth)
                sp.dma_start(r.y_rows[bass.DynSlice(row, MORE_ROWS), :], y[:, :]).then_inc(y_stored, 16)
                sp.wait_ge(y_stored, nth * 16)
                sp.sem_inc(round_over, 1)

            overfull(sp, "sp", at_expert, at_round)

        @block.gpsimd
        def _(pool):
            sems.clear(pool)
            def at_round(nth, b, e, k):
                pool.wait_ge(idx_loaded, nth * 16)
                pool.sem_inc(begun, 1)
                nc.gpsimd.indirect_dma_start(out=rows[:, :], out_offset=None, in_=r.h_rows,
                                             in_offset=bass.IndirectOffsetOnAxis(ap=idx[:, 0:1], axis=0)).then_inc(gathered, 16)

            overfull(pool, "pool", lambda *_: None, at_round)

        @block.scalar
        def _(act):
            def at_expert(nth, b, e):
                act.wait_ge(w_loaded, nth * 64)
                nc.scalar.activation(whi[:, :], raw[:, :], ACT.Copy).then_inc(whi_ready, 1)

            def at_round(nth, b, e, k):
                act.wait_ge(turned, nth)
                nc.scalar.activation(xT_hi[:, :, :], ps_turn[:, :, :], ACT.Copy).then_inc(xhi_ready, 1)
                act.wait_ge(up_done, nth)
                for m in range(KF):
                    last = nc.scalar.activation(g[:, m, :], ps_up[:, m, 0:MORE_ROWS], ACT.Gelu, bias=b1[:, m:m + 1])
                last.then_inc(g_made, 1)
                act.wait_ge(g_made, nth)
                nc.scalar.activation(g_hi[:, :, :], g[:, :, :], ACT.Copy).then_inc(ghi_ready, 1)

            overfull(act, "act", at_expert, at_round)

        @block.vector
        def _(dve):
            def at_expert(nth, b, e):
                dve.wait_ge(whi_ready, nth)
                nc.vector.tensor_tensor(wlo[:, :], raw[:, :], whi[:, :].bitcast(F32), ALU.subtract).then_inc(w_ready, 1)

            def at_round(nth, b, e, k):
                dve.wait_ge(xhi_ready, nth)
                nc.vector.tensor_tensor(xT_lo[:, :, :], ps_turn[:, :, :], xT_hi[:, :, :].bitcast(F32), ALU.subtract).then_inc(x_ready, 1)
                dve.wait_ge(ghi_ready, nth)
                nc.vector.tensor_tensor(g_lo[:, :, :], g[:, :, :], g_hi[:, :, :].bitcast(F32), ALU.subtract).then_inc(g_ready, 1)
                dve.wait_ge(down_done, nth)
                nc.vector.tensor_tensor(y[:, :], ps_down[:, :], b2[:, :], ALU.add).then_inc(y_ready, 1)

            overfull(dve, "dve", at_expert, at_round)

        @block.tensor
        def _(pe):
            experts = pe.alloc_register("pe_experts")
            rounds = pe.alloc_register("pe_rounds")
            pe.reg_mov(experts, 1)
            pe.reg_mov(rounds, 1)
            for b in range(NB):
                with pe.Fori(0, NE) as e:
                    count = pe.value_load(r.rounds[0:1, bass.DynSlice(e + b * NE, 1)], min_val=0, max_val=ROUNDS)
                    with pe.If(count > 0):
                        pe.wait_ge(w_ready, pe.snap(experts, min_val=1, max_val=NX))
                        pe.sem_inc(begun, 1)
                        with pe.Fori(0, count):
                            nth = pe.snap(rounds, min_val=1, max_val=NB * ROUNDS)
                            pe.wait_ge(gathered, nth * 16)
                            for k in range(KD):
                                last = nc.tensor.transpose(ps_turn[:, k, :], rows[:, k * 128:(k + 1) * 128], ident[:, :])
                            last.then_inc(turned, 1)
                            pe.wait_ge(x_ready, nth)
                            for m in range(KF):
                                for k in range(KD):
                                    ms = slice(m * 128, (m + 1) * 128)
                                    last = three(nc, ps_up[:, m, 0:MORE_ROWS], up_hi[:, k, ms], up_lo[:, k, ms],
                                                 xT_hi[:, k, :], xT_lo[:, k, :], k == 0, k == KD - 1)
                            last.then_inc(up_done, 1)
                            pe.wait_ge(g_ready, nth)
                            for k in range(KF):
                                last = three(nc, ps_down[:, :], g_hi[:, k, :], g_lo[:, k, :], down_hi[:, k, :], down_lo[:, k, :],
                                             k == 0, k == KF - 1)
                            last.then_inc(down_done, 1)
                            pe.reg_add(rounds, rounds, 1)
                        pe.wait_ge(y_ready, pe.snap(rounds, min_val=1, max_val=NB * ROUNDS) - 1)
                        pe.sem_inc(expert_over, 1)
                        pe.reg_add(experts, experts, 1)


def combine(nc, sems, X, CT, ident, r):
    NR = 6
    swaps = [(i, j, min(j + 4, NT)) for i in range(NT) for j in range(i + 1, NT, 4)]
    diagonal = [(j, min(j + 4, NT)) for j in range(0, NT, 4)]
    sems.next_phase()
    with ExitStack() as ctx:
        rows = [ctx.enter_context(nc.sbuf_tensor(f"c_rows{i}", [PT, D], F32)) for i in range(NR)]
        gathered = [sems.new(ctx, f"c_gathered{i}") for i in range(NR)]
        added = sems.new(ctx, "c_added")
        turned = sems.new(ctx, "c_turned")
        swapped = sems.new(ctx, "c_swapped")
        ps = [[ctx.enter_context(nc.psum_tensor(f"c_ps{n}{half}", [PT, 4, 128], F32)) for half in range(2)] for n in range(2)]
        block = ctx.enter_context(nc.Block())
        pairs = [(t, b) for t in range(NT) for b in range(NB)]

        @block.gpsimd
        def _(pool):
            sems.clear(pool)
            for n, (t, b) in enumerate(pairs):
                if n >= NR:
                    pool.wait_ge(added, n - NR + 1)
                nc.gpsimd.indirect_dma_start(out=rows[n % NR][:, :], out_offset=None, in_=r.y_rows,
                                             in_offset=bass.IndirectOffsetOnAxis(ap=r.slot[:, t, b:b + 1], axis=0)).then_inc(gathered[n % NR], 16)

        @block.vector
        def _(dve):
            for n, (t, b) in enumerate(pairs):
                dve.wait_ge(gathered[n % NR], 16 * (n // NR + 1))
                if b:
                    dve.wait_ge(added, n)
                nc.vector.scalar_tensor_tensor(X[:, t, :], rows[n % NR][:, :], r.gate[:, t, b:b + 1], X[:, t, :],
                                               ALU.mult, ALU.add).then_inc(added, 1)

        def block_of(i, j):
            return CT[:, i, j * PT:(j + 1) * PT]

        @block.tensor
        def _(pe):
            for n, (i, j0, j1) in enumerate(swaps):
                if n >= 2:
                    pe.wait_ge(swapped, n - 1)
                for j in range(j0, j1):
                    nc.tensor.transpose(ps[n % 2][0][:, j - j0, 0:PT], block_of(i, j), ident[0:PT, 0:PT])
                for j in range(j0, j1):
                    last = nc.tensor.transpose(ps[n % 2][1][:, j - j0, 0:PT], block_of(j, i), ident[0:PT, 0:PT])
                last.then_inc(turned, 1)
            for m, (j0, j1) in enumerate(diagonal):
                n = len(swaps) + m
                pe.wait_ge(swapped, n - 1)
                for j in range(j0, j1):
                    last = nc.tensor.transpose(ps[n % 2][0][:, j - j0, 0:PT], block_of(j, j), ident[0:PT, 0:PT])
                last.then_inc(turned, 1)

        @block.scalar
        def _(act):
            for n, (i, j0, j1) in enumerate(swaps):
                act.wait_ge(turned, n + 1)
                nc.scalar.activation(CT[:, j0:j1, i * PT:(i + 1) * PT], ps[n % 2][0][:, 0:j1 - j0, 0:PT], ACT.Copy)
                nc.scalar.activation(CT[:, i, j0 * PT:j1 * PT].rearrange("p (j q) -> p j q", q=PT), ps[n % 2][1][:, 0:j1 - j0, 0:PT],
                                     ACT.Copy).then_inc(swapped, 1)
            for m, (j0, j1) in enumerate(diagonal):
                n = len(swaps) + m
                act.wait_ge(turned, n + 1)
                for j in range(j0, j1):
                    last = nc.scalar.activation(block_of(j, j), ps[n % 2][0][:, j - j0, 0:PT], ACT.Copy)
                last.then_inc(swapped, 1)


HEADS = 8
DH = FF // HEADS
TINY = 1.1754944e-38
HUGE = 3.4028235e38


def project_qkv(nc, sems, a, X, H, hT_hi, hT_lo, ident, eps_col, V, r):
    sems.next_phase()
    with ExitStack() as ctx:
        def sb(name, shape, dt=F32):
            return ctx.enter_context(nc.sbuf_tensor(name, shape, dt))

        def pb(name, shape, dt=F32):
            return ctx.enter_context(nc.psum_tensor(name, shape, dt))

        def sem(name):
            return sems.new(ctx, "q_" + name)

        raw = [sb(f"q_raw{i}", [128, KD, FF]) for i in range(2)]
        whi = [sb(f"q_whi{i}", [128, KD, FF], F32R) for i in range(3)]
        wlo = [sb(f"q_wlo{i}", [128, KD, FF], F32R) for i in range(3)]
        bqk = sb("bqk", [128, 2, KF])
        bv = sb("bv", [PT, FF])
        full = sb("q_full", [128, N])
        hi = sb("q_hi", [128, N], F32R)
        lo = sb("q_lo", [128, N], F32R)
        ps_qk = [pb(f"ps_qk{i}", [128, 3, 512]) for i in range(2)]
        ps_turn = [pb(f"q_turn{i}", [128, 4, 128]) for i in range(2)]
        w_loaded, b_loaded = sem("w_loaded"), sem("b_loaded")
        whi_ready, wlo_ready, ones_made = sem("whi_ready"), sem("wlo_ready"), sem("ones_made")
        v_done, v_ready, qk_done, full_ready = sem("v_done"), sem("v_ready"), sem("qk_done"), sem("full_ready")
        hi_ready, lo_ready, stored, step = sem("hi_ready"), sem("lo_ready"), sem("stored"), sem("step")
        ln = Norm(nc, sems, ctx, "ln3", X, H, hT_hi, hT_lo, ps_turn, ident, eps_col)
        block = ctx.enter_context(nc.Block())

        @block.sync
        def _(sp):
            for i, name in enumerate("vqk"):
                if i >= 2:
                    sp.wait_ge(wlo_ready, i - 1)
                sp.dma_start(raw[i % 2][:, :, :], a[f"L1_gnn_W{name}"].rearrange("(k p) f -> p k f", p=128)).then_inc(w_loaded, 16)
                if i < 2:
                    sp.dma_start(bqk[:, i, :], a[f"L1_gnn_b{'qk'[i]}"]).then_inc(b_loaded, 16)
                sp.wait_ge(w_loaded, 16 * (i + 1))
            sp.dma_start(bv[:, :], a["L1_gnn_bv"].partition_broadcast(PT)).then_inc(b_loaded, 16)
            for u in range(2 * KF):
                q, m = u // KF, u % KF
                sp.wait_ge(hi_ready, u + 1)
                sp.dma_start(r.qk[2 * q, m * 128:(m + 1) * 128, :], hi[:, :].bitcast(F32)).then_inc(stored, 16)
                sp.wait_ge(lo_ready, u + 1)
                sp.dma_start(r.qk[2 * q + 1, m * 128:(m + 1) * 128, :], lo[:, :].bitcast(F32)).then_inc(stored, 16)
            sp.wait_ge(stored, 16 * 4 * KF)

        @block.gpsimd
        def _(pool):
            sems.clear(pool)
            nc.gpsimd.memset(V[:, :, :, DH:64], 1.0).then_inc(ones_made, 1)
            pool.wait_ge(ones_made, 1)

        @block.scalar
        def _(act):
            ln.scalar(act)
            for i in range(3):
                act.wait_ge(w_loaded, 16 * (i + 1))
                nc.scalar.activation(whi[i][:, :, :], raw[i % 2][:, :, :], ACT.Copy).then_inc(whi_ready, 1)
            act.wait_ge(b_loaded, 48)
            for u in range(2 * KF):
                act.wait_ge(qk_done, u + 1)
                if u:
                    act.wait_ge(lo_ready, u)
                for c, (c0, c1) in enumerate(CHUNKS):
                    last = nc.scalar.activation(full[:, c0:c1], ps_qk[u % 2][:, c, 0:c1 - c0], ACT.Identity,
                                                bias=bqk[:, u // KF, u % KF:u % KF + 1])
                last.then_inc(full_ready, 1)

        @block.vector
        def _(dve):
            link = chained(dve, step)
            ln.vector(dve, link)
            for i in range(3):
                dve.wait_ge(whi_ready, i + 1)
                nc.vector.tensor_tensor(wlo[i][:, :, :], raw[i % 2][:, :, :], whi[i][:, :, :].bitcast(F32), ALU.subtract).then_inc(wlo_ready, 1)
            for t in range(NT):
                last = nc.vector.tensor_tensor(X[:, t, :], X[:, t, :], H[:, t, :], ALU.add)
            link(last)
            dve.wait_ge(b_loaded, 48)
            for t in range(NT):
                dve.wait_ge(v_done, t + 1)
                nc.vector.tensor_tensor(V[:, t, :, 0:DH], ps_turn[t % 2][0:PT, 0:2, :].rearrange("p a (h d) -> p (a h) d", d=DH),
                                        bv[:, :].rearrange("p (h d) -> p h d", d=DH), ALU.add).then_inc(v_ready, 1)
            for u in range(2 * KF):
                dve.wait_ge(full_ready, u + 1)
                if u:
                    dve.wait_ge(stored, 32 * u)
                nc.vector.tensor_copy(hi[:, :], full[:, :]).then_inc(hi_ready, 1)
                dve.wait_ge(hi_ready, u + 1)
                nc.vector.tensor_tensor(lo[:, :], full[:, :], hi[:, :].bitcast(F32), ALU.subtract).then_inc(lo_ready, 1)

        @block.tensor
        def _(pe):
            ln.tensor(pe)
            pe.wait_ge(ln.lo_ready, NT)
            pe.wait_ge(wlo_ready, 1)
            for t in range(NT):
                tok = slice(t * PT, (t + 1) * PT)
                if t >= 2:
                    pe.wait_ge(v_ready, t - 1)
                out = ps_turn[t % 2][0:PT, 0:2, :].rearrange("p a f -> p (a f)")
                for k in range(KD):
                    last = three(nc, out, hT_hi[:, k, tok], hT_lo[:, k, tok], whi[0][:, k, :], wlo[0][:, k, :], k == 0, k == KD - 1)
                last.then_inc(v_done, 1)
            for u in range(2 * KF):
                q, m = u // KF, u % KF
                pe.wait_ge(wlo_ready, q + 2)
                if u >= 2:
                    pe.wait_ge(full_ready, u - 1)
                for c, (c0, c1) in enumerate(CHUNKS):
                    for k in range(KD):
                        ms = slice(m * 128, (m + 1) * 128)
                        last = three(nc, ps_qk[u % 2][:, c, 0:c1 - c0], whi[q + 1][:, k, ms], wlo[q + 1][:, k, ms],
                                     hT_hi[:, k, c0:c1], hT_lo[:, k, c0:c1], k == 0, k == KD - 1)
                last.then_inc(qk_done, 1)


def attention(nc, sems, oT_hi, oT_lo, CT, V, r):
    WIDTH = 418
    STARTS = (0, 418, N - 418)
    SKIP = (0, 0, 3 * 418 - N)
    units = [(h, s, c) for h in range(HEADS) for s in range(NT) for c in range(3)]
    NS, NP, LAG = 5, 4, 4
    HG = 128 // DH
    sems.next_phase()
    with ExitStack() as ctx:
        def sb(name, shape, dt=F32):
            return ctx.enter_context(nc.sbuf_tensor(name, shape, dt))

        def pb(name, shape, dt=F32):
            return ctx.enter_context(nc.psum_tensor(name, shape, dt))

        def sem(name):
            return sems.new(ctx, "a_" + name)

        q = [sb(f"a_q{i}", [3 * DH, N], F32R) for i in range(2)]
        k = [sb(f"a_k{i}", [3 * DH, N], F32R) for i in range(2)]
        e = [sb(f"a_e{i}", [PT, WIDTH]) for i in range(NP)]
        p = [sb(f"a_p{i}", [PT, WIDTH]) for i in range(NP)]
        num = sb("a_num", [128, N])
        den = sb("a_den", [128, N])
        ps_s = [pb(f"a_s{i}", [PT, 512]) for i in range(NS)]
        ps_o = [pb(f"a_o{i}", [64, 512]) for i in range(3)]
        loaded = [sem(f"loaded{i}") for i in range(2)]
        scored, exped, weighed = sem("scored"), sem("exped"), sem("weighed")
        summed_units = sem("summed_units")
        num_taken, den_taken, ratio_ready = sem("num_taken"), sem("den_taken"), sem("ratio_ready")
        step = sem("step")
        block = ctx.enter_context(nc.Block())

        @block.sync
        def _(sp):
            for h in range(HEADS):
                if h >= 2:
                    sp.wait_ge(scored, 3 * NT * (h - 1))
                rows = slice(h * DH, (h + 1) * DH)
                for j, (kq, kk) in enumerate(((0, 2), (1, 2), (0, 3))):
                    sp.dma_start(q[h % 2][j * DH:(j + 1) * DH, :].bitcast(F32), r.qk[kq, rows, :]).then_inc(loaded[h % 2], 16)
                    sp.dma_start(k[h % 2][j * DH:(j + 1) * DH, :].bitcast(F32), r.qk[kk, rows, :]).then_inc(loaded[h % 2], 16)

        @block.gpsimd
        def _(pool):
            sems.clear(pool)

        @block.scalar
        def _(act):
            def take_num(h, c):
                act.wait_ge(summed_units, (NT * (h + 1) - 1) * 3 + c + 1)
                if h == HG:
                    act.wait_ge(ratio_ready, 1)
                part = slice((h % HG) * DH, (h % HG + 1) * DH)
                nc.scalar.activation(num[part, STARTS[c] + SKIP[c]:STARTS[c] + WIDTH], ps_o[c][0:DH, SKIP[c]:WIDTH], ACT.Relu).then_inc(num_taken, 1)

            for u, (h, s, c) in enumerate(units):
                act.wait_ge(scored, u + 1)
                if u >= NP:
                    act.wait_ge(weighed, u - NP + 1)
                nc.scalar.activation(e[u % NP][:, :], ps_s[u % NS][:, 0:WIDTH], ACT.Exp, scale=DH ** -0.5).then_inc(exped, 1)
                if h and s == 0:
                    take_num(h - 1, c)
            for c in range(3):
                take_num(HEADS - 1, c)

        @block.vector
        def _(dve):
            link = chained(dve, step)

            def take_den(h, c):
                dve.wait_ge(summed_units, (NT * (h + 1) - 1) * 3 + c + 1)
                part = slice((h % HG) * DH, (h % HG + 1) * DH)
                nc.vector.tensor_scalar(den[part, STARTS[c] + SKIP[c]:STARTS[c] + WIDTH], ps_o[c][DH:2 * DH, SKIP[c]:WIDTH], TINY, None,
                                        ALU.max).then_inc(den_taken, 1)

            def divide(g):
                dve.wait_ge(den_taken, 3 * HG * (g + 1))
                dve.wait_ge(num_taken, 3 * HG * (g + 1))
                link(nc.vector.reciprocal(den[:, :], den[:, :]))
                link(nc.vector.tensor_tensor(num[:, :], num[:, :], den[:, :], ALU.mult))
                link(nc.vector.tensor_copy(oT_hi[:, g, :], num[:, :]))
                nc.vector.tensor_tensor(oT_lo[:, g, :], num[:, :], oT_hi[:, g, :].bitcast(F32), ALU.subtract).then_inc(ratio_ready, 1)
                dve.wait_ge(ratio_ready, g + 1)

            for u, (h, s, c) in enumerate(units):
                dve.wait_ge(exped, u + 1)
                if u >= NP:
                    dve.wait_ge(summed_units, u - NP + 1)
                nc.vector.scalar_tensor_tensor(p[u % NP][:, :], e[u % NP][:, :], HUGE, CT[:, s, STARTS[c]:STARTS[c] + WIDTH],
                                               ALU.min, ALU.mult).then_inc(weighed, 1)
                if h and s == 0:
                    take_den(h - 1, c)
                if h == HG and s == 1 and c == 0:
                    divide(0)
            for c in range(3):
                take_den(HEADS - 1, c)
            divide(1)

        @block.tensor
        def _(pe):
            for v in range(len(units) + LAG):
                if v < len(units):
                    h, s, c = units[v]
                    if s == 0 and c == 0:
                        pe.wait_ge(loaded[h % 2], 96 * (h // 2 + 1))
                    if v >= NS:
                        pe.wait_ge(exped, v - NS + 1)
                    nc.tensor.matmul(ps_s[v % NS][:, 0:WIDTH], k[h % 2][:, s * PT:(s + 1) * PT],
                                     q[h % 2][:, STARTS[c]:STARTS[c] + WIDTH], start=True, stop=True).then_inc(scored, 1)
                if v >= LAG:
                    u = v - LAG
                    h, s, c = units[u]
                    pe.wait_ge(weighed, u + 1)
                    if h and s == 0:
                        pe.wait_ge(num_taken, 3 * (h - 1) + c + 1)
                        pe.wait_ge(den_taken, 3 * (h - 1) + c + 1)
                    nc.tensor.matmul(ps_o[c][:, 0:WIDTH], V[:, s, h, :], p[u % NP][:, :], start=(s == 0),
                                     stop=(s == NT - 1)).then_inc(summed_units, 1)


def attention_out(nc, sems, a, X, oT_hi, oT_lo):
    UNITS = [(m, c) for m in range(KD) for c in range(len(CHUNKS))]
    sems.next_phase()
    with ExitStack() as ctx:
        def sb(name, shape, dt=F32):
            return ctx.enter_context(nc.sbuf_tensor(name, shape, dt))

        def pb(name, shape, dt=F32):
            return ctx.enter_context(nc.psum_tensor(name, shape, dt))

        def sem(name):
            return sems.new(ctx, "w_" + name)

        shapes = ([128, KF, D], [128, KD, D])
        raw = [sb(f"o2_raw{i}", shapes[i]) for i in range(2)]
        whi = [sb(f"o2_whi{i}", shapes[i], F32R) for i in range(2)]
        wlo = [sb(f"o2_wlo{i}", shapes[i], F32R) for i in range(2)]
        ba = sb("ba", [128, KD])
        bf = sb("bf", [PT, D])
        full = [sb(f"w_full{i}", [128, 512]) for i in range(2)]
        f_hi = sb("w_f_hi", [128, KD, N], F32R)
        f_lo = sb("w_f_lo", [128, KD, N], F32R)
        y = [sb(f"w_y{i}", [PT, D]) for i in range(2)]
        ps_f = [pb(f"w_f{i}", [128, 512]) for i in range(2)]
        ps_y = [pb(f"w_psy{i}", [PT, D]) for i in range(2)]
        w_loaded, b_loaded = [sem(f"w_loaded{i}") for i in range(2)], sem("b_loaded")
        whi_ready, wlo_ready = sem("whi_ready"), sem("wlo_ready")
        f_done, full_ready, fhi_ready, flo_ready = sem("f_done"), sem("full_ready"), sem("fhi_ready"), sem("flo_ready")
        y_done, y_ready, step = sem("y_done"), sem("y_ready"), sem("step")
        block = ctx.enter_context(nc.Block())

        @block.sync
        def _(sp):
            for i, name in enumerate("af"):
                sp.dma_start(raw[i][:, :, :], a[f"L1_gnn_W{name}"].rearrange("(k p) f -> p k f", p=128)).then_inc(w_loaded[i], 16)
            sp.dma_start(ba[:, :], a["L1_gnn_ba"]).then_inc(b_loaded, 16)
            sp.dma_start(bf[:, :], a["L1_gnn_bf"].partition_broadcast(PT)).then_inc(b_loaded, 16)

        @block.gpsimd
        def _(pool):
            sems.clear(pool)

        @block.scalar
        def _(act):
            for i in range(2):
                act.wait_ge(w_loaded[i], 16)
                nc.scalar.activation(whi[i][:, :, :], raw[i][:, :, :], ACT.Copy).then_inc(whi_ready, 1)
            act.wait_ge(b_loaded, 32)
            for u, (m, c) in enumerate(UNITS):
                w = CHUNKS[c][1] - CHUNKS[c][0]
                act.wait_ge(f_done, u + 1)
                if u >= 2:
                    act.wait_ge(flo_ready, u - 1)
                nc.scalar.activation(full[u % 2][:, 0:w], ps_f[u % 2][:, 0:w], ACT.Relu, bias=ba[:, m:m + 1]).then_inc(full_ready, 1)
                act.wait_ge(full_ready, u + 1)
                nc.scalar.activation(f_hi[:, m, CHUNKS[c][0]:CHUNKS[c][1]], full[u % 2][:, 0:w], ACT.Copy).then_inc(fhi_ready, 1)

        @block.vector
        def _(dve):
            link = chained(dve, step)
            for i in range(2):
                dve.wait_ge(whi_ready, i + 1)
                nc.vector.tensor_tensor(wlo[i][:, :, :], raw[i][:, :, :], whi[i][:, :, :].bitcast(F32), ALU.subtract).then_inc(wlo_ready, 1)
            for u, (m, c) in enumerate(UNITS):
                c0, c1 = CHUNKS[c]
                dve.wait_ge(fhi_ready, u + 1)
                nc.vector.tensor_tensor(f_lo[:, m, c0:c1], full[u % 2][:, 0:c1 - c0], f_hi[:, m, c0:c1].bitcast(F32),
                                        ALU.subtract).then_inc(flo_ready, 1)
            for t in range(NT):
                dve.wait_ge(y_done, t + 1)
                nc.vector.tensor_tensor(y[t % 2][:, :], ps_y[t % 2][:, :], bf[:, :], ALU.add).then_inc(y_ready, 1)
                dve.wait_ge(y_ready, t + 1)
                link(nc.vector.scalar_tensor_tensor(X[:, t, :], y[t % 2][:, :], 0.0, X[:, t, :], ALU.max, ALU.add))

        @block.tensor
        def _(pe):
            pe.wait_ge(wlo_ready, 1)
            for u, (m, c) in enumerate(UNITS):
                c0, c1 = CHUNKS[c]
                if u >= 2:
                    pe.wait_ge(full_ready, u - 1)
                for k in range(KF):
                    ms = slice(m * 128, (m + 1) * 128)
                    last = three(nc, ps_f[u % 2][:, 0:c1 - c0], whi[0][:, k, ms], wlo[0][:, k, ms], oT_hi[:, k, c0:c1], oT_lo[:, k, c0:c1],
                                 k == 0, k == KF - 1)
                last.then_inc(f_done, 1)
            pe.wait_ge(wlo_ready, 2)
            pe.wait_ge(flo_ready, len(UNITS))
            for t in range(NT):
                tok = slice(t * PT, (t + 1) * PT)
                if t >= 2:
                    pe.wait_ge(y_ready, t - 1)
                for k in range(KD):
                    last = three(nc, ps_y[t % 2][:, :], f_hi[:, k, tok], f_lo[:, k, tok], whi[1][:, k, :], wlo[1][:, k, :],
                                 k == 0, k == KD - 1)
                last.then_inc(y_done, 1)


MAX_THRESHOLD = 0.25


def gated_experts(nc, sems, a, X, H, hT_hi, hT_lo, ident, eps_col, out):
    NG = NE + 2
    NY = 4
    sems.next_phase()
    with ExitStack() as ctx:
        def sb(name, shape, dt=F32):
            return ctx.enter_context(nc.sbuf_tensor(name, shape, dt))

        def pb(name, shape, dt=F32):
            return ctx.enter_context(nc.psum_tensor(name, shape, dt))

        def sem(name):
            return sems.new(ctx, "f_" + name)

        wg_raw = sb("wg_raw", [128, KD, NG])
        wg_hi = sb("wg_hi", [128, KD, NG], F32R)
        wg_lo = sb("wg_lo", [128, KD, NG], F32R)
        wt_raw = sb("wt_raw", [128, KD])
        bg = sb("bg", [PT, NG])
        be = sb("be", [NE, D])
        raw = [sb(f"f_raw{i}", [128, KD, D]) for i in range(2)]
        whi = [sb(f"f_whi{i}", [128, KD, D], F32R) for i in range(2)]
        wlo = [sb(f"f_wlo{i}", [128, KD, D], F32R) for i in range(2)]
        logit = sb("f_logit", [PT, NT, NG])
        prob = sb("f_prob", [PT, NT, NE])
        peak = sb("f_peak", [PT, NT])
        total = sb("f_total", [PT, NT])
        thr = sb("f_thr", [PT, NT])
        weight = sb("f_weight", [PT, NT, NE])
        weight_T = sb("f_weight_T", [NE, NT, PT])
        ps_turn = [pb(f"f_turn{i}", [128, 4, 128]) for i in range(2)]
        ps_logit = pb("f_ps_logit", [PT, NT, NG])
        ps_y = [pb(f"f_y{i}", [PT, D]) for i in range(NY)]
        g_loaded, thr_loaded = sem("g_loaded"), sem("thr_loaded")
        w_loaded = [sem(f"w_loaded{i}") for i in range(2)]
        pad_made, ghi_ready, glo_ready = sem("pad_made"), sem("ghi_ready"), sem("glo_ready")
        whi_ready, wlo_ready = sem("whi_ready"), sem("wlo_ready")
        logits_done, shifted, exped = sem("logits_done"), sem("shifted"), sem("exped")
        weights_ready, wt_turned, wt_ready = sem("weights_ready"), sem("wt_turned"), sem("wt_ready")
        y_done, y_added, stored, step = sem("y_done"), sem("y_added"), sem("stored"), sem("step")
        ln = Norm(nc, sems, ctx, "ln4", X, H, hT_hi, hT_lo, ps_turn, ident, eps_col)
        block = ctx.enter_context(nc.Block())

        @block.sync
        def _(sp):
            sp.dma_start(wg_raw[:, :, 0:NE], a["L1_ffn_W_gate"].rearrange("(k p) e -> p k e", p=128)).then_inc(g_loaded, 16)
            sp.dma_start(wt_raw[:, :], a["L1_ffn_W_thr"]).then_inc(thr_loaded, 16)
            sp.dma_start(bg[:, 0:NE], a["L1_ffn_b_gate"].partition_broadcast(PT)).then_inc(g_loaded, 16)
            sp.dma_start(bg[:, NE:NE + 1], a["L1_ffn_b_thr"].partition_broadcast(PT)).then_inc(g_loaded, 16)
            sp.dma_start(be[:, :], a["L1_ffn_b_exp"]).then_inc(g_loaded, 16)
            for x in range(NE):
                if x >= 2:
                    sp.wait_ge(wlo_ready, x - 1)
                sp.dma_start(raw[x % 2][:, :, :], a["L1_ffn_W_exp"][x].rearrange("(k p) f -> p k f", p=128)).then_inc(w_loaded[x % 2], 16)
            for t in range(NT):
                sp.wait_ge(y_added, NT * NE + t + 1)
                sp.dma_start(out[t * PT:(t + 1) * PT, :], X[:, t, :]).then_inc(stored, 16)
            sp.wait_ge(stored, 16 * NT)

        @block.gpsimd
        def _(pool):
            sems.clear(pool)
            nc.gpsimd.memset(wg_raw[:, :, NE + 1:NG], 0.0).then_inc(pad_made, 1)
            nc.gpsimd.memset(bg[:, NE + 1:NG], 0.0).then_inc(pad_made, 1)
            pool.wait_ge(thr_loaded, 16)
            nc.gpsimd.tensor_copy(wg_raw[:, :, NE], wt_raw[:, :]).then_inc(pad_made, 1)

        @block.scalar
        def _(act):
            ln.scalar(act)
            act.wait_ge(g_loaded, 64)
            act.wait_ge(pad_made, 3)
            nc.scalar.activation(wg_hi[:, :, :], wg_raw[:, :, :], ACT.Copy).then_inc(ghi_ready, 1)

            def split_w(x):
                act.wait_ge(w_loaded[x % 2], 16 * (x // 2 + 1))
                if x >= 2:
                    act.wait_ge(y_done, NT * x)
                nc.scalar.activation(whi[x % 2][:, :, :], raw[x % 2][:, :, :], ACT.Copy).then_inc(whi_ready, 1)

            split_w(0)
            act.wait_ge(shifted, 1)
            nc.scalar.activation(prob[:, :, :], logit[:, :, 0:NE], ACT.Exp).then_inc(exped, 1)
            nc.scalar.activation(thr[:, :], logit[:, :, NE], ACT.Exp, scale=-1.0).then_inc(exped, 1)
            for t in range(NT):
                act.wait_ge(wt_turned, t + 1)
                nc.scalar.activation(weight_T[:, t, :], ps_turn[t % 2][0:NE, 0, 0:PT], ACT.Copy).then_inc(wt_ready, 1)
            for x in range(1, NE):
                split_w(x)

        @block.vector
        def _(dve):
            link = chained(dve, step)
            ln.vector(dve, link)
            dve.wait_ge(ghi_ready, 1)
            nc.vector.tensor_tensor(wg_lo[:, :, :], wg_raw[:, :, :], wg_hi[:, :, :].bitcast(F32), ALU.subtract).then_inc(glo_ready, 1)

            def split_w(x):
                dve.wait_ge(whi_ready, x + 1)
                nc.vector.tensor_tensor(wlo[x % 2][:, :, :], raw[x % 2][:, :, :], whi[x % 2][:, :, :].bitcast(F32), ALU.subtract).then_inc(wlo_ready, 1)

            def spread(t):
                return t[:, :].unsqueeze(2).to_broadcast([PT, NT, NE])

            split_w(0)
            dve.wait_ge(logits_done, 1)
            link(nc.vector.tensor_tensor(logit[:, :, :], ps_logit[:, :, :], bg[:, :].unsqueeze(1).to_broadcast([PT, NT, NG]), ALU.add))
            link(nc.vector.tensor_reduce(peak[:, :], logit[:, :, 0:NE], AX.X, ALU.max))
            nc.vector.tensor_tensor(logit[:, :, 0:NE], logit[:, :, 0:NE], spread(peak), ALU.subtract).then_inc(shifted, 1)
            dve.wait_ge(exped, 2)
            link(nc.vector.tensor_reduce(total[:, :], prob[:, :, :], AX.X, ALU.add))
            link(nc.vector.reciprocal(total[:, :], total[:, :]))
            link(nc.vector.tensor_tensor(prob[:, :, :], prob[:, :, :], spread(total), ALU.mult))
            link(nc.vector.tensor_scalar(thr[:, :], thr[:, :], 1.0, None, ALU.add))
            link(nc.vector.reciprocal(thr[:, :], thr[:, :]))
            link(nc.vector.tensor_scalar(thr[:, :], thr[:, :], MAX_THRESHOLD, None, ALU.mult))
            link(nc.vector.tensor_tensor(weight[:, :, :], prob[:, :, :], spread(thr), ALU.subtract))
            link(nc.vector.tensor_scalar(weight[:, :, :], weight[:, :, :], 0.0, None, ALU.max))
            link(nc.vector.tensor_reduce(total[:, :], weight[:, :, :], AX.X, ALU.add))
            link(nc.vector.scalar_tensor_tensor(total[:, :], total[:, :], 0.0, total[:, :], ALU.is_equal, ALU.add))
            link(nc.vector.reciprocal(total[:, :], total[:, :]))
            nc.vector.tensor_tensor(weight[:, :, :], weight[:, :, :], spread(total), ALU.mult).then_inc(weights_ready, 1)
            split_w(1)
            for t in range(NT):
                dve.wait_ge(y_done, t + 1)
                nc.vector.tensor_tensor(X[:, t, :], X[:, t, :], ps_y[t % NY][:, :], ALU.add).then_inc(y_added, 1)
            dve.wait_ge(weights_ready, 1)
            for x in range(NE):
                if 1 <= x and x + 1 < NE:
                    split_w(x + 1)
                for t in range(NT):
                    n = NT * (x + 1) + t
                    dve.wait_ge(y_done, n + 1)
                    dve.wait_ge(y_added, n - NT + 1)
                    nc.vector.scalar_tensor_tensor(X[:, t, :], ps_y[n % NY][:, :], weight[:, t, x:x + 1], X[:, t, :],
                                                   ALU.mult, ALU.add).then_inc(y_added, 1)

        @block.tensor
        def _(pe):
            ln.tensor(pe)
            pe.wait_ge(ln.lo_ready, NT)
            pe.wait_ge(glo_ready, 1)
            for t in range(NT):
                tok = slice(t * PT, (t + 1) * PT)
                for k in range(KD):
                    last = three(nc, ps_logit[:, t, :], hT_hi[:, k, tok], hT_lo[:, k, tok], wg_hi[:, k, :], wg_lo[:, k, :],
                                 k == 0, k == KD - 1)
            last.then_inc(logits_done, 1)
            pe.wait_ge(weights_ready, 1)
            for t in range(NT):
                if t >= 2:
                    pe.wait_ge(wt_ready, t - 1)
                nc.tensor.transpose(ps_turn[t % 2][0:NE, 0, 0:PT], weight[:, t, :], ident[0:PT, 0:PT]).then_inc(wt_turned, 1)
            for t in range(NT):
                pe.wait_ge(wt_ready, t + 1)
                if t >= NY:
                    pe.wait_ge(y_added, t - NY + 1)
                nc.tensor.matmul(ps_y[t % NY][:, :], weight_T[:, t, :], be[:, :], start=True, stop=True).then_inc(y_done, 1)
            for x in range(NE):
                pe.wait_ge(wlo_ready, x + 1)
                for t in range(NT):
                    n = NT * (x + 1) + t
                    tok = slice(t * PT, (t + 1) * PT)
                    pe.wait_ge(y_added, n - NY + 1)
                    for k in range(KD):
                        last = three(nc, ps_y[n % NY][:, :], hT_hi[:, k, tok], hT_lo[:, k, tok], whi[x % 2][:, k, :], wlo[x % 2][:, k, :],
                                     k == 0, k == KD - 1)
                    last.then_inc(y_done, 1)


def build(nc, a, outs):
    with ExitStack() as ctx:
        def sb(name, shape, dt=F32):
            return ctx.enter_context(nc.sbuf_tensor(name, shape, dt))

        X = sb("X", [PT, NT, D])
        hT_hi = sb("hT_hi", [128, KD, N], F32R)
        hT_lo = sb("hT_lo", [128, KD, N], F32R)
        ident = sb("ident", [128, 128])
        eps_col = sb("eps_col", [128, 1])
        r = route_tensors(nc, ctx)
        sems = Semaphores(nc)
        with nc.sbuf_tensor("CT", [PT, NT, N], F32) as CT:
            with nc.sbuf_tensor("H1", [PT, NT, D], F32) as H:
                count_matrix_and_first_norm(nc, sems, a, X, H, hT_hi, hT_lo, ident, eps_col, CT)
                mean_aggregation(nc, sems, a, X, H, hT_hi, hT_lo, CT)
                dump(nc, sems, outs, "X1", X)
            with nc.sbuf_tensor("H2", [PT, NT, D], F32) as H:
                route_and_shared_expert(nc, sems, a, X, H, hT_hi, hT_lo, ident, eps_col, r)
                dump(nc, sems, outs, "X1s", X)
            routed_experts(nc, sems, a, ident, r)
            overfull_experts(nc, sems, a, ident, r)
            combine(nc, sems, X, CT, ident, r)
            dump(nc, sems, outs, "X2", X)
            with nc.sbuf_tensor("V", [PT, NT, HEADS, 64], F32) as V:
                with nc.sbuf_tensor("H3", [PT, NT, D], F32) as H:
                    project_qkv(nc, sems, a, X, H, hT_hi, hT_lo, ident, eps_col, V, r)
                attention(nc, sems, hT_hi, hT_lo, CT, V, r)
        attention_out(nc, sems, a, X, hT_hi, hT_lo)
        dump(nc, sems, outs, "X3", X)
        with nc.sbuf_tensor("H4", [PT, NT, D], F32) as H:
            gated_experts(nc, sems, a, X, H, hT_hi, hT_lo, ident, eps_col, outs["out"])


def dump(nc, sems, outs, name, X):
    if name not in outs:
        return
    with ExitStack() as ctx:
        done = sems.new(ctx, "dbg" + name)
        block = ctx.enter_context(nc.Block())

        @block.sync
        def _(sp):
            sp.dma_start(outs[name].rearrange("(t p) d -> p t d", p=PT), X[:, :, :]).then_inc(done, 16)
            sp.wait_ge(done, 16)


def kernel(**inputs):
    import numpy as _np
    import concourse.bacc as _bacc
    from concourse import mybir as _mybir
    from concourse.bass_utils import run_bass_kernel_spmd as _run

    nc = _bacc.Bacc("TRN2", target_bir_lowering=False, num_devices=1)
    arrays, a = {}, {}
    for name in inputs:
        v = _np.asarray(inputs[name])
        if name in ("L0_gnn_W_self", "L0_gnn_W_neigh"):
            v = v.T
        if name in ("L0_ffn_bs1", "L1_gnn_bq", "L1_gnn_bk", "L1_gnn_ba", "L1_ffn_W_thr"):
            v = v.reshape(-1, 128).T
        if name in ("L0_ffn_b1_sp", "L0_ffn_b1_fq"):
            v = v.reshape(8, 2, 128).transpose(2, 0, 1)
        v = _np.ascontiguousarray(v)
        arrays[f"in_{name}"] = v
        a[name] = nc.dram_tensor(f"in_{name}", v.shape, _mybir.dt.from_np(v.dtype), kind="ExternalInput").ap()
    outs = {"out": nc.dram_tensor("out_0", (N, D), F32, kind="ExternalOutput").ap()}
    for nm in DUMPS:
        outs[nm] = nc.dram_tensor(f"out_{nm}", (N, D), F32, kind="ExternalOutput").ap()
    build(nc, a, outs)
    r = _run(nc, [arrays], core_ids=[0])
    return r.results[0]["out_0"]
```

```python
from contextlib import ExitStack

import concourse.bass as bass
from concourse import mybir

F32 = mybir.dt.float32
F32R = mybir.dt.float32r
F16 = mybir.dt.float16
I32 = mybir.dt.int32
ALU = mybir.AluOpType
ACT = mybir.ActivationFunctionType
AX = mybir.AxisListType

N = 1250
D = 512
E = 40000
PT = 125
NT = N // PT
KD = D // 128
CHUNKS = [(0, 512), (512, 1024), (1024, N)]

WIN = 50
NWIN = N // WIN
CELLS = NT * WIN
EB = 512
NEB = (E + EB - 1) // EB
EC = EB // 128
TAIL = E - (NEB - 1) * EB
GT = 2
GW = GT * PT // WIN
NG = NT // GT
ROUND = 12582912.0
EPS = 1e-5


def chained(eng, sem):
    count = [0]

    def link(ins):
        count[0] += 1
        ins.then_inc(sem, 1)
        eng.wait_ge(sem, count[0])

    return link


class Semaphores:

    def __init__(self, nc):
        self.nc, self.used, self.stale = nc, [], []

    def new(self, ctx, name):
        handle = ctx.enter_context(self.nc.semaphore(name))
        self.used.append(handle)
        return handle

    def next_phase(self):
        self.used, self.stale = [], self.used

    def clear(self, pool):
        for handle in self.stale:
            pool.sem_clear(handle)


class Norm:

    def __init__(self, nc, sems, ctx, tag, X, H, hT_hi, hT_lo, ps, ident, eps_col):
        self.nc, self.X, self.H, self.hi, self.lo, self.ps, self.ident = nc, X, H, hT_hi, hT_lo, ps, ident
        self.eps_col = eps_col

        def sb(name, shape):
            return ctx.enter_context(nc.sbuf_tensor(f"{tag}_{name}", shape, F32))

        def sem(name):
            return sems.new(ctx, f"{tag}_{name}")

        self.stats = sb("stats", [PT, NT, 6])
        self.mv = sb("mv", [PT, NT, 2])
        self.sd = sb("sd", [PT, NT])
        self.rs = sb("rs", [PT, NT])
        self.t0 = sb("t0", [PT, NT])
        self.nmr = sb("nmr", [PT, NT])
        self.var_ready = sem("var_ready")
        self.sd_ready = sem("sd_ready")
        self.h_ready = sem("h_ready")
        self.turned = sem("turned")
        self.hi_ready = sem("hi_ready")
        self.lo_ready = sem("lo_ready")

    def vector(self, dve, link):
        nc = self.nc
        for t in range(NT):
            last = nc.vector.bn_stats(self.stats[:, t, :], self.X[:, t, :])
        link(last)
        for t in range(NT):
            last = nc.vector.bn_aggr(self.mv[:, t, :], self.stats[:, t, :])
        last.then_inc(self.var_ready, 1)
        dve.wait_ge(self.var_ready, 1)
        link(nc.vector.tensor_scalar(self.t0[:, :], self.mv[:, :, 1], EPS, -0.5, ALU.add, ALU.mult))
        dve.wait_ge(self.sd_ready, 1)
        link(nc.vector.reciprocal(self.rs[:, :], self.sd[:, :]))
        link(nc.vector.tensor_tensor(self.nmr[:, :], self.rs[:, :], self.rs[:, :], ALU.mult))
        link(nc.vector.tensor_tensor(self.nmr[:, :], self.nmr[:, :], self.t0[:, :], ALU.mult))
        link(nc.vector.scalar_tensor_tensor(self.rs[:, :], self.nmr[:, :], 1.5, self.rs[:, :], ALU.add, ALU.mult))
        link(nc.vector.scalar_tensor_tensor(self.nmr[:, :], self.mv[:, :, 0], -1.0, self.rs[:, :], ALU.mult, ALU.mult))
        for t in range(NT):
            nc.vector.tensor_scalar(self.H[:, t, :], self.X[:, t, :], self.rs[:, t:t + 1], self.nmr[:, t:t + 1],
                                    ALU.mult, ALU.add).then_inc(self.h_ready, 1)
        for t in range(NT):
            dve.wait_ge(self.hi_ready, t + 1)
            cols = slice(t * PT, (t + 1) * PT)
            nc.vector.tensor_tensor(self.lo[:, :, cols], self.ps[t % 2][:, :, 0:PT],
                                    self.hi[:, :, cols].bitcast(F32), ALU.subtract).then_inc(self.lo_ready, 1)

    def scalar(self, act):
        nc = self.nc
        act.wait_ge(self.var_ready, 1)
        nc.scalar.activation(self.sd[:, :], self.mv[:, :, 1], ACT.Sqrt, bias=self.eps_col[0:PT, :]).then_inc(self.sd_ready, 1)
        for t in range(NT):
            act.wait_ge(self.turned, t + 1)
            nc.scalar.activation(self.hi[:, :, t * PT:(t + 1) * PT], self.ps[t % 2][:, :, 0:PT],
                                 ACT.Copy).then_inc(self.hi_ready, 1)

    def tensor(self, pe):
        nc = self.nc
        for t in range(NT):
            pe.wait_ge(self.h_ready, t + 1)
            if t >= 2:
                pe.wait_ge(self.lo_ready, t - 1)
                pe.wait_ge(self.hi_ready, t - 1)
            for k in range(KD):
                last = nc.tensor.transpose(self.ps[t % 2][:, k, 0:PT], self.H[:, t, k * 128:(k + 1) * 128],
                                           self.ident[0:PT, 0:PT])
            last.then_inc(self.turned, 1)


def three(nc, out, a_hi, a_lo, b_hi, b_lo, start, stop):
    nc.tensor.matmul(out, a_lo, b_hi, start=start, stop=False)
    nc.tensor.matmul(out, a_hi, b_lo, start=False, stop=False)
    return nc.tensor.matmul(out, a_hi, b_hi, start=False, stop=stop)


def neighbour_mean_layer(nc, sems, a, X, H, hT_hi, hT_lo, ident, eps_col, CT):
    sems.next_phase()
    with ExitStack() as ctx:
        def sb(name, shape, dt=F32):
            return ctx.enter_context(nc.sbuf_tensor(name, shape, dt))

        def pb(name, shape, dt=F32):
            return ctx.enter_context(nc.psum_tensor(name, shape, dt))

        def sem(name):
            return sems.new(ctx, name)

        SLOTS = 2 * EC
        edges = sb("edges", [NEB, 2, EB], I32)
        edges_f = edges[:, :, :].bitcast(F32)
        reach = sb("reach", [NEB, 2])
        reach_b = sb("reach_b", [NEB, 2, NWIN])
        sender_tile = sb("sender_tile", [128, EC, NEB])
        sender_row = sb("sender_row", [128, EC, NEB])
        window = sb("window", [128, EC, NEB])
        cell = sb("cell", [128, EC, NEB])
        iota_b = sb("iota_b", [NWIN, NEB])
        win_first = sb("win_first", [NWIN, 1])
        meets = sb("meets", [NWIN, NEB])
        cand = sb("cand", [NWIN, 2, NEB])
        span = sb("span", [NWIN, 2])
        span_row = sb("span_row", [1, 2 * NWIN], I32)
        iota_c = sb("iota_c", [128, CELLS], F16)
        rows1h = sb("rows1h", [128, SLOTS, PT], F16)
        cells1h = sb("cells1h", [128, SLOTS, CELLS], F16)
        zeros = sb("zeros", [128, CELLS], F16)
        ps_turn = [pb(f"ps_turn{i}", [128, 4, 128]) for i in range(2)]
        ps_span = pb("ps_span", [128, 512])
        w_raw = sb("w_raw", [128, KD, D])
        w_hi = [sb(f"w_hi{i}", [128, KD, D], F32R) for i in range(2)]
        w_lo = [sb(f"w_lo{i}", [128, KD, D], F32R) for i in range(2)]
        agg_hi = sb("agg_hi", [128, KD, GT * PT], F32R)
        agg_lo = sb("agg_lo", [128, KD, GT * PT], F32R)
        bias = sb("bias", [PT, D])
        ones = sb("ones", [PT, 1])
        rdeg = sb("rdeg", [PT, NT])
        mean = [sb(f"mean{i}", [PT, D]) for i in range(2)]
        ps_agg = [pb(f"ps_agg{i}", [128, 512]) for i in range(2)]
        ps_self = ps_turn
        ps_count = [pb(f"ps_count{i}", [PT, NT, WIN]) for i in range(2)]

        made = sem("made")
        edges_loaded = sem("edges_loaded")
        edges_ready = sem("edges_ready")
        reach_ready = sem("reach_ready")
        edges_turned = sem("edges_turned")
        edges_taken = sem("edges_taken")
        reach_spread = sem("reach_spread")
        span_ready = sem("span_ready")
        span_turned = sem("span_turned")
        span_known = sem("span_known")
        onehot_ready = sem("onehot_ready")
        onehot_used = sem("onehot_used")
        counted = sem("counted")
        copied = sem("copied")
        x_loaded = sem("x_loaded")
        dve_step = sem("dve_step")
        w_loaded = sem("g_w_loaded")
        bias_loaded = sem("g_bias_loaded")
        whi_ready = sem("g_whi_ready")
        wlo_ready = sem("g_wlo_ready")
        deg_done = sem("deg_done")
        rdeg_ready = sem("rdeg_ready")
        agg_done = sem("agg_done")
        agghi_ready = sem("agghi_ready")
        agglo_ready = sem("agglo_ready")
        self_done = sem("self_done")
        neigh_done = sem("neigh_done")
        mean_ready = sem("mean_ready")
        self_added = sem("self_added")
        summed = sem("g_summed")
        pool_step = sem("g_pool_step")
        ln = Norm(nc, sems, ctx, "ln1", X, H, hT_hi, hT_lo, ps_turn, ident, eps_col)
        block = ctx.enter_context(nc.Block())

        @block.sync
        def _(sp):
            full = (NEB - 1) * EB
            for i, name in enumerate(("dst", "src")):
                sp.dma_start(edges[0:NEB - 1, i, :], a[name][0:full].rearrange("(b q) -> b q", q=EB)).then_inc(edges_loaded, 16)
                for j in range(EB // TAIL):
                    sp.dma_start(edges[NEB - 1:NEB, i, j * TAIL:(j + 1) * TAIL],
                                 a[name][full:E].rearrange("(b q) -> b q", b=1)).then_inc(edges_loaded, 16)
            for t in range(NT):
                sp.dma_start(X[:, t, :], a["x"][t * PT:(t + 1) * PT, :]).then_inc(x_loaded, 16)
            for i, name in enumerate(("L0_gnn_W_self", "L0_gnn_W_neigh")):
                if i:
                    sp.wait_ge(wlo_ready, i)
                sp.dma_start(w_raw[:, :, :], a[name].rearrange("(k p) n -> p k n", p=128)).then_inc(w_loaded, 16)
            sp.dma_start(bias[:, :], a["L0_gnn_b"].partition_broadcast(PT)).then_inc(bias_loaded, 16)

        @block.gpsimd
        def _(pool):
            sems.clear(pool)
            nc.gpsimd.memset(ident[:, :], 0.0).then_inc(made, 1)
            nc.gpsimd.memset(eps_col[:, :], EPS).then_inc(made, 1)
            nc.gpsimd.memset(zeros[:, :], 0.0).then_inc(made, 1)
            nc.gpsimd.iota(iota_c[:, :], [[1, CELLS]], base=0, channel_multiplier=0,
                           allow_small_or_imprecise_dtypes=True).then_inc(made, 1)
            nc.gpsimd.memset(ones[:, :], 1.0).then_inc(made, 1)
            nc.gpsimd.iota(iota_b[:, :], [[1, NEB]], base=0, channel_multiplier=0,
                           allow_small_or_imprecise_dtypes=True).then_inc(made, 1)
            nc.gpsimd.iota(win_first[:, :], [[1, 1]], base=0, channel_multiplier=WIN,
                           allow_small_or_imprecise_dtypes=True).then_inc(made, 1)
            pool.wait_ge(made, 1)
            nc.gpsimd.affine_select(out=ident[:, :], in_=ident[:, :], compare_op=ALU.not_equal, fill=1.0,
                                    base=0, pattern=[[-1, 128]], channel_multiplier=1).then_inc(made, 1)
            for i in range(2):
                pool.wait_ge(w_loaded, 16 * (i + 1))
                pool.wait_ge(whi_ready, i + 1)
                nc.gpsimd.tensor_tensor(w_lo[i][:, :, :], w_raw[:, :, :], w_hi[i][:, :, :].bitcast(F32),
                                        ALU.subtract).then_inc(wlo_ready, 1)
            pool.wait_ge(bias_loaded, 16)
            for t in range(NT):
                m = mean[t % 2]
                pool.wait_ge(self_added, t + 1)
                nc.gpsimd.tensor_tensor(m[:, :], m[:, :], bias[:, :], ALU.add).then_inc(pool_step, 1)
                pool.wait_ge(pool_step, 2 * t + 1)
                nc.gpsimd.tensor_scalar(m[:, :], m[:, :], 0.0, None, ALU.max).then_inc(pool_step, 1)
                pool.wait_ge(pool_step, 2 * t + 2)
                nc.gpsimd.tensor_tensor(X[:, t, :], m[:, :], X[:, t, :], ALU.add).then_inc(summed, 1)

        @block.vector
        def _(dve):
            link = chained(dve, dve_step)
            dve.wait_ge(edges_loaded, 32 * (1 + EB // TAIL))
            nc.vector.tensor_copy(edges_f, edges[:, :, :]).then_inc(edges_ready, 1)
            dve.wait_ge(edges_ready, 1)
            nc.vector.tensor_reduce(reach[:, 0:1], edges_f[:, 0, :], AX.X, ALU.min)
            link(nc.vector.tensor_reduce(reach[:, 1:2], edges_f[:, 0, :], AX.X, ALU.max))
            for i in range(2):
                last = nc.vector.tensor_scalar(reach_b[:, i, :], edges_f[:, 0, 0:NWIN], 0.0, reach[:, i:i + 1],
                                               ALU.mult, ALU.add)
            last.then_inc(reach_ready, 1)
            dve.wait_ge(edges_turned, 2)
            dst_t, src_t = (ps_turn[i][:, 0:EC, 0:NEB] for i in range(2))
            link(nc.vector.tensor_scalar(sender_tile[:, :, :], src_t, 1.0 / PT, -(PT - 1) / (2 * PT), ALU.mult, ALU.add))
            link(nc.vector.tensor_scalar(sender_tile[:, :, :], sender_tile[:, :, :], ROUND, -ROUND, ALU.add, ALU.add))
            link(nc.vector.scalar_tensor_tensor(sender_row[:, :, :], sender_tile[:, :, :], -float(PT), src_t, ALU.mult, ALU.add))
            link(nc.vector.tensor_scalar(window[:, :, :], dst_t, 1.0 / WIN, -(WIN - 1) / (2 * WIN), ALU.mult, ALU.add))
            link(nc.vector.tensor_scalar(window[:, :, :], window[:, :, :], ROUND, -ROUND, ALU.add, ALU.add))
            link(nc.vector.scalar_tensor_tensor(cell[:, :, :], window[:, :, :], float(CELLS - WIN), dst_t, ALU.mult, ALU.add))
            link(nc.vector.scalar_tensor_tensor(cell[:, :, :], sender_tile[:, :, :], float(WIN), cell[:, :, :], ALU.mult, ALU.add))
            first, used = TAIL // 128, TAIL % 128
            nc.vector.memset(cell[used:128, first, NEB - 1:NEB], -1.0e6)
            link(nc.vector.memset(cell[:, first + 1:EC, NEB - 1:NEB], -1.0e6))
            nc.vector.tensor_copy(window[0:1, 0, 0:1], cell[0:1, 0, 0:1]).then_inc(edges_taken, 1)
            dve.wait_ge(made, 8)
            dve.wait_ge(reach_spread, 1)
            low, high = ps_span[0:NWIN, 0:NEB], ps_span[0:NWIN, 128:128 + NEB]
            link(nc.vector.tensor_scalar(meets[:, :], high, win_first[:, :], None, ALU.is_ge))
            link(nc.vector.tensor_scalar(cand[:, 0, :], low, win_first[:, :], float(WIN - 1), ALU.subtract, ALU.is_le))
            link(nc.vector.tensor_tensor(meets[:, :], meets[:, :], cand[:, 0, :], ALU.mult))
            nc.vector.scalar_tensor_tensor(cand[:, 1, :], iota_b[:, :], 1.0, meets[:, :], ALU.add, ALU.mult)
            link(nc.vector.scalar_tensor_tensor(cand[:, 0, :], iota_b[:, :], -float(NEB), meets[:, :], ALU.add, ALU.mult))
            nc.vector.tensor_reduce(span[:, 1:2], cand[:, 1, :], AX.X, ALU.max)
            link(nc.vector.tensor_reduce(span[:, 0:1], cand[:, 0, :], AX.X, ALU.min))
            link(nc.vector.tensor_scalar(span[:, 0:1], span[:, 0:1], float(NEB), float(NEB - 1), ALU.add, ALU.min))
            nc.vector.scalar_tensor_tensor(span[:, 1:2], span[:, 0:1], 1.0, span[:, 1:2], ALU.add, ALU.max).then_inc(span_ready, 1)
            dve.wait_ge(span_turned, 1)
            nc.vector.tensor_copy(span_row[:, :], ps_span[0:1, 256:256 + 2 * NWIN]).then_inc(span_known, 1)
            dve.wait_ge(span_known, 1)
            dve.wait_ge(x_loaded, 16 * NT)
            ln.vector(dve, link)
            done = dve.alloc_register("dve_chunks")
            slot = dve.alloc_register("dve_slot")
            dve.reg_mov(done, 0)
            dve.reg_mov(slot, 0)
            for w in range(NWIN + GW + 1):
                if w < NWIN:
                    lo_b = dve.value_load(span_row[0:1, w:w + 1], min_val=0, max_val=NEB - 1)
                    hi_b = dve.value_load(span_row[0:1, NWIN + w:NWIN + w + 1], min_val=1, max_val=NEB)
                    with dve.Fori(lo_b, hi_b) as b:
                        n = dve.snap(done, min_val=0, max_val=NWIN * NEB * EC)
                        s = dve.snap(slot, min_val=0, max_val=EC)
                        dve.wait_ge(onehot_used, n + EC)
                        for j in range(EC):
                            nc.vector.tensor_scalar(rows1h[:, bass.DynSlice(s + j, 1), :], iota_c[:, 0:PT].unsqueeze(1),
                                                    sender_row[:, j, bass.DynSlice(b, 1)], None, ALU.is_equal)
                            last = nc.vector.tensor_scalar(cells1h[:, bass.DynSlice(s + j, 1), :], iota_c[:, :].unsqueeze(1),
                                                           cell[:, j, bass.DynSlice(b, 1)], -float(CELLS * w),
                                                           ALU.subtract, ALU.is_equal)
                        last.then_inc(onehot_ready, EC)
                        dve.reg_add(done, done, EC)
                        dve.reg_mod(slot, done, SLOTS)
                if w <= GW:
                    continue
                g, k = divmod(w - GW - 1, GW)
                if k == 0:
                    dve.wait_ge(deg_done, g + 1)
                    cols = rdeg[:, g * GT:(g + 1) * GT]
                    link(nc.vector.tensor_scalar(cols, ps_span[0:PT, g * GT:(g + 1) * GT], 1.0, None, ALU.max))
                    nc.vector.reciprocal(cols, cols).then_inc(rdeg_ready, 1)
                if k < KD:
                    dve.wait_ge(agghi_ready, g * KD + k + 1)
                    nc.vector.tensor_tensor(agg_lo[:, k, :], ps_agg[k % 2][:, 0:GT * PT],
                                            agg_hi[:, k, :].bitcast(F32), ALU.subtract).then_inc(agglo_ready, 1)
                else:
                    for t in range(g * GT, (g + 1) * GT):
                        dve.wait_ge(self_done, t + 1)
                        dve.wait_ge(mean_ready, t + 1)
                        nc.vector.tensor_tensor(mean[t % 2][:, :], mean[t % 2][:, :], ps_self[t % 2][0:PT, :, :].rearrange("p a b -> p (a b)"),
                                                ALU.add).then_inc(self_added, 1)

        @block.tensor
        def _(pe):
            pe.wait_ge(made, 8)
            pe.wait_ge(edges_ready, 1)
            for i in range(2):
                for j in range(EC):
                    last = nc.tensor.transpose(ps_turn[i][:, j, 0:NEB], edges_f[:, i, j * 128:(j + 1) * 128],
                                               ident[0:NEB, 0:NEB])
                last.then_inc(edges_turned, 1)
            pe.wait_ge(reach_ready, 1)
            for i in range(2):
                last = nc.tensor.matmul(ps_span[0:NWIN, i * 128:i * 128 + NEB], reach_b[:, i, :], ident[0:NEB, 0:NEB],
                                        start=True, stop=True)
            last.then_inc(reach_spread, 1)
            pe.wait_ge(span_ready, 1)
            for i in range(2):
                last = nc.tensor.matmul(ps_span[0:1, 256 + i * NWIN:256 + (i + 1) * NWIN], span[:, i:i + 1],
                                        ident[0:NWIN, 0:NWIN], start=True, stop=True)
            last.then_inc(span_turned, 1)
            pe.wait_ge(edges_taken, 1)
            ln.tensor(pe)
            pe.wait_ge(span_known, 1)
            pe.sem_inc(onehot_used, SLOTS)
            done = pe.alloc_register("pe_chunks")
            slot = pe.alloc_register("pe_slot")
            pe.reg_mov(done, 0)
            pe.reg_mov(slot, 0)

            def self_product(t):
                if t == 0:
                    pe.wait_ge(wlo_ready, 1)
                    pe.wait_ge(ln.hi_ready, NT)
                    pe.wait_ge(ln.lo_ready, NT)
                if t >= 2:
                    pe.wait_ge(self_added, t - 1)
                tok = slice(t * PT, (t + 1) * PT)
                for k in range(KD):
                    last = three(nc, ps_self[t % 2][0:PT, :, :], hT_hi[:, k, tok], hT_lo[:, k, tok],
                                 w_hi[0][:, k, :], w_lo[0][:, k, :], k == 0, k == KD - 1)
                last.then_inc(self_done, 1)

            def neighbours_product(t):
                if t == 0:
                    pe.wait_ge(wlo_ready, 2)
                if t % GT == 0:
                    pe.wait_ge(agglo_ready, (t // GT + 1) * KD)
                tok = slice(t % GT * PT, (t % GT + 1) * PT)
                for k in range(KD):
                    last = three(nc, ps_agg[t % 2][0:PT, :], agg_hi[:, k, tok], agg_lo[:, k, tok],
                                 w_hi[1][:, k, :], w_lo[1][:, k, :], k == 0, k == KD - 1)
                last.then_inc(neigh_done, 1)

            def aggregate(g, f):
                cols = slice(g * GT * PT, (g + 1) * GT * PT)
                if f == 0:
                    pe.wait_ge(copied, (g + 1) * GW + 2)
                    for d in range(g * GT, (g + 1) * GT):
                        for s in range(NT):
                            last = nc.tensor.matmul(ps_span[0:PT, d:d + 1], CT[:, s, d * PT:(d + 1) * PT], ones[:, :],
                                                    start=(s == 0), stop=(s == NT - 1))
                    last.then_inc(deg_done, 1)
                if f >= 2:
                    pe.wait_ge(agglo_ready, g * KD + f - 1)
                elif g:
                    pe.wait_ge(mean_ready, (g - 1) * GT + f + 1)
                for s in range(NT):
                    last = nc.tensor.matmul(ps_agg[f % 2][:, 0:GT * PT], H[:, s, f * 128:(f + 1) * 128],
                                            CT[:, s, cols], start=(s == 0), stop=(s == NT - 1))
                last.then_inc(agg_done, 1)

            for w in range(NWIN + GW):
                if w < NWIN:
                    ps = ps_count[w % 2]
                    lo_b = pe.value_load(span_row[0:1, w:w + 1], min_val=0, max_val=NEB - 1)
                    hi_b = pe.value_load(span_row[0:1, NWIN + w:NWIN + w + 1], min_val=1, max_val=NEB)
                    if w >= 2:
                        pe.wait_ge(copied, w + 1)
                    nc.tensor.matmul(ps[:, :, :], zeros[:, 0:PT], zeros[:, :], start=True, stop=False, skip_group_check=True)
                    with pe.Fori(lo_b, hi_b):
                        n = pe.snap(done, min_val=0, max_val=NWIN * NEB * EC)
                        so = pe.snap(slot, min_val=0, max_val=EC)
                        pe.wait_ge(onehot_ready, n + EC)
                        for j in range(EC):
                            last = nc.tensor.matmul(ps[:, :, :], rows1h[:, bass.DynSlice(so + j, 1), :],
                                                    cells1h[:, bass.DynSlice(so + j, 1), :],
                                                    start=False, stop=False, skip_group_check=True)
                        last.then_inc(onehot_used, EC)
                        pe.reg_add(done, done, EC)
                        pe.reg_mod(slot, done, SLOTS)
                    nc.tensor.matmul(ps[:, 0, 0:2], zeros[:, 0:PT], zeros[:, 0:2], start=False, stop=True,
                                     skip_group_check=True).then_inc(counted, 1)
                if w < GW:
                    continue
                g, k = divmod(w - GW, GW)
                if k < KD:
                    aggregate(g, k)
                if k >= KD - 1:
                    self_product(g * GT + k - (KD - 1))
                if k == KD:
                    for t in range(g * GT, (g + 1) * GT):
                        neighbours_product(t)

        @block.scalar
        def _(act):
            act.wait_ge(made, 8)
            ln.scalar(act)
            for i in range(2):
                act.wait_ge(w_loaded, 16 * (i + 1))
                nc.scalar.activation(w_hi[i][:, :, :], w_raw[:, :, :], ACT.Copy).then_inc(whi_ready, 1)
            act.sem_inc(copied, 2)
            for w in range(NWIN + GW):
                if w < NWIN:
                    act.wait_ge(counted, w + 1)
                    nc.scalar.activation(CT[:, :, w * WIN:(w + 1) * WIN], ps_count[w % 2][:, :, :],
                                         ACT.Copy).then_inc(copied, 1)
                if w < GW:
                    continue
                g, k = divmod(w - GW, GW)
                if k < KD:
                    if k == 0 and g:
                        act.wait_ge(neigh_done, g * GT)
                    act.wait_ge(agg_done, g * KD + k + 1)
                    nc.scalar.activation(agg_hi[:, k, :], ps_agg[k % 2][:, 0:GT * PT], ACT.Copy).then_inc(agghi_ready, 1)
                    continue
                act.wait_ge(rdeg_ready, g + 1)
                for t in range(g * GT, (g + 1) * GT):
                    act.wait_ge(neigh_done, t + 1)
                    if t >= 2:
                        act.wait_ge(summed, t - 1)
                    nc.scalar.activation(mean[t % 2][:, :], ps_agg[t % 2][0:PT, :], ACT.Copy,
                                         scale=rdeg[:, t:t + 1]).then_inc(mean_ready, 1)




NB = 2
NE = 8
NX = NB * NE
FF = 256
KF = FF // 128
FIRST_ROWS = 256
MORE_ROWS = 128
ROUNDS = (N - FIRST_ROWS + MORE_ROWS - 1) // MORE_ROWS
MORE_FROM = NX * FIRST_ROWS
ROWS = MORE_FROM + NB * ROUNDS * MORE_ROWS
BANKS = ("sp", "fq")


class Route:
    pass


def route_tensors(nc, ctx):
    r = Route()

    def sb(name, shape, dt=F32):
        return ctx.enter_context(nc.sbuf_tensor(name, shape, dt))

    r.gate = sb("gate", [PT, NT, NB])
    r.slot = sb("slot", [PT, NT, NB], I32)
    r.rounds = sb("rounds", [1, NX], I32)
    r.h_rows = nc.dram_tensor("h_rows", (N, D), F32).ap()
    r.y_rows = nc.dram_tensor("y_rows", (ROWS, D), F32).ap()
    r.token_of = nc.dram_tensor("token_of", (ROWS, 1), I32).ap()
    r.qk = nc.dram_tensor("qk_rows", (4, FF, N), F32).ap()
    return r


def route_and_shared_expert(nc, sems, a, X, H, hT_hi, hT_lo, ident, eps_col, r):
    UNITS = [(m, c) for m in range(KF) for c in range(len(CHUNKS))]
    sems.next_phase()
    with ExitStack() as ctx:
        def sb(name, shape, dt=F32):
            return ctx.enter_context(nc.sbuf_tensor(name, shape, dt))

        def pb(name, shape, dt=F32):
            return ctx.enter_context(nc.psum_tensor(name, shape, dt))

        def sem(name):
            return sems.new(ctx, "r_" + name)

        wr_raw = sb("wr_raw", [128, KD, NX])
        wr_hi = sb("wr_hi", [128, KD, NX], F32R)
        wr_lo = sb("wr_lo", [128, KD, NX], F32R)
        br = sb("br", [PT, NX])
        s_raw = sb("s_raw", [128, 2048])
        s_hi = sb("s_hi", [128, 2048], F32R)
        s_lo = sb("s_lo", [128, 2048], F32R)
        bs1 = sb("bs1", [128, KF])
        bs2 = sb("bs2", [PT, D])
        act1 = [sb(f"act1_{i}", [128, 512]) for i in range(2)]
        gT_hi = sb("gT_hi", [128, KF, N], F32R)
        gT_lo = sb("gT_lo", [128, KF, N], F32R)
        y = [sb(f"ys{i}", [PT, D]) for i in range(2)]
        logit = sb("logit", [PT, NT, NX])
        work = sb("work", [PT, NT, NX])
        prob = sb("prob", [PT, NT, NX])
        peak = sb("peak", [PT, NT * NB])
        onehot = sb("onehot", [PT, NT, NX])
        onehot16 = sb("onehot16", [PT, NT, NX], F16)
        slot_f = sb("slot_f", [PT, NT * NB])
        falling = sb("falling", [PT, NT * NB, NE])
        row0 = sb("row0", [PT, NT, NX])
        before = sb("before", [PT, NX])
        ones16 = sb("ones16", [PT, NX])
        jump = sb("jump", [PT, NX])
        zero_f = sb("zero_f", [128, D])
        upto = sb("upto", [PT, PT], F16)
        every = sb("every", [PT, PT], F16)
        zero_i = sb("zero_i", [128, ROWS // 128], I32)
        token = sb("token", [PT, NT], I32)
        more = sb("more", [PT, NX])
        kth = sb("kth", [PT, NX])
        ps_turn = [pb(f"r_turn{i}", [128, 4, 128]) for i in range(2)]
        ps_logit = pb("ps_logit", [PT, NT, NX])
        ps_rank = pb("ps_rank", [PT, 512])
        ps_up = [pb(f"ps_up{i}", [128, 512]) for i in range(2)]
        ps_down = [pb(f"ps_down{i}", [PT, D]) for i in range(2)]

        w_loaded, b_loaded = sem("w_loaded"), sem("b_loaded")
        whi_ready, wlo_ready = sem("whi_ready"), sem("wlo_ready")
        made, saved = sem("made"), sem("saved")
        logits_done, shifted, exped = sem("logits_done"), sem("shifted"), sem("exped")
        onehot_ready, ranked = sem("onehot_ready"), sem("ranked")
        slot_ready, cleared, scattered = sem("slot_ready"), sem("cleared"), sem("scattered")
        up_done, act_ready, ghi_ready, glo_ready = sem("up_done"), sem("act_ready"), sem("ghi_ready"), sem("glo_ready")
        down_done, y_ready, step = sem("down_done"), sem("y_ready"), sem("step")
        ln = Norm(nc, sems, ctx, "ln2", X, H, hT_hi, hT_lo, ps_turn, ident, eps_col)
        block = ctx.enter_context(nc.Block())
        w1 = (s_hi[:, 0:1024].rearrange("p (k f) -> p k f", k=KD), s_lo[:, 0:1024].rearrange("p (k f) -> p k f", k=KD))
        w2 = (s_hi[:, 1024:2048].rearrange("p (k f) -> p k f", k=KF), s_lo[:, 1024:2048].rearrange("p (k f) -> p k f", k=KF))

        @block.sync
        def _(sp):
            for b, bank in enumerate(BANKS):
                sp.dma_start(wr_raw[:, :, b * NE:(b + 1) * NE],
                             a[f"L0_ffn_Wr_{bank}"].rearrange("(k p) e -> p k e", p=128)).then_inc(w_loaded, 16)
                sp.dma_start(br[:, b * NE:(b + 1) * NE], a[f"L0_ffn_br_{bank}"].partition_broadcast(PT)).then_inc(b_loaded, 16)
            sp.dma_start(s_raw[:, 0:1024].rearrange("p (k f) -> p k f", k=KD),
                         a["L0_ffn_Ws1"].rearrange("(k p) f -> p k f", p=128)).then_inc(w_loaded, 16)
            sp.dma_start(s_raw[:, 1024:2048].rearrange("p (k f) -> p k f", k=KF),
                         a["L0_ffn_Ws2"].rearrange("(k p) f -> p k f", p=128)).then_inc(w_loaded, 16)
            sp.dma_start(bs1[:, :], a["L0_ffn_bs1"]).then_inc(b_loaded, 16)
            sp.dma_start(bs2[:, :], a["L0_ffn_bs2"].partition_broadcast(PT)).then_inc(b_loaded, 16)
            sp.wait_ge(made, 4)
            sp.dma_start(r.token_of.rearrange("(p f) o -> p (f o)", p=128), zero_i[:, :]).then_inc(cleared, 16)
            sp.dma_start(r.y_rows[MORE_FROM:ROWS, :].rearrange("(p i) d -> p i d", p=128),
                         zero_f[:, :].unsqueeze(1).to_broadcast([128, (ROWS - MORE_FROM) // 128, D])).then_inc(saved, 16)
            for t in range(NT):
                sp.wait_ge(ln.h_ready, t + 1)
                sp.dma_start(r.h_rows[t * PT:(t + 1) * PT, :], H[:, t, :]).then_inc(saved, 16)
            sp.wait_ge(saved, 16 * (NT + 1))

        @block.gpsimd
        def _(pool):
            sems.clear(pool)
            small = dict(allow_small_or_imprecise_dtypes=True)
            nc.gpsimd.memset(every[:, :], 1.0).then_inc(made, 1)
            nc.gpsimd.memset(zero_i[:, :], 0).then_inc(made, 1)
            nc.gpsimd.memset(zero_f[:, :], 0.0).then_inc(made, 1)
            nc.gpsimd.memset(ones16[:, :], 1.0).then_inc(made, 1)
            nc.gpsimd.iota(token[:, :], [[PT, NT]], base=0, channel_multiplier=1).then_inc(made, 1)
            nc.gpsimd.iota(falling[:, :, :], [[0, NT * NB], [-1, NE]], base=NE, channel_multiplier=0, **small).then_inc(made, 1)
            nc.gpsimd.iota(row0[:, :, :], [[0, NT], [FIRST_ROWS, NX]], base=-1, channel_multiplier=0, **small).then_inc(made, 1)
            pool.wait_ge(made, 2)
            nc.gpsimd.affine_select(out=upto[:, :], in_=every[:, :], compare_op=ALU.is_ge, fill=0.0,
                                    base=0, pattern=[[1, PT]], channel_multiplier=-1).then_inc(made, 1)
            pool.wait_ge(cleared, 16)
            pool.wait_ge(slot_ready, 1)
            pool.wait_ge(made, 8)
            for t in range(NT):
                for b in range(NB):
                    nc.gpsimd.indirect_dma_start(
                        out=r.token_of, out_offset=bass.IndirectOffsetOnAxis(ap=r.slot[:, t, b:b + 1], axis=0),
                        in_=token[:, t:t + 1], in_offset=None).then_inc(scattered, 16)
            pool.wait_ge(scattered, 16 * NT * NB)

        @block.scalar
        def _(act):
            ln.scalar(act)
            act.wait_ge(w_loaded, 64)
            nc.scalar.activation(wr_hi[:, :, :], wr_raw[:, :, :], ACT.Copy).then_inc(whi_ready, 1)
            nc.scalar.activation(s_hi[:, :], s_raw[:, :], ACT.Copy).then_inc(whi_ready, 1)
            act.wait_ge(shifted, 1)
            nc.scalar.activation(prob[:, :, :], logit[:, :, :], ACT.Exp).then_inc(exped, 1)
            act.wait_ge(b_loaded, 64)
            for u, (m, c) in enumerate(UNITS):
                c0, c1 = CHUNKS[c]
                act.wait_ge(up_done, u + 1)
                if u >= 2:
                    act.wait_ge(glo_ready, u - 1)
                nc.scalar.activation(act1[u % 2][:, 0:c1 - c0], ps_up[u % 2][:, 0:c1 - c0], ACT.Gelu,
                                     bias=bs1[:, m:m + 1]).then_inc(act_ready, 1)
                act.wait_ge(act_ready, u + 1)
                nc.scalar.activation(gT_hi[:, m, c0:c1], act1[u % 2][:, 0:c1 - c0], ACT.Copy).then_inc(ghi_ready, 1)

        @block.vector
        def _(dve):
            link = chained(dve, step)
            ln.vector(dve, link)
            dve.wait_ge(whi_ready, 2)
            nc.vector.tensor_tensor(wr_lo[:, :, :], wr_raw[:, :, :], wr_hi[:, :, :].bitcast(F32), ALU.subtract).then_inc(wlo_ready, 1)
            nc.vector.tensor_tensor(s_lo[:, :], s_raw[:, :], s_hi[:, :].bitcast(F32), ALU.subtract).then_inc(wlo_ready, 1)

            def banked(t):
                return t[:, :, :].rearrange("p t (b e) -> p (t b) e", b=NB)

            def spread(t):
                return t[:, :].unsqueeze(2).to_broadcast([PT, NT * NB, NE])

            dve.wait_ge(logits_done, 1)
            dve.wait_ge(b_loaded, 64)
            dve.wait_ge(made, 8)
            link(nc.vector.tensor_tensor(logit[:, :, :], ps_logit[:, :, :],
                                         br[:, :].unsqueeze(1).to_broadcast([PT, NT, NX]), ALU.add))
            link(nc.vector.tensor_reduce(peak[:, :], banked(logit), AX.X, ALU.max))
            nc.vector.tensor_tensor(banked(logit), banked(logit), spread(peak), ALU.subtract).then_inc(shifted, 1)
            dve.wait_ge(shifted, 1)
            link(nc.vector.scalar_tensor_tensor(banked(work), banked(logit), 0.0, falling[:, :, :], ALU.is_ge, ALU.mult))
            link(nc.vector.tensor_reduce(peak[:, :], banked(work), AX.X, ALU.max))
            link(nc.vector.tensor_tensor(banked(onehot), banked(work), spread(peak), ALU.is_equal))
            nc.vector.tensor_copy(onehot16[:, :, :], onehot[:, :, :]).then_inc(onehot_ready, 1)
            dve.wait_ge(exped, 1)
            link(nc.vector.tensor_reduce(peak[:, :], banked(prob), AX.X, ALU.add))
            link(nc.vector.reciprocal(r.gate[:, :, :].rearrange("p t b -> p (t b)"), peak[:, :]))
            dve.wait_ge(ranked, 1)
            total = ps_rank[:, NT * NX:(NT + 1) * NX]
            link(nc.vector.tensor_scalar(more[:, :], total, float(FIRST_ROWS), None, ALU.is_gt))
            for k in range(1, ROUNDS):
                link(nc.vector.tensor_scalar(kth[:, :], total, float(FIRST_ROWS + k * MORE_ROWS), None, ALU.is_gt))
                link(nc.vector.tensor_tensor(more[:, :], more[:, :], kth[:, :], ALU.add))
            nc.vector.tensor_copy(r.rounds[:, :], more[0:1, :])
            link(nc.vector.tensor_tensor_scan(before[:, :], ones16[:, :], more[:, :], 0.0, ALU.mult, ALU.add))
            link(nc.vector.tensor_tensor(before[:, :], before[:, :], more[:, :], ALU.subtract))
            link(nc.vector.tensor_scalar(before[:, :], before[:, :], float(MORE_ROWS), float(MORE_FROM - FIRST_ROWS - 1),
                                         ALU.mult, ALU.add))
            link(nc.vector.tensor_tensor(jump[:, :], before[:, :], row0[:, 0, :], ALU.subtract))
            upto_now = ps_rank[:, 0:NT * NX].rearrange("p (t e) -> p t e", e=NX)
            link(nc.vector.tensor_scalar(work[:, :, :], upto_now, float(FIRST_ROWS), None, ALU.is_gt))
            link(nc.vector.tensor_tensor(work[:, :, :], work[:, :, :], jump[:, :].unsqueeze(1).to_broadcast([PT, NT, NX]), ALU.mult))
            link(nc.vector.tensor_tensor(work[:, :, :], work[:, :, :], upto_now, ALU.add))
            link(nc.vector.tensor_tensor(work[:, :, :], work[:, :, :], row0[:, :, :], ALU.add))
            link(nc.vector.tensor_tensor(work[:, :, :], work[:, :, :], onehot[:, :, :], ALU.mult))
            link(nc.vector.tensor_reduce(slot_f[:, :], banked(work), AX.X, ALU.add))
            nc.vector.tensor_copy(r.slot[:, :, :].rearrange("p t b -> p (t b)"), slot_f[:, :]).then_inc(slot_ready, 1)
            for u, (m, c) in enumerate(UNITS):
                c0, c1 = CHUNKS[c]
                dve.wait_ge(ghi_ready, u + 1)
                nc.vector.tensor_tensor(gT_lo[:, m, c0:c1], act1[u % 2][:, 0:c1 - c0], gT_hi[:, m, c0:c1].bitcast(F32),
                                        ALU.subtract).then_inc(glo_ready, 1)
            for t in range(NT):
                dve.wait_ge(down_done, t + 1)
                nc.vector.tensor_tensor(y[t % 2][:, :], ps_down[t % 2][:, :], bs2[:, :], ALU.add).then_inc(y_ready, 1)
                dve.wait_ge(y_ready, t + 1)
                link(nc.vector.tensor_tensor(X[:, t, :], X[:, t, :], y[t % 2][:, :], ALU.add))

        @block.tensor
        def _(pe):
            ln.tensor(pe)
            pe.wait_ge(wlo_ready, 2)
            pe.wait_ge(ln.lo_ready, NT)
            for t in range(NT):
                tok = slice(t * PT, (t + 1) * PT)
                for k in range(KD):
                    last = three(nc, ps_logit[:, t, :], hT_hi[:, k, tok], hT_lo[:, k, tok], wr_hi[:, k, :], wr_lo[:, k, :],
                                 k == 0, k == KD - 1)
            last.then_inc(logits_done, 1)
            for u, (m, c) in enumerate(UNITS):
                c0, c1 = CHUNKS[c]
                if u >= 2:
                    pe.wait_ge(act_ready, u - 1)
                for k in range(KD):
                    ms = slice(m * 128, (m + 1) * 128)
                    last = three(nc, ps_up[u % 2][:, 0:c1 - c0], w1[0][:, k, ms], w1[1][:, k, ms],
                                 hT_hi[:, k, c0:c1], hT_lo[:, k, c0:c1], k == 0, k == KD - 1)
                last.then_inc(up_done, 1)
                if u == 1:
                    pe.wait_ge(onehot_ready, 1)
                    pe.wait_ge(made, 8)
                    for t in range(NT + 1):
                        for q in range(min(t + 1, NT)):
                            lhs = upto if q == t else every
                            last = nc.tensor.matmul(ps_rank[:, t * NX:(t + 1) * NX], lhs[:, :], onehot16[:, q, :],
                                                    start=(q == 0), stop=(q == min(t, NT - 1)))
                    last.then_inc(ranked, 1)
            pe.wait_ge(glo_ready, len(UNITS))
            for t in range(NT):
                tok = slice(t * PT, (t + 1) * PT)
                if t >= 2:
                    pe.wait_ge(y_ready, t - 1)
                for k in range(KF):
                    last = three(nc, ps_down[t % 2][:, :], gT_hi[:, k, tok], gT_lo[:, k, tok], w2[0][:, k, :], w2[1][:, k, :],
                                 k == 0, k == KF - 1)
                last.then_inc(down_done, 1)


def expert_weights(a, x):
    bank, e = BANKS[x // NE], x % NE
    return (a[f"L0_ffn_W1_{bank}"][e].rearrange("(k p) f -> p k f", p=128),
            a[f"L0_ffn_W2_{bank}"][e].rearrange("(k p) f -> p k f", p=128), a[f"L0_ffn_b2_{bank}"][e])


def routed_experts(nc, sems, a, ident, r):
    ST = FIRST_ROWS // 128
    sems.next_phase()
    with ExitStack() as ctx:
        def sb(name, shape, dt=F32):
            return ctx.enter_context(nc.sbuf_tensor(name, shape, dt))

        def pb(name, shape, dt=F32):
            return ctx.enter_context(nc.psum_tensor(name, shape, dt))

        def sem(name):
            return sems.new(ctx, "e_" + name)

        UP, DOWN = 0, 1
        raw = [[sb(f"e_raw{m}{i}", [128, 1024]) for i in range(2)] for m in (UP, DOWN)]
        whi = [[sb(f"e_whi{m}{i}", [128, 1024], F32R) for i in range(2)] for m in (UP, DOWN)]
        wlo = [[sb(f"e_wlo{m}{i}", [128, 1024], F32R) for i in range(2)] for m in (UP, DOWN)]
        b1 = sb("e_b1", [128, NX, KF])
        b2 = [sb(f"e_b2_{i}", [128, D]) for i in range(2)]
        idx_rows = sb("e_idx_rows", [ST * NX, 128], I32)
        idx_f = sb("e_idx_f", [ST * NX, 128])
        idx = sb("e_idx", [128, ST * NX], I32)
        rows = [sb(f"e_rows{i}", [128, ST, D]) for i in range(2)]
        xT_hi = [sb(f"e_xT_hi{i}", [128, KD, FIRST_ROWS], F32R) for i in range(2)]
        xT_lo = [sb(f"e_xT_lo{i}", [128, KD, FIRST_ROWS], F32R) for i in range(2)]
        g = sb("e_g", [128, KF, FIRST_ROWS])
        g_hi = [sb(f"e_g_hi{i}", [128, KF, FIRST_ROWS], F32R) for i in range(2)]
        g_lo = [sb(f"e_g_lo{i}", [128, KF, FIRST_ROWS], F32R) for i in range(2)]
        y = [sb(f"e_y{i}", [128, D]) for i in range(ST)]
        ps_turn = [pb(f"e_turn{s}", [128, KD, 128]) for s in range(ST)]
        ps_up = [pb(f"e_up{i}", [128, KF, FIRST_ROWS]) for i in range(2)]
        ps_down = [pb(f"e_down{s}", [128, D]) for s in range(ST)]
        b1_loaded, idx_loaded = sem("b1_loaded"), sem("idx_loaded")
        idx_float, idx_turned, idx_ready = sem("idx_float"), sem("idx_turned"), sem("idx_ready")
        w_loaded = [[sem(f"w_loaded{m}{i}") for i in range(2)] for m in (UP, DOWN)]
        b2_loaded = [sem(f"b2_loaded{i}") for i in range(2)]
        gathered = [sem(f"gathered{i}") for i in range(2 * ST)]
        whi_ready, wlo_ready = ([sem(f"{n}{m}") for m in (UP, DOWN)] for n in ("whi_ready", "wlo_ready"))
        turned, xhi_ready, xlo_ready = sem("turned"), sem("xhi_ready"), sem("xlo_ready")
        up_done, g_ready, ghi_ready, glo_ready = sem("up_done"), sem("g_ready"), sem("ghi_ready"), sem("glo_ready")
        down_done, y_ready = sem("down_done"), sem("y_ready")
        y_stored = [sem(f"y_stored{s}") for s in range(ST)]
        block = ctx.enter_context(nc.Block())

        def as_lhs(t, m, i):
            return t[m][i][:, :].rearrange("p (k f) -> p k f", k=(KD, KF)[m])


        @block.sync
        def _(sp):
            def load_w(x, m):
                if x >= NX:
                    return
                if x >= 2:
                    sp.wait_ge(whi_ready[m], x - 1)
                    sp.wait_ge(wlo_ready[m], x - 1)
                sp.dma_start(as_lhs(raw, m, x % 2), expert_weights(a, x)[m]).then_inc(w_loaded[m][x % 2], 16)

            def load_b2(x):
                if x >= NX:
                    return
                if x >= 2:
                    sp.wait_ge(y_ready, ST * (x - 1))
                sp.dma_start(b2[x % 2][:, :], expert_weights(a, x)[2].partition_broadcast(128)).then_inc(b2_loaded[x % 2], 16)

            tok = r.token_of[0:MORE_FROM, :].rearrange("(x s p) o -> s x (p o)", x=NX, p=128)
            for s in range(ST):
                sp.dma_start(idx_rows[s * NX:(s + 1) * NX, :], tok[s]).then_inc(idx_loaded, 16)
            load_w(0, UP)
            load_w(1, UP)
            load_w(0, DOWN)
            for b, bank in enumerate(BANKS):
                sp.dma_start(b1[:, b * NE:(b + 1) * NE, :], a[f"L0_ffn_b1_{bank}"]).then_inc(b1_loaded, 16)
            load_w(1, DOWN)
            load_b2(0)
            load_b2(1)
            load_w(2, UP)
            for x in range(NX):
                load_w(x + 3, UP)
                load_w(x + 2, DOWN)
                for s in range(ST):
                    sp.wait_ge(y_ready, x * ST + s + 1)
                    row = x * FIRST_ROWS + s * 128
                    sp.dma_start(r.y_rows[row:row + 128, :], y[s][:, :]).then_inc(y_stored[s], 16)
                load_b2(x + 2)
            for s in range(ST):
                sp.wait_ge(y_stored[s], 16 * NX)

        @block.gpsimd
        def _(pool):
            sems.clear(pool)
            pool.wait_ge(idx_ready, 1)
            for x in range(NX):
                for s in range(ST):
                    if x >= 2:
                        pool.wait_ge(turned, ST * (x - 2) + s + 1)
                    nc.gpsimd.indirect_dma_start(
                        out=rows[x % 2][:, s, :], out_offset=None, in_=r.h_rows,
                        in_offset=bass.IndirectOffsetOnAxis(ap=idx[:, s * NX + x:s * NX + x + 1], axis=0)).then_inc(gathered[(x % 2) * ST + s], 16)

        @block.scalar
        def _(act):
            def split_w(x, m):
                act.wait_ge(w_loaded[m][x % 2], 16 * (x // 2 + 1))
                if x >= 2 and m == UP:
                    act.wait_ge(up_done, x - 1)
                elif x >= 2:
                    act.wait_ge(down_done, ST * (x - 1))
                nc.scalar.activation(whi[m][x % 2][:, :], raw[m][x % 2][:, :], ACT.Copy).then_inc(whi_ready[m], 1)

            def split_x(x):
                if x >= 2:
                    act.wait_ge(up_done, x - 1)
                for s in range(ST):
                    act.wait_ge(turned, ST * x + s + 1)
                    nc.scalar.activation(xT_hi[x % 2][:, :, s * 128:(s + 1) * 128], ps_turn[s][:, :, :], ACT.Copy).then_inc(xhi_ready, 1)

            def activate(x):
                act.wait_ge(up_done, x + 1)
                if x:
                    act.wait_ge(glo_ready, x)
                for m in range(KF):
                    nc.scalar.activation(g[:, m, :], ps_up[x % 2][:, m, :], ACT.Gelu, bias=b1[:, x, m:m + 1]).then_inc(g_ready, 1)
                act.wait_ge(g_ready, KF * (x + 1))
                if x >= 2:
                    act.wait_ge(down_done, ST * (x - 1))
                nc.scalar.activation(g_hi[x % 2][:, :, :], g[:, :, :], ACT.Copy).then_inc(ghi_ready, 1)

            split_w(0, UP)
            act.wait_ge(b1_loaded, 16 * NB)
            for x in range(-2, NX):
                if x + 2 < NX:
                    split_x(x + 2)
                    if x + 2 > 0:
                        split_w(x + 2, UP)
                if 0 <= x + 1 < NX:
                    split_w(x + 1, DOWN)
                    activate(x + 1)

        @block.vector
        def _(dve):
            def split_w(x, m):
                dve.wait_ge(whi_ready[m], x + 1)
                nc.vector.tensor_tensor(wlo[m][x % 2][:, :], raw[m][x % 2][:, :], whi[m][x % 2][:, :].bitcast(F32),
                                        ALU.subtract).then_inc(wlo_ready[m], 1)

            def split_x(x):
                for s in range(ST):
                    dve.wait_ge(xhi_ready, ST * x + s + 1)
                    cols = slice(s * 128, (s + 1) * 128)
                    nc.vector.tensor_tensor(xT_lo[x % 2][:, :, cols], ps_turn[s][:, :, :], xT_hi[x % 2][:, :, cols].bitcast(F32),
                                            ALU.subtract).then_inc(xlo_ready, 1)

            dve.wait_ge(idx_loaded, 16 * ST)
            nc.vector.tensor_copy(idx_f[:, :], idx_rows[:, :]).then_inc(idx_float, 1)
            dve.wait_ge(idx_turned, 1)
            nc.vector.tensor_copy(idx[:, :], ps_down[0][:, 0:ST * NX]).then_inc(idx_ready, 1)
            split_w(0, UP)
            for x in range(-2, NX):
                if x + 2 < NX:
                    split_x(x + 2)
                    if x + 2 > 0:
                        split_w(x + 2, UP)
                if 0 <= x + 1 < NX:
                    split_w(x + 1, DOWN)
                    dve.wait_ge(ghi_ready, x + 2)
                    i = (x + 1) % 2
                    nc.vector.tensor_tensor(g_lo[i][:, :, :], g[:, :, :], g_hi[i][:, :, :].bitcast(F32), ALU.subtract).then_inc(glo_ready, 1)
                if x >= 0:
                    dve.wait_ge(b2_loaded[x % 2], 16 * (x // 2 + 1))
                    for s in range(ST):
                        dve.wait_ge(down_done, ST * x + s + 1)
                        if x:
                            dve.wait_ge(y_stored[s], 16 * x)
                        nc.vector.tensor_tensor(y[s][:, :], ps_down[s][:, :], b2[x % 2][:, :], ALU.add).then_inc(y_ready, 1)

        @block.tensor
        def _(pe):
            def turn(x):
                for s in range(ST):
                    pe.wait_ge(gathered[(x % 2) * ST + s], 16 * (x // 2 + 1))
                    if x:
                        pe.wait_ge(xlo_ready, ST * (x - 1) + s + 1)
                    for k in range(KD):
                        last = nc.tensor.transpose(ps_turn[s][:, k, :], rows[x % 2][:, s, k * 128:(k + 1) * 128], ident[:, :])
                    last.then_inc(turned, 1)

            def up(x):
                u_hi, u_lo, i = as_lhs(whi, UP, x % 2), as_lhs(wlo, UP, x % 2), x % 2
                pe.wait_ge(xlo_ready, ST * (x + 1))
                pe.wait_ge(wlo_ready[UP], x + 1)
                if x >= 2:
                    pe.wait_ge(g_ready, KF * (x - 1))
                for m in range(KF):
                    ms = slice(m * 128, (m + 1) * 128)
                    for k in range(KD):
                        last = three(nc, ps_up[i][:, m, :], u_hi[:, k, ms], u_lo[:, k, ms], xT_hi[i][:, k, :], xT_lo[i][:, k, :],
                                     k == 0, k == KD - 1)
                last.then_inc(up_done, 1)

            def down(x):
                d_hi, d_lo, i = as_lhs(whi, DOWN, x % 2), as_lhs(wlo, DOWN, x % 2), x % 2
                pe.wait_ge(glo_ready, x + 1)
                pe.wait_ge(wlo_ready[DOWN], x + 1)
                for s in range(ST):
                    if x:
                        pe.wait_ge(y_ready, ST * (x - 1) + s + 1)
                    for k in range(KF):
                        cols = slice(s * 128, (s + 1) * 128)
                        last = three(nc, ps_down[s][:, :], g_hi[i][:, k, cols], g_lo[i][:, k, cols], d_hi[:, k, :], d_lo[:, k, :],
                                     k == 0, k == KF - 1)
                    last.then_inc(down_done, 1)

            pe.wait_ge(idx_float, 1)
            nc.tensor.transpose(ps_down[0][:, 0:ST * NX], idx_f[:, :], ident[0:ST * NX, 0:ST * NX]).then_inc(idx_turned, 1)
            pe.wait_ge(idx_ready, 1)
            for x in range(-2, NX):
                if x + 2 < NX:
                    turn(x + 2)
                if 0 <= x + 1 < NX:
                    up(x + 1)
                if x >= 0:
                    down(x)


def overfull_experts(nc, sems, a, ident, r):
    sems.next_phase()
    with ExitStack() as ctx:
        def sb(name, shape, dt=F32):
            return ctx.enter_context(nc.sbuf_tensor(name, shape, dt))

        def pb(name, shape, dt=F32):
            return ctx.enter_context(nc.psum_tensor(name, shape, dt))

        def sem(name):
            return sems.new(ctx, "o_" + name)

        raw = sb("o_raw", [128, 2048])
        whi = sb("o_whi", [128, 2048], F32R)
        wlo = sb("o_wlo", [128, 2048], F32R)
        b1 = sb("o_b1", [128, KF])
        b2 = sb("o_b2", [128, D])
        idx = sb("o_idx", [128, 1], I32)
        rows = sb("o_rows", [128, D])
        xT_hi = sb("o_xT_hi", [128, KD, MORE_ROWS], F32R)
        xT_lo = sb("o_xT_lo", [128, KD, MORE_ROWS], F32R)
        g = sb("o_g", [128, KF, MORE_ROWS])
        g_hi = sb("o_g_hi", [128, KF, MORE_ROWS], F32R)
        g_lo = sb("o_g_lo", [128, KF, MORE_ROWS], F32R)
        y = sb("o_y", [128, D])
        ps_turn = pb("o_turn", [128, KD, 128])
        ps_up = pb("o_up", [128, KF, 256])
        ps_down = pb("o_down", [128, D])
        w_loaded, whi_ready, w_ready = sem("w_loaded"), sem("whi_ready"), sem("w_ready")
        begun = sem("begun")
        expert_over = sem("expert_over")
        idx_loaded, gathered, turned = sem("idx_loaded"), sem("gathered"), sem("turned")
        xhi_ready, x_ready, up_done, g_made = sem("xhi_ready"), sem("x_ready"), sem("up_done"), sem("g_made")
        ghi_ready, g_ready, down_done, y_ready, y_stored, round_over = (
            sem("ghi_ready"), sem("g_ready"), sem("down_done"), sem("y_ready"), sem("y_stored"), sem("round_over"))
        block = ctx.enter_context(nc.Block())
        up_hi, down_hi = (whi[:, 0:1024].rearrange("p (k f) -> p k f", k=KD), whi[:, 1024:2048].rearrange("p (k f) -> p k f", k=KF))
        up_lo, down_lo = (wlo[:, 0:1024].rearrange("p (k f) -> p k f", k=KD), wlo[:, 1024:2048].rearrange("p (k f) -> p k f", k=KF))

        def overfull(eng, tag, at_expert, at_round):
            experts = eng.alloc_register(f"{tag}_experts")
            rounds = eng.alloc_register(f"{tag}_rounds")
            eng.reg_mov(experts, 1)
            eng.reg_mov(rounds, 1)
            for b in range(NB):
                with eng.Fori(0, NE) as e:
                    count = eng.value_load(r.rounds[0:1, bass.DynSlice(e + b * NE, 1)], min_val=0, max_val=ROUNDS)
                    with eng.If(count > 0):
                        nth = eng.snap(experts, min_val=1, max_val=NX)
                        at_expert(nth, b, e)
                        with eng.Fori(0, count) as k:
                            at_round(eng.snap(rounds, min_val=1, max_val=NB * ROUNDS), b, e, k)
                            eng.reg_add(rounds, rounds, 1)
                        eng.reg_add(experts, experts, 1)

        @block.sync
        def _(sp):
            sp.sem_inc(round_over, 1)
            sp.sem_inc(expert_over, 1)

            def at_expert(nth, b, e):
                sp.wait_ge(expert_over, nth)
                bank, one = BANKS[b], bass.DynSlice(e, 1)
                sp.dma_start(raw[:, 0:1024].rearrange("p (k f) -> p k f", k=KD),
                             a[f"L0_ffn_W1_{bank}"][one].rearrange("o (k p) f -> p (o k) f", p=128)).then_inc(w_loaded, 16)
                sp.dma_start(raw[:, 1024:2048].rearrange("p (k f) -> p k f", k=KF),
                             a[f"L0_ffn_W2_{bank}"][one].rearrange("o (k p) f -> p (o k) f", p=128)).then_inc(w_loaded, 16)
                sp.dma_start(b1[:, :], a[f"L0_ffn_b1_{bank}"][:, one, :].rearrange("p o m -> p (o m)")).then_inc(w_loaded, 16)
                sp.dma_start(b2[:, :], a[f"L0_ffn_b2_{bank}"][one].rearrange("o d -> (o d)").partition_broadcast(128)).then_inc(w_loaded, 16)

            def at_round(nth, b, e, k):
                row = nth * MORE_ROWS + (MORE_FROM - MORE_ROWS)
                sp.wait_ge(round_over, nth)
                sp.dma_start(idx[:, :], r.token_of[bass.DynSlice(row, MORE_ROWS), :]).then_inc(idx_loaded, 16)
                sp.wait_ge(y_ready, nth)
                sp.dma_start(r.y_rows[bass.DynSlice(row, MORE_ROWS), :], y[:, :]).then_inc(y_stored, 16)
                sp.wait_ge(y_stored, nth * 16)
                sp.sem_inc(round_over, 1)

            overfull(sp, "sp", at_expert, at_round)

        @block.gpsimd
        def _(pool):
            sems.clear(pool)
            def at_round(nth, b, e, k):
                pool.wait_ge(idx_loaded, nth * 16)
                pool.sem_inc(begun, 1)
                nc.gpsimd.indirect_dma_start(out=rows[:, :], out_offset=None, in_=r.h_rows,
                                             in_offset=bass.IndirectOffsetOnAxis(ap=idx[:, 0:1], axis=0)).then_inc(gathered, 16)

            overfull(pool, "pool", lambda *_: None, at_round)

        @block.scalar
        def _(act):
            def at_expert(nth, b, e):
                act.wait_ge(w_loaded, nth * 64)
                nc.scalar.activation(whi[:, :], raw[:, :], ACT.Copy).then_inc(whi_ready, 1)

            def at_round(nth, b, e, k):
                act.wait_ge(turned, nth)
                nc.scalar.activation(xT_hi[:, :, :], ps_turn[:, :, :], ACT.Copy).then_inc(xhi_ready, 1)
                act.wait_ge(up_done, nth)
                for m in range(KF):
                    last = nc.scalar.activation(g[:, m, :], ps_up[:, m, 0:MORE_ROWS], ACT.Gelu, bias=b1[:, m:m + 1])
                last.then_inc(g_made, 1)
                act.wait_ge(g_made, nth)
                nc.scalar.activation(g_hi[:, :, :], g[:, :, :], ACT.Copy).then_inc(ghi_ready, 1)

            overfull(act, "act", at_expert, at_round)

        @block.vector
        def _(dve):
            def at_expert(nth, b, e):
                dve.wait_ge(whi_ready, nth)
                nc.vector.tensor_tensor(wlo[:, :], raw[:, :], whi[:, :].bitcast(F32), ALU.subtract).then_inc(w_ready, 1)

            def at_round(nth, b, e, k):
                dve.wait_ge(xhi_ready, nth)
                nc.vector.tensor_tensor(xT_lo[:, :, :], ps_turn[:, :, :], xT_hi[:, :, :].bitcast(F32), ALU.subtract).then_inc(x_ready, 1)
                dve.wait_ge(ghi_ready, nth)
                nc.vector.tensor_tensor(g_lo[:, :, :], g[:, :, :], g_hi[:, :, :].bitcast(F32), ALU.subtract).then_inc(g_ready, 1)
                dve.wait_ge(down_done, nth)
                nc.vector.tensor_tensor(y[:, :], ps_down[:, :], b2[:, :], ALU.add).then_inc(y_ready, 1)

            overfull(dve, "dve", at_expert, at_round)

        @block.tensor
        def _(pe):
            experts = pe.alloc_register("pe_experts")
            rounds = pe.alloc_register("pe_rounds")
            pe.reg_mov(experts, 1)
            pe.reg_mov(rounds, 1)
            for b in range(NB):
                with pe.Fori(0, NE) as e:
                    count = pe.value_load(r.rounds[0:1, bass.DynSlice(e + b * NE, 1)], min_val=0, max_val=ROUNDS)
                    with pe.If(count > 0):
                        pe.wait_ge(w_ready, pe.snap(experts, min_val=1, max_val=NX))
                        pe.sem_inc(begun, 1)
                        with pe.Fori(0, count):
                            nth = pe.snap(rounds, min_val=1, max_val=NB * ROUNDS)
                            pe.wait_ge(gathered, nth * 16)
                            for k in range(KD):
                                last = nc.tensor.transpose(ps_turn[:, k, :], rows[:, k * 128:(k + 1) * 128], ident[:, :])
                            last.then_inc(turned, 1)
                            pe.wait_ge(x_ready, nth)
                            for m in range(KF):
                                for k in range(KD):
                                    ms = slice(m * 128, (m + 1) * 128)
                                    last = three(nc, ps_up[:, m, 0:MORE_ROWS], up_hi[:, k, ms], up_lo[:, k, ms],
                                                 xT_hi[:, k, :], xT_lo[:, k, :], k == 0, k == KD - 1)
                            last.then_inc(up_done, 1)
                            pe.wait_ge(g_ready, nth)
                            for k in range(KF):
                                last = three(nc, ps_down[:, :], g_hi[:, k, :], g_lo[:, k, :], down_hi[:, k, :], down_lo[:, k, :],
                                             k == 0, k == KF - 1)
                            last.then_inc(down_done, 1)
                            pe.reg_add(rounds, rounds, 1)
                        pe.wait_ge(y_ready, pe.snap(rounds, min_val=1, max_val=NB * ROUNDS) - 1)
                        pe.sem_inc(expert_over, 1)
                        pe.reg_add(experts, experts, 1)


def combine(nc, sems, X, CT, ident, r):
    NR = 6
    swaps = [(i, j, min(j + 4, NT)) for i in range(NT) for j in range(i + 1, NT, 4)]
    diagonal = [(j, min(j + 4, NT)) for j in range(0, NT, 4)]
    sems.next_phase()
    with ExitStack() as ctx:
        rows = [ctx.enter_context(nc.sbuf_tensor(f"c_rows{i}", [PT, D], F32)) for i in range(NR)]
        gathered = [sems.new(ctx, f"c_gathered{i}") for i in range(NR)]
        added = sems.new(ctx, "c_added")
        turned = sems.new(ctx, "c_turned")
        swapped = sems.new(ctx, "c_swapped")
        ps = [[ctx.enter_context(nc.psum_tensor(f"c_ps{n}{half}", [PT, 4, 128], F32)) for half in range(2)] for n in range(2)]
        block = ctx.enter_context(nc.Block())
        pairs = [(t, b) for t in range(NT) for b in range(NB)]

        @block.gpsimd
        def _(pool):
            sems.clear(pool)
            for n, (t, b) in enumerate(pairs):
                if n >= NR:
                    pool.wait_ge(added, n - NR + 1)
                nc.gpsimd.indirect_dma_start(out=rows[n % NR][:, :], out_offset=None, in_=r.y_rows,
                                             in_offset=bass.IndirectOffsetOnAxis(ap=r.slot[:, t, b:b + 1], axis=0)).then_inc(gathered[n % NR], 16)

        @block.vector
        def _(dve):
            for n, (t, b) in enumerate(pairs):
                dve.wait_ge(gathered[n % NR], 16 * (n // NR + 1))
                if b:
                    dve.wait_ge(added, n)
                nc.vector.scalar_tensor_tensor(X[:, t, :], rows[n % NR][:, :], r.gate[:, t, b:b + 1], X[:, t, :],
                                               ALU.mult, ALU.add).then_inc(added, 1)

        def block_of(i, j):
            return CT[:, i, j * PT:(j + 1) * PT]

        @block.tensor
        def _(pe):
            for n, (i, j0, j1) in enumerate(swaps):
                if n >= 2:
                    pe.wait_ge(swapped, n - 1)
                for j in range(j0, j1):
                    nc.tensor.transpose(ps[n % 2][0][:, j - j0, 0:PT], block_of(i, j), ident[0:PT, 0:PT])
                for j in range(j0, j1):
                    last = nc.tensor.transpose(ps[n % 2][1][:, j - j0, 0:PT], block_of(j, i), ident[0:PT, 0:PT])
                last.then_inc(turned, 1)
            for m, (j0, j1) in enumerate(diagonal):
                n = len(swaps) + m
                pe.wait_ge(swapped, n - 1)
                for j in range(j0, j1):
                    last = nc.tensor.transpose(ps[n % 2][0][:, j - j0, 0:PT], block_of(j, j), ident[0:PT, 0:PT])
                last.then_inc(turned, 1)

        @block.scalar
        def _(act):
            for n, (i, j0, j1) in enumerate(swaps):
                act.wait_ge(turned, n + 1)
                nc.scalar.activation(CT[:, j0:j1, i * PT:(i + 1) * PT], ps[n % 2][0][:, 0:j1 - j0, 0:PT], ACT.Copy)
                nc.scalar.activation(CT[:, i, j0 * PT:j1 * PT].rearrange("p (j q) -> p j q", q=PT), ps[n % 2][1][:, 0:j1 - j0, 0:PT],
                                     ACT.Copy).then_inc(swapped, 1)
            for m, (j0, j1) in enumerate(diagonal):
                n = len(swaps) + m
                act.wait_ge(turned, n + 1)
                for j in range(j0, j1):
                    last = nc.scalar.activation(block_of(j, j), ps[n % 2][0][:, j - j0, 0:PT], ACT.Copy)
                last.then_inc(swapped, 1)


HEADS = 8
DH = FF // HEADS
TINY = 1.1754944e-38
HUGE = 3.4028235e38


def project_qkv(nc, sems, a, X, H, hT_hi, hT_lo, ident, eps_col, V, r):
    sems.next_phase()
    with ExitStack() as ctx:
        def sb(name, shape, dt=F32):
            return ctx.enter_context(nc.sbuf_tensor(name, shape, dt))

        def pb(name, shape, dt=F32):
            return ctx.enter_context(nc.psum_tensor(name, shape, dt))

        def sem(name):
            return sems.new(ctx, "q_" + name)

        raw = [sb(f"q_raw{i}", [128, KD, FF]) for i in range(2)]
        whi = [sb(f"q_whi{i}", [128, KD, FF], F32R) for i in range(3)]
        wlo = [sb(f"q_wlo{i}", [128, KD, FF], F32R) for i in range(3)]
        bqk = sb("bqk", [128, 2, KF])
        bv = sb("bv", [PT, FF])
        full = sb("q_full", [128, N])
        hi = sb("q_hi", [128, N], F32R)
        lo = sb("q_lo", [128, N], F32R)
        ps_qk = [pb(f"ps_qk{i}", [128, 3, 512]) for i in range(2)]
        ps_turn = [pb(f"q_turn{i}", [128, 4, 128]) for i in range(2)]
        w_loaded, b_loaded = sem("w_loaded"), sem("b_loaded")
        whi_ready, wlo_ready, ones_made = sem("whi_ready"), sem("wlo_ready"), sem("ones_made")
        v_done, v_ready, qk_done, full_ready = sem("v_done"), sem("v_ready"), sem("qk_done"), sem("full_ready")
        hi_ready, lo_ready, stored, step = sem("hi_ready"), sem("lo_ready"), sem("stored"), sem("step")
        ln = Norm(nc, sems, ctx, "ln3", X, H, hT_hi, hT_lo, ps_turn, ident, eps_col)
        block = ctx.enter_context(nc.Block())

        @block.sync
        def _(sp):
            for i, name in enumerate("vqk"):
                if i >= 2:
                    sp.wait_ge(wlo_ready, i - 1)
                sp.dma_start(raw[i % 2][:, :, :], a[f"L1_gnn_W{name}"].rearrange("(k p) f -> p k f", p=128)).then_inc(w_loaded, 16)
                if i < 2:
                    sp.dma_start(bqk[:, i, :], a[f"L1_gnn_b{'qk'[i]}"]).then_inc(b_loaded, 16)
                sp.wait_ge(w_loaded, 16 * (i + 1))
            sp.dma_start(bv[:, :], a["L1_gnn_bv"].partition_broadcast(PT)).then_inc(b_loaded, 16)
            for u in range(2 * KF):
                q, m = u // KF, u % KF
                sp.wait_ge(hi_ready, u + 1)
                sp.dma_start(r.qk[2 * q, m * 128:(m + 1) * 128, :], hi[:, :].bitcast(F32)).then_inc(stored, 16)
                sp.wait_ge(lo_ready, u + 1)
                sp.dma_start(r.qk[2 * q + 1, m * 128:(m + 1) * 128, :], lo[:, :].bitcast(F32)).then_inc(stored, 16)
            sp.wait_ge(stored, 16 * 4 * KF)

        @block.gpsimd
        def _(pool):
            sems.clear(pool)
            nc.gpsimd.memset(V[:, :, :, DH:64], 1.0).then_inc(ones_made, 1)
            pool.wait_ge(ones_made, 1)

        @block.scalar
        def _(act):
            ln.scalar(act)
            for i in range(3):
                act.wait_ge(w_loaded, 16 * (i + 1))
                nc.scalar.activation(whi[i][:, :, :], raw[i % 2][:, :, :], ACT.Copy).then_inc(whi_ready, 1)
            act.wait_ge(b_loaded, 48)
            for u in range(2 * KF):
                act.wait_ge(qk_done, u + 1)
                if u:
                    act.wait_ge(lo_ready, u)
                for c, (c0, c1) in enumerate(CHUNKS):
                    last = nc.scalar.activation(full[:, c0:c1], ps_qk[u % 2][:, c, 0:c1 - c0], ACT.Identity,
                                                bias=bqk[:, u // KF, u % KF:u % KF + 1])
                last.then_inc(full_ready, 1)

        @block.vector
        def _(dve):
            link = chained(dve, step)
            ln.vector(dve, link)
            for i in range(3):
                dve.wait_ge(whi_ready, i + 1)
                nc.vector.tensor_tensor(wlo[i][:, :, :], raw[i % 2][:, :, :], whi[i][:, :, :].bitcast(F32), ALU.subtract).then_inc(wlo_ready, 1)
            for t in range(NT):
                last = nc.vector.tensor_tensor(X[:, t, :], X[:, t, :], H[:, t, :], ALU.add)
            link(last)
            dve.wait_ge(b_loaded, 48)
            for t in range(NT):
                dve.wait_ge(v_done, t + 1)
                nc.vector.tensor_tensor(V[:, t, :, 0:DH], ps_turn[t % 2][0:PT, 0:2, :].rearrange("p a (h d) -> p (a h) d", d=DH),
                                        bv[:, :].rearrange("p (h d) -> p h d", d=DH), ALU.add).then_inc(v_ready, 1)
            for u in range(2 * KF):
                dve.wait_ge(full_ready, u + 1)
                if u:
                    dve.wait_ge(stored, 32 * u)
                nc.vector.tensor_copy(hi[:, :], full[:, :]).then_inc(hi_ready, 1)
                dve.wait_ge(hi_ready, u + 1)
                nc.vector.tensor_tensor(lo[:, :], full[:, :], hi[:, :].bitcast(F32), ALU.subtract).then_inc(lo_ready, 1)

        @block.tensor
        def _(pe):
            ln.tensor(pe)
            pe.wait_ge(ln.lo_ready, NT)
            pe.wait_ge(wlo_ready, 1)
            for t in range(NT):
                tok = slice(t * PT, (t + 1) * PT)
                if t >= 2:
                    pe.wait_ge(v_ready, t - 1)
                out = ps_turn[t % 2][0:PT, 0:2, :].rearrange("p a f -> p (a f)")
                for k in range(KD):
                    last = three(nc, out, hT_hi[:, k, tok], hT_lo[:, k, tok], whi[0][:, k, :], wlo[0][:, k, :], k == 0, k == KD - 1)
                last.then_inc(v_done, 1)
            for u in range(2 * KF):
                q, m = u // KF, u % KF
                pe.wait_ge(wlo_ready, q + 2)
                if u >= 2:
                    pe.wait_ge(full_ready, u - 1)
                for c, (c0, c1) in enumerate(CHUNKS):
                    for k in range(KD):
                        ms = slice(m * 128, (m + 1) * 128)
                        last = three(nc, ps_qk[u % 2][:, c, 0:c1 - c0], whi[q + 1][:, k, ms], wlo[q + 1][:, k, ms],
                                     hT_hi[:, k, c0:c1], hT_lo[:, k, c0:c1], k == 0, k == KD - 1)
                last.then_inc(qk_done, 1)


def attention(nc, sems, oT_hi, oT_lo, CT, V, r):
    WIDTH = 418
    STARTS = (0, 418, N - 418)
    SKIP = (0, 0, 3 * 418 - N)
    units = [(h, s, c) for h in range(HEADS) for s in range(NT) for c in range(3)]
    NS, NP, LAG = 5, 4, 4
    HG = 128 // DH
    sems.next_phase()
    with ExitStack() as ctx:
        def sb(name, shape, dt=F32):
            return ctx.enter_context(nc.sbuf_tensor(name, shape, dt))

        def pb(name, shape, dt=F32):
            return ctx.enter_context(nc.psum_tensor(name, shape, dt))

        def sem(name):
            return sems.new(ctx, "a_" + name)

        q = [sb(f"a_q{i}", [3 * DH, N], F32R) for i in range(2)]
        k = [sb(f"a_k{i}", [3 * DH, N], F32R) for i in range(2)]
        e = [sb(f"a_e{i}", [PT, WIDTH]) for i in range(NP)]
        p = [sb(f"a_p{i}", [PT, WIDTH]) for i in range(NP)]
        num = sb("a_num", [128, N])
        den = sb("a_den", [128, N])
        ps_s = [pb(f"a_s{i}", [PT, 512]) for i in range(NS)]
        ps_o = [pb(f"a_o{i}", [64, 512]) for i in range(3)]
        loaded = [sem(f"loaded{i}") for i in range(2)]
        scored, exped, weighed = sem("scored"), sem("exped"), sem("weighed")
        summed_units = sem("summed_units")
        num_taken, den_taken, ratio_ready = sem("num_taken"), sem("den_taken"), sem("ratio_ready")
        step = sem("step")
        block = ctx.enter_context(nc.Block())

        @block.sync
        def _(sp):
            for h in range(HEADS):
                if h >= 2:
                    sp.wait_ge(scored, 3 * NT * (h - 1))
                rows = slice(h * DH, (h + 1) * DH)
                for j, (kq, kk) in enumerate(((0, 2), (1, 2), (0, 3))):
                    sp.dma_start(q[h % 2][j * DH:(j + 1) * DH, :].bitcast(F32), r.qk[kq, rows, :]).then_inc(loaded[h % 2], 16)
                    sp.dma_start(k[h % 2][j * DH:(j + 1) * DH, :].bitcast(F32), r.qk[kk, rows, :]).then_inc(loaded[h % 2], 16)

        @block.gpsimd
        def _(pool):
            sems.clear(pool)

        @block.scalar
        def _(act):
            def take_num(h, c):
                act.wait_ge(summed_units, (NT * (h + 1) - 1) * 3 + c + 1)
                if h == HG:
                    act.wait_ge(ratio_ready, 1)
                part = slice((h % HG) * DH, (h % HG + 1) * DH)
                nc.scalar.activation(num[part, STARTS[c] + SKIP[c]:STARTS[c] + WIDTH], ps_o[c][0:DH, SKIP[c]:WIDTH], ACT.Relu).then_inc(num_taken, 1)

            for u, (h, s, c) in enumerate(units):
                act.wait_ge(scored, u + 1)
                if u >= NP:
                    act.wait_ge(weighed, u - NP + 1)
                nc.scalar.activation(e[u % NP][:, :], ps_s[u % NS][:, 0:WIDTH], ACT.Exp, scale=DH ** -0.5).then_inc(exped, 1)
                if h and s == 0:
                    take_num(h - 1, c)
            for c in range(3):
                take_num(HEADS - 1, c)

        @block.vector
        def _(dve):
            link = chained(dve, step)

            def take_den(h, c):
                dve.wait_ge(summed_units, (NT * (h + 1) - 1) * 3 + c + 1)
                part = slice((h % HG) * DH, (h % HG + 1) * DH)
                nc.vector.tensor_scalar(den[part, STARTS[c] + SKIP[c]:STARTS[c] + WIDTH], ps_o[c][DH:2 * DH, SKIP[c]:WIDTH], TINY, None,
                                        ALU.max).then_inc(den_taken, 1)

            def divide(g):
                dve.wait_ge(den_taken, 3 * HG * (g + 1))
                dve.wait_ge(num_taken, 3 * HG * (g + 1))
                link(nc.vector.reciprocal(den[:, :], den[:, :]))
                link(nc.vector.tensor_tensor(num[:, :], num[:, :], den[:, :], ALU.mult))
                link(nc.vector.tensor_copy(oT_hi[:, g, :], num[:, :]))
                nc.vector.tensor_tensor(oT_lo[:, g, :], num[:, :], oT_hi[:, g, :].bitcast(F32), ALU.subtract).then_inc(ratio_ready, 1)
                dve.wait_ge(ratio_ready, g + 1)

            for u, (h, s, c) in enumerate(units):
                dve.wait_ge(exped, u + 1)
                if u >= NP:
                    dve.wait_ge(summed_units, u - NP + 1)
                nc.vector.scalar_tensor_tensor(p[u % NP][:, :], e[u % NP][:, :], HUGE, CT[:, s, STARTS[c]:STARTS[c] + WIDTH],
                                               ALU.min, ALU.mult).then_inc(weighed, 1)
                if h and s == 0:
                    take_den(h - 1, c)
                if h == HG and s == 1 and c == 0:
                    divide(0)
            for c in range(3):
                take_den(HEADS - 1, c)
            divide(1)

        @block.tensor
        def _(pe):
            for v in range(len(units) + LAG):
                if v < len(units):
                    h, s, c = units[v]
                    if s == 0 and c == 0:
                        pe.wait_ge(loaded[h % 2], 96 * (h // 2 + 1))
                    if v >= NS:
                        pe.wait_ge(exped, v - NS + 1)
                    nc.tensor.matmul(ps_s[v % NS][:, 0:WIDTH], k[h % 2][:, s * PT:(s + 1) * PT],
                                     q[h % 2][:, STARTS[c]:STARTS[c] + WIDTH], start=True, stop=True).then_inc(scored, 1)
                if v >= LAG:
                    u = v - LAG
                    h, s, c = units[u]
                    pe.wait_ge(weighed, u + 1)
                    if h and s == 0:
                        pe.wait_ge(num_taken, 3 * (h - 1) + c + 1)
                        pe.wait_ge(den_taken, 3 * (h - 1) + c + 1)
                    nc.tensor.matmul(ps_o[c][:, 0:WIDTH], V[:, s, h, :], p[u % NP][:, :], start=(s == 0),
                                     stop=(s == NT - 1)).then_inc(summed_units, 1)


def attention_out(nc, sems, a, X, oT_hi, oT_lo):
    UNITS = [(m, c) for m in range(KD) for c in range(len(CHUNKS))]
    sems.next_phase()
    with ExitStack() as ctx:
        def sb(name, shape, dt=F32):
            return ctx.enter_context(nc.sbuf_tensor(name, shape, dt))

        def pb(name, shape, dt=F32):
            return ctx.enter_context(nc.psum_tensor(name, shape, dt))

        def sem(name):
            return sems.new(ctx, "w_" + name)

        shapes = ([128, KF, D], [128, KD, D])
        raw = [sb(f"o2_raw{i}", shapes[i]) for i in range(2)]
        whi = [sb(f"o2_whi{i}", shapes[i], F32R) for i in range(2)]
        wlo = [sb(f"o2_wlo{i}", shapes[i], F32R) for i in range(2)]
        ba = sb("ba", [128, KD])
        bf = sb("bf", [PT, D])
        full = [sb(f"w_full{i}", [128, 512]) for i in range(2)]
        f_hi = sb("w_f_hi", [128, KD, N], F32R)
        f_lo = sb("w_f_lo", [128, KD, N], F32R)
        y = [sb(f"w_y{i}", [PT, D]) for i in range(2)]
        ps_f = [pb(f"w_f{i}", [128, 512]) for i in range(2)]
        ps_y = [pb(f"w_psy{i}", [PT, D]) for i in range(2)]
        w_loaded, b_loaded = [sem(f"w_loaded{i}") for i in range(2)], sem("b_loaded")
        whi_ready, wlo_ready = sem("whi_ready"), sem("wlo_ready")
        f_done, full_ready, fhi_ready, flo_ready = sem("f_done"), sem("full_ready"), sem("fhi_ready"), sem("flo_ready")
        y_done, y_ready, step = sem("y_done"), sem("y_ready"), sem("step")
        block = ctx.enter_context(nc.Block())

        @block.sync
        def _(sp):
            for i, name in enumerate("af"):
                sp.dma_start(raw[i][:, :, :], a[f"L1_gnn_W{name}"].rearrange("(k p) f -> p k f", p=128)).then_inc(w_loaded[i], 16)
            sp.dma_start(ba[:, :], a["L1_gnn_ba"]).then_inc(b_loaded, 16)
            sp.dma_start(bf[:, :], a["L1_gnn_bf"].partition_broadcast(PT)).then_inc(b_loaded, 16)

        @block.gpsimd
        def _(pool):
            sems.clear(pool)

        @block.scalar
        def _(act):
            for i in range(2):
                act.wait_ge(w_loaded[i], 16)
                nc.scalar.activation(whi[i][:, :, :], raw[i][:, :, :], ACT.Copy).then_inc(whi_ready, 1)
            act.wait_ge(b_loaded, 32)
            for u, (m, c) in enumerate(UNITS):
                w = CHUNKS[c][1] - CHUNKS[c][0]
                act.wait_ge(f_done, u + 1)
                if u >= 2:
                    act.wait_ge(flo_ready, u - 1)
                nc.scalar.activation(full[u % 2][:, 0:w], ps_f[u % 2][:, 0:w], ACT.Relu, bias=ba[:, m:m + 1]).then_inc(full_ready, 1)
                act.wait_ge(full_ready, u + 1)
                nc.scalar.activation(f_hi[:, m, CHUNKS[c][0]:CHUNKS[c][1]], full[u % 2][:, 0:w], ACT.Copy).then_inc(fhi_ready, 1)

        @block.vector
        def _(dve):
            link = chained(dve, step)
            for i in range(2):
                dve.wait_ge(whi_ready, i + 1)
                nc.vector.tensor_tensor(wlo[i][:, :, :], raw[i][:, :, :], whi[i][:, :, :].bitcast(F32), ALU.subtract).then_inc(wlo_ready, 1)
            for u, (m, c) in enumerate(UNITS):
                c0, c1 = CHUNKS[c]
                dve.wait_ge(fhi_ready, u + 1)
                nc.vector.tensor_tensor(f_lo[:, m, c0:c1], full[u % 2][:, 0:c1 - c0], f_hi[:, m, c0:c1].bitcast(F32),
                                        ALU.subtract).then_inc(flo_ready, 1)
            for t in range(NT):
                dve.wait_ge(y_done, t + 1)
                nc.vector.tensor_tensor(y[t % 2][:, :], ps_y[t % 2][:, :], bf[:, :], ALU.add).then_inc(y_ready, 1)
                dve.wait_ge(y_ready, t + 1)
                link(nc.vector.scalar_tensor_tensor(X[:, t, :], y[t % 2][:, :], 0.0, X[:, t, :], ALU.max, ALU.add))

        @block.tensor
        def _(pe):
            pe.wait_ge(wlo_ready, 1)
            for u, (m, c) in enumerate(UNITS):
                c0, c1 = CHUNKS[c]
                if u >= 2:
                    pe.wait_ge(full_ready, u - 1)
                for k in range(KF):
                    ms = slice(m * 128, (m + 1) * 128)
                    last = three(nc, ps_f[u % 2][:, 0:c1 - c0], whi[0][:, k, ms], wlo[0][:, k, ms], oT_hi[:, k, c0:c1], oT_lo[:, k, c0:c1],
                                 k == 0, k == KF - 1)
                last.then_inc(f_done, 1)
            pe.wait_ge(wlo_ready, 2)
            pe.wait_ge(flo_ready, len(UNITS))
            for t in range(NT):
                tok = slice(t * PT, (t + 1) * PT)
                if t >= 2:
                    pe.wait_ge(y_ready, t - 1)
                for k in range(KD):
                    last = three(nc, ps_y[t % 2][:, :], f_hi[:, k, tok], f_lo[:, k, tok], whi[1][:, k, :], wlo[1][:, k, :],
                                 k == 0, k == KD - 1)
                last.then_inc(y_done, 1)


MAX_THRESHOLD = 0.25


def gated_experts(nc, sems, a, X, H, hT_hi, hT_lo, ident, eps_col, out):
    NG = NE + 2
    NY = 4
    sems.next_phase()
    with ExitStack() as ctx:
        def sb(name, shape, dt=F32):
            return ctx.enter_context(nc.sbuf_tensor(name, shape, dt))

        def pb(name, shape, dt=F32):
            return ctx.enter_context(nc.psum_tensor(name, shape, dt))

        def sem(name):
            return sems.new(ctx, "f_" + name)

        wg_raw = sb("wg_raw", [128, KD, NG])
        wg_hi = sb("wg_hi", [128, KD, NG], F32R)
        wg_lo = sb("wg_lo", [128, KD, NG], F32R)
        wt_raw = sb("wt_raw", [128, KD])
        bg = sb("bg", [PT, NG])
        be = sb("be", [NE, D])
        raw = [sb(f"f_raw{i}", [128, KD, D]) for i in range(2)]
        whi = [sb(f"f_whi{i}", [128, KD, D], F32R) for i in range(2)]
        wlo = [sb(f"f_wlo{i}", [128, KD, D], F32R) for i in range(2)]
        logit = sb("f_logit", [PT, NT, NG])
        prob = sb("f_prob", [PT, NT, NE])
        peak = sb("f_peak", [PT, NT])
        total = sb("f_total", [PT, NT])
        thr = sb("f_thr", [PT, NT])
        weight = sb("f_weight", [PT, NT, NE])
        weight_T = sb("f_weight_T", [NE, NT, PT])
        ps_turn = [pb(f"f_turn{i}", [128, 4, 128]) for i in range(2)]
        ps_logit = pb("f_ps_logit", [PT, NT, NG])
        ps_y = [pb(f"f_y{i}", [PT, D]) for i in range(NY)]
        g_loaded, thr_loaded = sem("g_loaded"), sem("thr_loaded")
        w_loaded = [sem(f"w_loaded{i}") for i in range(2)]
        pad_made, ghi_ready, glo_ready = sem("pad_made"), sem("ghi_ready"), sem("glo_ready")
        whi_ready, wlo_ready = sem("whi_ready"), sem("wlo_ready")
        logits_done, shifted, exped = sem("logits_done"), sem("shifted"), sem("exped")
        weights_ready, wt_turned, wt_ready = sem("weights_ready"), sem("wt_turned"), sem("wt_ready")
        y_done, y_added, stored, step = sem("y_done"), sem("y_added"), sem("stored"), sem("step")
        ln = Norm(nc, sems, ctx, "ln4", X, H, hT_hi, hT_lo, ps_turn, ident, eps_col)
        block = ctx.enter_context(nc.Block())

        @block.sync
        def _(sp):
            sp.dma_start(wg_raw[:, :, 0:NE], a["L1_ffn_W_gate"].rearrange("(k p) e -> p k e", p=128)).then_inc(g_loaded, 16)
            sp.dma_start(wt_raw[:, :], a["L1_ffn_W_thr"]).then_inc(thr_loaded, 16)
            sp.dma_start(bg[:, 0:NE], a["L1_ffn_b_gate"].partition_broadcast(PT)).then_inc(g_loaded, 16)
            sp.dma_start(bg[:, NE:NE + 1], a["L1_ffn_b_thr"].partition_broadcast(PT)).then_inc(g_loaded, 16)
            sp.dma_start(be[:, :], a["L1_ffn_b_exp"]).then_inc(g_loaded, 16)
            for x in range(NE):
                if x >= 2:
                    sp.wait_ge(wlo_ready, x - 1)
                sp.dma_start(raw[x % 2][:, :, :], a["L1_ffn_W_exp"][x].rearrange("(k p) f -> p k f", p=128)).then_inc(w_loaded[x % 2], 16)
            for t in range(NT):
                sp.wait_ge(y_added, NT * NE + t + 1)
                sp.dma_start(out[t * PT:(t + 1) * PT, :], X[:, t, :]).then_inc(stored, 16)
            sp.wait_ge(stored, 16 * NT)

        @block.gpsimd
        def _(pool):
            sems.clear(pool)
            nc.gpsimd.memset(wg_raw[:, :, NE + 1:NG], 0.0).then_inc(pad_made, 1)
            nc.gpsimd.memset(bg[:, NE + 1:NG], 0.0).then_inc(pad_made, 1)
            pool.wait_ge(thr_loaded, 16)
            nc.gpsimd.tensor_copy(wg_raw[:, :, NE], wt_raw[:, :]).then_inc(pad_made, 1)

        @block.scalar
        def _(act):
            ln.scalar(act)
            act.wait_ge(g_loaded, 64)
            act.wait_ge(pad_made, 3)
            nc.scalar.activation(wg_hi[:, :, :], wg_raw[:, :, :], ACT.Copy).then_inc(ghi_ready, 1)

            def split_w(x):
                act.wait_ge(w_loaded[x % 2], 16 * (x // 2 + 1))
                if x >= 2:
                    act.wait_ge(y_done, NT * x)
                nc.scalar.activation(whi[x % 2][:, :, :], raw[x % 2][:, :, :], ACT.Copy).then_inc(whi_ready, 1)

            split_w(0)
            act.wait_ge(shifted, 1)
            nc.scalar.activation(prob[:, :, :], logit[:, :, 0:NE], ACT.Exp).then_inc(exped, 1)
            nc.scalar.activation(thr[:, :], logit[:, :, NE], ACT.Exp, scale=-1.0).then_inc(exped, 1)
            for t in range(NT):
                act.wait_ge(wt_turned, t + 1)
                nc.scalar.activation(weight_T[:, t, :], ps_turn[t % 2][0:NE, 0, 0:PT], ACT.Copy).then_inc(wt_ready, 1)
            for x in range(1, NE):
                split_w(x)

        @block.vector
        def _(dve):
            link = chained(dve, step)
            ln.vector(dve, link)
            dve.wait_ge(ghi_ready, 1)
            nc.vector.tensor_tensor(wg_lo[:, :, :], wg_raw[:, :, :], wg_hi[:, :, :].bitcast(F32), ALU.subtract).then_inc(glo_ready, 1)

            def split_w(x):
                dve.wait_ge(whi_ready, x + 1)
                nc.vector.tensor_tensor(wlo[x % 2][:, :, :], raw[x % 2][:, :, :], whi[x % 2][:, :, :].bitcast(F32), ALU.subtract).then_inc(wlo_ready, 1)

            def spread(t):
                return t[:, :].unsqueeze(2).to_broadcast([PT, NT, NE])

            split_w(0)
            dve.wait_ge(logits_done, 1)
            link(nc.vector.tensor_tensor(logit[:, :, :], ps_logit[:, :, :], bg[:, :].unsqueeze(1).to_broadcast([PT, NT, NG]), ALU.add))
            link(nc.vector.tensor_reduce(peak[:, :], logit[:, :, 0:NE], AX.X, ALU.max))
            nc.vector.tensor_tensor(logit[:, :, 0:NE], logit[:, :, 0:NE], spread(peak), ALU.subtract).then_inc(shifted, 1)
            dve.wait_ge(exped, 2)
            link(nc.vector.tensor_reduce(total[:, :], prob[:, :, :], AX.X, ALU.add))
            link(nc.vector.reciprocal(total[:, :], total[:, :]))
            link(nc.vector.tensor_tensor(prob[:, :, :], prob[:, :, :], spread(total), ALU.mult))
            link(nc.vector.tensor_scalar(thr[:, :], thr[:, :], 1.0, None, ALU.add))
            link(nc.vector.reciprocal(thr[:, :], thr[:, :]))
            link(nc.vector.tensor_scalar(thr[:, :], thr[:, :], MAX_THRESHOLD, None, ALU.mult))
            link(nc.vector.tensor_tensor(weight[:, :, :], prob[:, :, :], spread(thr), ALU.subtract))
            link(nc.vector.tensor_scalar(weight[:, :, :], weight[:, :, :], 0.0, None, ALU.max))
            link(nc.vector.tensor_reduce(total[:, :], weight[:, :, :], AX.X, ALU.add))
            link(nc.vector.scalar_tensor_tensor(total[:, :], total[:, :], 0.0, total[:, :], ALU.is_equal, ALU.add))
            link(nc.vector.reciprocal(total[:, :], total[:, :]))
            nc.vector.tensor_tensor(weight[:, :, :], weight[:, :, :], spread(total), ALU.mult).then_inc(weights_ready, 1)
            split_w(1)
            for t in range(NT):
                dve.wait_ge(y_done, t + 1)
                nc.vector.tensor_tensor(X[:, t, :], X[:, t, :], ps_y[t % NY][:, :], ALU.add).then_inc(y_added, 1)
            dve.wait_ge(weights_ready, 1)
            for x in range(NE):
                if 1 <= x and x + 1 < NE:
                    split_w(x + 1)
                for t in range(NT):
                    n = NT * (x + 1) + t
                    dve.wait_ge(y_done, n + 1)
                    dve.wait_ge(y_added, n - NT + 1)
                    nc.vector.scalar_tensor_tensor(X[:, t, :], ps_y[n % NY][:, :], weight[:, t, x:x + 1], X[:, t, :],
                                                   ALU.mult, ALU.add).then_inc(y_added, 1)

        @block.tensor
        def _(pe):
            ln.tensor(pe)
            pe.wait_ge(ln.lo_ready, NT)
            pe.wait_ge(glo_ready, 1)
            for t in range(NT):
                tok = slice(t * PT, (t + 1) * PT)
                for k in range(KD):
                    last = three(nc, ps_logit[:, t, :], hT_hi[:, k, tok], hT_lo[:, k, tok], wg_hi[:, k, :], wg_lo[:, k, :],
                                 k == 0, k == KD - 1)
            last.then_inc(logits_done, 1)
            pe.wait_ge(weights_ready, 1)
            for t in range(NT):
                if t >= 2:
                    pe.wait_ge(wt_ready, t - 1)
                nc.tensor.transpose(ps_turn[t % 2][0:NE, 0, 0:PT], weight[:, t, :], ident[0:PT, 0:PT]).then_inc(wt_turned, 1)
            for t in range(NT):
                pe.wait_ge(wt_ready, t + 1)
                if t >= NY:
                    pe.wait_ge(y_added, t - NY + 1)
                nc.tensor.matmul(ps_y[t % NY][:, :], weight_T[:, t, :], be[:, :], start=True, stop=True).then_inc(y_done, 1)
            for x in range(NE):
                pe.wait_ge(wlo_ready, x + 1)
                for t in range(NT):
                    n = NT * (x + 1) + t
                    tok = slice(t * PT, (t + 1) * PT)
                    pe.wait_ge(y_added, n - NY + 1)
                    for k in range(KD):
                        last = three(nc, ps_y[n % NY][:, :], hT_hi[:, k, tok], hT_lo[:, k, tok], whi[x % 2][:, k, :], wlo[x % 2][:, k, :],
                                     k == 0, k == KD - 1)
                    last.then_inc(y_done, 1)


def build(nc, a, outs):
    with ExitStack() as ctx:
        def sb(name, shape, dt=F32):
            return ctx.enter_context(nc.sbuf_tensor(name, shape, dt))

        X = sb("X", [PT, NT, D])
        hT_hi = sb("hT_hi", [128, KD, N], F32R)
        hT_lo = sb("hT_lo", [128, KD, N], F32R)
        ident = sb("ident", [128, 128])
        eps_col = sb("eps_col", [128, 1])
        r = route_tensors(nc, ctx)
        sems = Semaphores(nc)
        with nc.sbuf_tensor("CT", [PT, NT, N], F32) as CT:
            with nc.sbuf_tensor("H1", [PT, NT, D], F32) as H:
                neighbour_mean_layer(nc, sems, a, X, H, hT_hi, hT_lo, ident, eps_col, CT)
            with nc.sbuf_tensor("H2", [PT, NT, D], F32) as H:
                route_and_shared_expert(nc, sems, a, X, H, hT_hi, hT_lo, ident, eps_col, r)
            routed_experts(nc, sems, a, ident, r)
            overfull_experts(nc, sems, a, ident, r)
            combine(nc, sems, X, CT, ident, r)
            with nc.sbuf_tensor("V", [PT, NT, HEADS, 64], F32) as V:
                with nc.sbuf_tensor("H3", [PT, NT, D], F32) as H:
                    project_qkv(nc, sems, a, X, H, hT_hi, hT_lo, ident, eps_col, V, r)
                attention(nc, sems, hT_hi, hT_lo, CT, V, r)
        attention_out(nc, sems, a, X, hT_hi, hT_lo)
        with nc.sbuf_tensor("H4", [PT, NT, D], F32) as H:
            gated_experts(nc, sems, a, X, H, hT_hi, hT_lo, ident, eps_col, outs["out"])


def kernel(**inputs):
    import numpy as _np
    import concourse.bacc as _bacc
    from concourse import mybir as _mybir
    from concourse.bass_utils import run_bass_kernel_spmd as _run

    nc = _bacc.Bacc("TRN2", target_bir_lowering=False, num_devices=1)
    arrays, a = {}, {}
    for name in inputs:
        v = _np.asarray(inputs[name])
        if name in ("L0_gnn_W_self", "L0_gnn_W_neigh"):
            v = v.T
        if name in ("L0_ffn_bs1", "L1_gnn_bq", "L1_gnn_bk", "L1_gnn_ba", "L1_ffn_W_thr"):
            v = v.reshape(-1, 128).T
        if name in ("L0_ffn_b1_sp", "L0_ffn_b1_fq"):
            v = v.reshape(8, 2, 128).transpose(2, 0, 1)
        v = _np.ascontiguousarray(v)
        arrays[f"in_{name}"] = v
        a[name] = nc.dram_tensor(f"in_{name}", v.shape, _mybir.dt.from_np(v.dtype), kind="ExternalInput").ap()
    outs = {"out": nc.dram_tensor("out_0", (N, D), F32, kind="ExternalOutput").ap()}
    build(nc, a, outs)
    r = _run(nc, [arrays], core_ids=[0])
    return r.results[0]["out_0"]
```

```python
from contextlib import ExitStack

import concourse.bass as bass
from concourse import mybir

F32 = mybir.dt.float32
F32R = mybir.dt.float32r
F16 = mybir.dt.float16
I32 = mybir.dt.int32
ALU = mybir.AluOpType
ACT = mybir.ActivationFunctionType
AX = mybir.AxisListType

N = 1250
D = 512
E = 40000
PT = 125
NT = N // PT
KD = D // 128
CHUNKS = [(0, 512), (512, 1024), (1024, N)]

WIN = 50
NWIN = N // WIN
CELLS = NT * WIN
EB = 512
NEB = (E + EB - 1) // EB
EC = EB // 128
TAIL = E - (NEB - 1) * EB
GT = 2
GW = GT * PT // WIN
NG = NT // GT
ROUND = 12582912.0
EPS = 1e-5


def chained(eng, sem):
    count = [0]

    def link(ins):
        count[0] += 1
        ins.then_inc(sem, 1)
        eng.wait_ge(sem, count[0])

    return link


class Semaphores:

    def __init__(self, nc):
        self.nc, self.used, self.stale = nc, [], []

    def new(self, ctx, name):
        handle = ctx.enter_context(self.nc.semaphore(name))
        self.used.append(handle)
        return handle

    def next_phase(self):
        self.used, self.stale = [], self.used

    def clear(self, pool):
        for handle in self.stale:
            pool.sem_clear(handle)


class Norm:

    def __init__(self, nc, sems, ctx, tag, X, H, hT_hi, hT_lo, ps, ident, eps_col, stats):
        self.nc, self.X, self.H, self.hi, self.lo, self.ps, self.ident = nc, X, H, hT_hi, hT_lo, ps, ident
        self.eps_col = eps_col

        def sb(name, shape):
            return ctx.enter_context(nc.sbuf_tensor(f"{tag}_{name}", shape, F32))

        def sem(name):
            return sems.new(ctx, f"{tag}_{name}")

        self.stats = stats
        self.mv = sb("mv", [PT, NT, 2])
        self.sd = sb("sd", [PT, NT])
        self.rs = sb("rs", [PT, NT])
        self.t0 = sb("t0", [PT, NT])
        self.nmr = sb("nmr", [PT, NT])
        self.var_ready = sem("var_ready")
        self.sd_ready = sem("sd_ready")
        self.h_ready = sem("h_ready")
        self.turned = sem("turned")
        self.hi_ready = sem("hi_ready")
        self.lo_ready = sem("lo_ready")

    def vector(self, dve, link, measured):
        nc = self.nc
        if not measured:
            for t in range(NT):
                last = nc.vector.bn_stats(self.stats[:, t, :], self.X[:, t, :])
            link(last)
        for t in range(NT):
            last = nc.vector.bn_aggr(self.mv[:, t, :], self.stats[:, t, :])
        last.then_inc(self.var_ready, 1)
        dve.wait_ge(self.var_ready, 1)
        link(nc.vector.tensor_scalar(self.t0[:, :], self.mv[:, :, 1], EPS, -0.5, ALU.add, ALU.mult))
        dve.wait_ge(self.sd_ready, 1)
        link(nc.vector.reciprocal(self.rs[:, :], self.sd[:, :]))
        link(nc.vector.tensor_tensor(self.nmr[:, :], self.rs[:, :], self.rs[:, :], ALU.mult))
        link(nc.vector.tensor_tensor(self.nmr[:, :], self.nmr[:, :], self.t0[:, :], ALU.mult))
        link(nc.vector.scalar_tensor_tensor(self.rs[:, :], self.nmr[:, :], 1.5, self.rs[:, :], ALU.add, ALU.mult))
        link(nc.vector.scalar_tensor_tensor(self.nmr[:, :], self.mv[:, :, 0], -1.0, self.rs[:, :], ALU.mult, ALU.mult))
        for t in range(NT):
            nc.vector.tensor_scalar(self.H[:, t, :], self.X[:, t, :], self.rs[:, t:t + 1], self.nmr[:, t:t + 1],
                                    ALU.mult, ALU.add).then_inc(self.h_ready, 1)
        for t in range(NT):
            dve.wait_ge(self.hi_ready, t + 1)
            cols = slice(t * PT, (t + 1) * PT)
            nc.vector.tensor_tensor(self.lo[:, :, cols], self.ps[t % 2][:, :, 0:PT],
                                    self.hi[:, :, cols].bitcast(F32), ALU.subtract).then_inc(self.lo_ready, 1)

    def scalar(self, act):
        nc = self.nc
        act.wait_ge(self.var_ready, 1)
        nc.scalar.activation(self.sd[:, :], self.mv[:, :, 1], ACT.Sqrt, bias=self.eps_col[0:PT, :]).then_inc(self.sd_ready, 1)
        for t in range(NT):
            act.wait_ge(self.turned, t + 1)
            nc.scalar.activation(self.hi[:, :, t * PT:(t + 1) * PT], self.ps[t % 2][:, :, 0:PT],
                                 ACT.Copy).then_inc(self.hi_ready, 1)

    def tensor(self, pe):
        nc = self.nc
        for t in range(NT):
            pe.wait_ge(self.h_ready, t + 1)
            if t >= 2:
                pe.wait_ge(self.lo_ready, t - 1)
                pe.wait_ge(self.hi_ready, t - 1)
            for k in range(KD):
                last = nc.tensor.transpose(self.ps[t % 2][:, k, 0:PT], self.H[:, t, k * 128:(k + 1) * 128],
                                           self.ident[0:PT, 0:PT])
            last.then_inc(self.turned, 1)


def three(nc, out, a_hi, a_lo, b_hi, b_lo, start, stop):
    nc.tensor.matmul(out, a_lo, b_hi, start=start, stop=False)
    nc.tensor.matmul(out, a_hi, b_lo, start=False, stop=False)
    return nc.tensor.matmul(out, a_hi, b_hi, start=False, stop=stop)


def neighbour_mean_layer(nc, sems, a, X, H, hT_hi, hT_lo, ident, eps_col, stats, CT):
    sems.next_phase()
    with ExitStack() as ctx:
        def sb(name, shape, dt=F32):
            return ctx.enter_context(nc.sbuf_tensor(name, shape, dt))

        def pb(name, shape, dt=F32):
            return ctx.enter_context(nc.psum_tensor(name, shape, dt))

        def sem(name):
            return sems.new(ctx, name)

        ACT_ROWS = 2
        SLOTS = 2 * EC
        edges = sb("edges", [NEB, 2, EB], I32)
        edges_f = edges[:, :, :].bitcast(F32)
        reach = sb("reach", [NEB, 2])
        reach_b = sb("reach_b", [NEB, 2, NWIN])
        sender_tile = sb("sender_tile", [128, EC, NEB])
        sender_row = sb("sender_row", [128, EC, NEB])
        window = sb("window", [128, EC, NEB])
        cell = sb("cell", [128, EC, NEB])
        iota_b = sb("iota_b", [NWIN, NEB])
        win_first = sb("win_first", [NWIN, 1])
        meets = sb("meets", [NWIN, NEB])
        cand = sb("cand", [NWIN, 2, NEB])
        span = sb("span", [NWIN, 2])
        span_row = sb("span_row", [1, 2 * NWIN], I32)
        iota_c = sb("iota_c", [128, CELLS], F16)
        rows1h = sb("rows1h", [128, SLOTS, PT], F16)
        cells1h = sb("cells1h", [128, SLOTS, CELLS], F16)
        distance = sb("distance", [128, ACT_ROWS, PT], F16)
        one_col = sb("one_col", [128, 1])
        zeros = sb("zeros", [128, CELLS], F16)
        ps_turn = [pb(f"ps_turn{i}", [128, 4, 128]) for i in range(2)]
        ps_span = pb("ps_span", [128, 512])
        w_raw = sb("w_raw", [128, KD, D])
        w_hi = [sb(f"w_hi{i}", [128, KD, D], F32R) for i in range(2)]
        w_lo = [sb(f"w_lo{i}", [128, KD, D], F32R) for i in range(2)]
        agg_hi = sb("agg_hi", [128, KD, GT * PT], F32R)
        agg_lo = sb("agg_lo", [128, KD, GT * PT], F32R)
        bias = sb("bias", [PT, D])
        ones = sb("ones", [PT, 1])
        csum = sb("csum", [PT, GT * PT])
        rdeg = sb("rdeg", [PT, NT])
        mean = [sb(f"mean{i}", [PT, D]) for i in range(2)]
        ps_agg = [pb(f"ps_agg{i}", [128, 512]) for i in range(2)]
        ps_self = ps_turn
        ps_count = [pb(f"ps_count{i}", [PT, NT, WIN]) for i in range(2)]

        made = sem("made")
        edges_loaded = sem("edges_loaded")
        edges_ready = sem("edges_ready")
        reach_ready = sem("reach_ready")
        edges_turned = sem("edges_turned")
        edges_taken = sem("edges_taken")
        reach_spread = sem("reach_spread")
        span_ready = sem("span_ready")
        span_turned = sem("span_turned")
        span_known = sem("span_known")
        onehot_ready = sem("onehot_ready")
        onehot_used = sem("onehot_used")
        counted = sem("counted")
        copied = sem("copied")
        x_loaded = sem("x_loaded")
        distances_made = sem("distances_made")
        rows_ready = sem("rows_ready")
        dve_step = sem("dve_step")
        w_loaded = sem("g_w_loaded")
        bias_loaded = sem("g_bias_loaded")
        whi_ready = sem("g_whi_ready")
        wlo_ready = sem("g_wlo_ready")
        csum_ready = sem("csum_ready")
        csum_step = sem("csum_step")
        deg_done = sem("deg_done")
        rdeg_ready = sem("rdeg_ready")
        agg_done = sem("agg_done")
        agghi_ready = sem("agghi_ready")
        agglo_ready = sem("agglo_ready")
        self_done = sem("self_done")
        neigh_done = sem("neigh_done")
        mean_ready = sem("mean_ready")
        self_added = sem("self_added")
        summed = sem("g_summed")
        pool_step = sem("g_pool_step")
        ln = Norm(nc, sems, ctx, "ln1", X, H, hT_hi, hT_lo, ps_turn, ident, eps_col, stats)
        block = ctx.enter_context(nc.Block())

        @block.sync
        def _(sp):
            full = (NEB - 1) * EB
            for i, name in enumerate(("dst", "src")):
                sp.dma_start(edges[0:NEB - 1, i, :], a[name][0:full].rearrange("(b q) -> b q", q=EB)).then_inc(edges_loaded, 16)
                for j in range(EB // TAIL):
                    sp.dma_start(edges[NEB - 1:NEB, i, j * TAIL:(j + 1) * TAIL],
                                 a[name][full:E].rearrange("(b q) -> b q", b=1)).then_inc(edges_loaded, 16)
            for t in range(NT):
                sp.dma_start(X[:, t, :], a["x"][t * PT:(t + 1) * PT, :]).then_inc(x_loaded, 16)
            for i, name in enumerate(("L0_gnn_W_self", "L0_gnn_W_neigh")):
                if i:
                    sp.wait_ge(wlo_ready, i)
                sp.dma_start(w_raw[:, :, :], a[name].rearrange("(k p) n -> p k n", p=128)).then_inc(w_loaded, 16)
            sp.dma_start(bias[:, :], a["L0_gnn_b"].partition_broadcast(PT)).then_inc(bias_loaded, 16)

        @block.gpsimd
        def _(pool):
            sems.clear(pool)
            nc.gpsimd.memset(ident[:, :], 0.0).then_inc(made, 1)
            nc.gpsimd.memset(eps_col[:, :], EPS).then_inc(made, 1)
            nc.gpsimd.memset(zeros[:, :], 0.0).then_inc(made, 1)
            nc.gpsimd.iota(iota_c[:, :], [[1, CELLS]], base=0, channel_multiplier=0,
                           allow_small_or_imprecise_dtypes=True).then_inc(made, 1)
            nc.gpsimd.memset(ones[:, :], 1.0).then_inc(made, 1)
            nc.gpsimd.memset(one_col[:, :], 1.0).then_inc(made, 1)
            nc.gpsimd.iota(iota_b[:, :], [[1, NEB]], base=0, channel_multiplier=0,
                           allow_small_or_imprecise_dtypes=True).then_inc(made, 1)
            nc.gpsimd.iota(win_first[:, :], [[1, 1]], base=0, channel_multiplier=WIN,
                           allow_small_or_imprecise_dtypes=True).then_inc(made, 1)
            pool.wait_ge(made, 1)
            nc.gpsimd.affine_select(out=ident[:, :], in_=ident[:, :], compare_op=ALU.not_equal, fill=1.0,
                                    base=0, pattern=[[-1, 128]], channel_multiplier=1).then_inc(made, 1)
            for i in range(2):
                pool.wait_ge(w_loaded, 16 * (i + 1))
                pool.wait_ge(whi_ready, i + 1)
                nc.gpsimd.tensor_tensor(w_lo[i][:, :, :], w_raw[:, :, :], w_hi[i][:, :, :].bitcast(F32),
                                        ALU.subtract).then_inc(wlo_ready, 1)
            def sum_counts(g):
                cols = slice(g * GT * PT, (g + 1) * GT * PT)
                pool.wait_ge(copied, (g + 1) * GW + 2)
                if g:
                    pool.wait_ge(deg_done, g)
                nc.gpsimd.tensor_tensor(csum[:, :], CT[:, 0, cols], CT[:, 1, cols], ALU.add).then_inc(csum_step, 1)
                for s in range(2, NT):
                    pool.wait_ge(csum_step, (NT - 2) * g + s - 1)
                    last = nc.gpsimd.tensor_tensor(csum[:, :], csum[:, :], CT[:, s, cols], ALU.add)
                    last.then_inc(csum_step if s < NT - 1 else csum_ready, 1)

            def finish(t):
                if t == 0:
                    pool.wait_ge(bias_loaded, 16)
                m = mean[t % 2]
                pool.wait_ge(self_added, t + 1)
                nc.gpsimd.tensor_tensor(m[:, :], m[:, :], bias[:, :], ALU.add).then_inc(pool_step, 1)
                pool.wait_ge(pool_step, 2 * t + 1)
                nc.gpsimd.tensor_scalar(m[:, :], m[:, :], 0.0, None, ALU.max).then_inc(pool_step, 1)
                pool.wait_ge(pool_step, 2 * t + 2)
                nc.gpsimd.tensor_tensor(X[:, t, :], m[:, :], X[:, t, :], ALU.add).then_inc(summed, 1)

            for g in range(NG):
                sum_counts(g)
                if g:
                    for t in range((g - 1) * GT, g * GT):
                        finish(t)

        @block.vector
        def _(dve):
            link = chained(dve, dve_step)
            dve.wait_ge(edges_loaded, 32 * (1 + EB // TAIL))
            nc.vector.tensor_copy(edges_f, edges[:, :, :]).then_inc(edges_ready, 1)
            dve.wait_ge(edges_ready, 1)
            nc.vector.tensor_reduce(reach[:, 0:1], edges_f[:, 0, :], AX.X, ALU.min)
            link(nc.vector.tensor_reduce(reach[:, 1:2], edges_f[:, 0, :], AX.X, ALU.max))
            for i in range(2):
                last = nc.vector.tensor_scalar(reach_b[:, i, :], edges_f[:, 0, 0:NWIN], 0.0, reach[:, i:i + 1],
                                               ALU.mult, ALU.add)
            last.then_inc(reach_ready, 1)
            dve.wait_ge(edges_turned, 2)
            dst_t, src_t = (ps_turn[i][:, 0:EC, 0:NEB] for i in range(2))
            link(nc.vector.tensor_scalar(sender_tile[:, :, :], src_t, 1.0 / PT, -(PT - 1) / (2 * PT), ALU.mult, ALU.add))
            link(nc.vector.tensor_scalar(sender_tile[:, :, :], sender_tile[:, :, :], ROUND, -ROUND, ALU.add, ALU.add))
            link(nc.vector.scalar_tensor_tensor(sender_row[:, :, :], sender_tile[:, :, :], -float(PT), src_t, ALU.mult, ALU.add))
            link(nc.vector.tensor_scalar(window[:, :, :], dst_t, 1.0 / WIN, -(WIN - 1) / (2 * WIN), ALU.mult, ALU.add))
            link(nc.vector.tensor_scalar(window[:, :, :], window[:, :, :], ROUND, -ROUND, ALU.add, ALU.add))
            link(nc.vector.scalar_tensor_tensor(cell[:, :, :], window[:, :, :], float(CELLS - WIN), dst_t, ALU.mult, ALU.add))
            link(nc.vector.scalar_tensor_tensor(cell[:, :, :], sender_tile[:, :, :], float(WIN), cell[:, :, :], ALU.mult, ALU.add))
            first, used = TAIL // 128, TAIL % 128
            nc.vector.memset(cell[used:128, first, NEB - 1:NEB], -1.0e6)
            link(nc.vector.memset(cell[:, first + 1:EC, NEB - 1:NEB], -1.0e6))
            nc.vector.tensor_copy(window[0:1, 0, 0:1], cell[0:1, 0, 0:1]).then_inc(edges_taken, 1)
            dve.wait_ge(made, 9)
            dve.wait_ge(reach_spread, 1)
            low, high = ps_span[0:NWIN, 0:NEB], ps_span[0:NWIN, 128:128 + NEB]
            link(nc.vector.tensor_scalar(meets[:, :], high, win_first[:, :], None, ALU.is_ge))
            link(nc.vector.tensor_scalar(cand[:, 0, :], low, win_first[:, :], float(WIN - 1), ALU.subtract, ALU.is_le))
            link(nc.vector.tensor_tensor(meets[:, :], meets[:, :], cand[:, 0, :], ALU.mult))
            nc.vector.scalar_tensor_tensor(cand[:, 1, :], iota_b[:, :], 1.0, meets[:, :], ALU.add, ALU.mult)
            link(nc.vector.scalar_tensor_tensor(cand[:, 0, :], iota_b[:, :], -float(NEB), meets[:, :], ALU.add, ALU.mult))
            nc.vector.tensor_reduce(span[:, 1:2], cand[:, 1, :], AX.X, ALU.max)
            link(nc.vector.tensor_reduce(span[:, 0:1], cand[:, 0, :], AX.X, ALU.min))
            link(nc.vector.tensor_scalar(span[:, 0:1], span[:, 0:1], float(NEB), float(NEB - 1), ALU.add, ALU.min))
            nc.vector.scalar_tensor_tensor(span[:, 1:2], span[:, 0:1], 1.0, span[:, 1:2], ALU.add, ALU.max).then_inc(span_ready, 1)
            dve.wait_ge(span_turned, 1)
            nc.vector.tensor_copy(span_row[:, :], ps_span[0:1, 256:256 + 2 * NWIN]).then_inc(span_known, 1)
            dve.wait_ge(span_known, 1)
            dve.wait_ge(x_loaded, 16 * NT)
            ln.vector(dve, link, measured=False)
            done = dve.alloc_register("dve_chunks")
            slot = dve.alloc_register("dve_slot")
            dve.reg_mov(done, 0)
            dve.reg_mov(slot, 0)
            for w in range(NWIN + GW + 1):
                if w < NWIN:
                    lo_b = dve.value_load(span_row[0:1, w:w + 1], min_val=0, max_val=NEB - 1)
                    hi_b = dve.value_load(span_row[0:1, NWIN + w:NWIN + w + 1], min_val=1, max_val=NEB)
                    with dve.Fori(lo_b, hi_b) as b:
                        n = dve.snap(done, min_val=0, max_val=NWIN * NEB * EC)
                        s = dve.snap(slot, min_val=0, max_val=EC)
                        dve.wait_ge(onehot_used, n + EC)
                        for j in range(EC):
                            if j >= ACT_ROWS:
                                nc.vector.tensor_scalar(rows1h[:, bass.DynSlice(s + j, 1), :], iota_c[:, 0:PT].unsqueeze(1),
                                                        sender_row[:, j, bass.DynSlice(b, 1)], None, ALU.is_equal)
                            last = nc.vector.tensor_scalar(cells1h[:, bass.DynSlice(s + j, 1), :], iota_c[:, :].unsqueeze(1),
                                                           cell[:, j, bass.DynSlice(b, 1)], -float(CELLS * w),
                                                           ALU.subtract, ALU.is_equal)
                        last.then_inc(onehot_ready, EC)
                        dve.reg_add(done, done, EC)
                        dve.reg_mod(slot, done, SLOTS)
                if NWIN <= w < NWIN + NG - 1:
                    for t in range((w - NWIN) * GT, (w - NWIN + 1) * GT):
                        dve.wait_ge(summed, t + 1)
                        nc.vector.bn_stats(stats[:, t, :], X[:, t, :])
                if w <= GW:
                    continue
                g, k = divmod(w - GW - 1, GW)
                if k == KD - 1:
                    dve.wait_ge(deg_done, g + 1)
                    cols = rdeg[:, g * GT:(g + 1) * GT]
                    link(nc.vector.tensor_scalar(cols, ps_span[0:PT, g * GT:(g + 1) * GT], 1.0, None, ALU.max))
                    nc.vector.reciprocal(cols, cols).then_inc(rdeg_ready, 1)
                if k < KD:
                    dve.wait_ge(agghi_ready, g * KD + k + 1)
                    nc.vector.tensor_tensor(agg_lo[:, k, :], ps_agg[k % 2][:, 0:GT * PT],
                                            agg_hi[:, k, :].bitcast(F32), ALU.subtract).then_inc(agglo_ready, 1)
                else:
                    for t in range(g * GT, (g + 1) * GT):
                        dve.wait_ge(self_done, t + 1)
                        dve.wait_ge(mean_ready, t + 1)
                        nc.vector.tensor_tensor(mean[t % 2][:, :], mean[t % 2][:, :], ps_self[t % 2][0:PT, :, :].rearrange("p a b -> p (a b)"),
                                                ALU.add).then_inc(self_added, 1)
            dve.wait_ge(bias_loaded, 16)
            for t in range(NT - GT, NT):
                m = mean[t % 2]
                dve.wait_ge(self_added, t + 1)
                link(nc.vector.tensor_tensor(m[:, :], m[:, :], bias[:, :], ALU.add))
                link(nc.vector.scalar_tensor_tensor(X[:, t, :], m[:, :], 0.0, X[:, t, :], ALU.max, ALU.add))
                link(nc.vector.bn_stats(stats[:, t, :], X[:, t, :]))

        @block.tensor
        def _(pe):
            pe.wait_ge(made, 9)
            pe.wait_ge(edges_ready, 1)
            for i in range(2):
                for j in range(EC):
                    last = nc.tensor.transpose(ps_turn[i][:, j, 0:NEB], edges_f[:, i, j * 128:(j + 1) * 128],
                                               ident[0:NEB, 0:NEB])
                last.then_inc(edges_turned, 1)
            pe.wait_ge(reach_ready, 1)
            for i in range(2):
                last = nc.tensor.matmul(ps_span[0:NWIN, i * 128:i * 128 + NEB], reach_b[:, i, :], ident[0:NEB, 0:NEB],
                                        start=True, stop=True)
            last.then_inc(reach_spread, 1)
            pe.wait_ge(span_ready, 1)
            for i in range(2):
                last = nc.tensor.matmul(ps_span[0:1, 256 + i * NWIN:256 + (i + 1) * NWIN], span[:, i:i + 1],
                                        ident[0:NWIN, 0:NWIN], start=True, stop=True)
            last.then_inc(span_turned, 1)
            pe.wait_ge(edges_taken, 1)
            ln.tensor(pe)
            pe.wait_ge(span_known, 1)
            pe.sem_inc(onehot_used, SLOTS)
            done = pe.alloc_register("pe_chunks")
            slot = pe.alloc_register("pe_slot")
            pe.reg_mov(done, 0)
            pe.reg_mov(slot, 0)

            def self_product(t):
                if t == 0:
                    pe.wait_ge(wlo_ready, 1)
                    pe.wait_ge(ln.hi_ready, NT)
                    pe.wait_ge(ln.lo_ready, NT)
                if t >= 2:
                    pe.wait_ge(self_added, t - 1)
                tok = slice(t * PT, (t + 1) * PT)
                for k in range(KD):
                    last = three(nc, ps_self[t % 2][0:PT, :, :], hT_hi[:, k, tok], hT_lo[:, k, tok],
                                 w_hi[0][:, k, :], w_lo[0][:, k, :], k == 0, k == KD - 1)
                last.then_inc(self_done, 1)

            def neighbours_product(t):
                if t == 0:
                    pe.wait_ge(wlo_ready, 2)
                if t % GT == 0:
                    pe.wait_ge(agglo_ready, (t // GT + 1) * KD)
                tok = slice(t % GT * PT, (t % GT + 1) * PT)
                for k in range(KD):
                    last = three(nc, ps_agg[t % 2][0:PT, :], agg_hi[:, k, tok], agg_lo[:, k, tok],
                                 w_hi[1][:, k, :], w_lo[1][:, k, :], k == 0, k == KD - 1)
                last.then_inc(neigh_done, 1)

            def aggregate(g, f):
                cols = slice(g * GT * PT, (g + 1) * GT * PT)
                if f == 0:
                    pe.wait_ge(copied, (g + 1) * GW + 2)
                if f == KD - 1:
                    pe.wait_ge(csum_ready, g + 1)
                    for d in range(GT):
                        last = nc.tensor.matmul(ps_span[0:PT, g * GT + d:g * GT + d + 1], csum[:, d * PT:(d + 1) * PT], ones[:, :],
                                                start=True, stop=True)
                    last.then_inc(deg_done, 1)
                if f >= 2:
                    pe.wait_ge(agglo_ready, g * KD + f - 1)
                elif g:
                    pe.wait_ge(mean_ready, (g - 1) * GT + f + 1)
                for s in range(NT):
                    last = nc.tensor.matmul(ps_agg[f % 2][:, 0:GT * PT], H[:, s, f * 128:(f + 1) * 128],
                                            CT[:, s, cols], start=(s == 0), stop=(s == NT - 1))
                last.then_inc(agg_done, 1)

            for w in range(NWIN + GW):
                if w < NWIN:
                    ps = ps_count[w % 2]
                    lo_b = pe.value_load(span_row[0:1, w:w + 1], min_val=0, max_val=NEB - 1)
                    hi_b = pe.value_load(span_row[0:1, NWIN + w:NWIN + w + 1], min_val=1, max_val=NEB)
                    if w >= 2:
                        pe.wait_ge(copied, w + 1)
                    nc.tensor.matmul(ps[:, :, :], zeros[:, 0:PT], zeros[:, :], start=True, stop=False, skip_group_check=True)
                    with pe.Fori(lo_b, hi_b):
                        n = pe.snap(done, min_val=0, max_val=NWIN * NEB * EC)
                        so = pe.snap(slot, min_val=0, max_val=EC)
                        pe.wait_ge(rows_ready, n + EC)
                        pe.wait_ge(onehot_ready, n + EC)
                        for j in range(EC):
                            last = nc.tensor.matmul(ps[:, :, :], rows1h[:, bass.DynSlice(so + j, 1), :],
                                                    cells1h[:, bass.DynSlice(so + j, 1), :],
                                                    start=False, stop=False, skip_group_check=True)
                        last.then_inc(onehot_used, EC)
                        pe.reg_add(done, done, EC)
                        pe.reg_mod(slot, done, SLOTS)
                    nc.tensor.matmul(ps[:, 0, 0:2], zeros[:, 0:PT], zeros[:, 0:2], start=False, stop=True,
                                     skip_group_check=True).then_inc(counted, 1)
                if w < GW:
                    continue
                g, k = divmod(w - GW, GW)
                if k < KD:
                    aggregate(g, k)
                if k >= KD - 1:
                    self_product(g * GT + k - (KD - 1))
                if k == KD:
                    for t in range(g * GT, (g + 1) * GT):
                        neighbours_product(t)

        @block.scalar
        def _(act):
            act.wait_ge(made, 9)
            ln.scalar(act)
            for i in range(2):
                act.wait_ge(w_loaded, 16 * (i + 1))
                nc.scalar.activation(w_hi[i][:, :, :], w_raw[:, :, :], ACT.Copy).then_inc(whi_ready, 1)
            act.sem_inc(copied, 2)
            act.wait_ge(span_known, 1)
            done = act.alloc_register("act_chunks")
            slot = act.alloc_register("act_slot")
            act.reg_mov(done, 0)
            act.reg_mov(slot, 0)

            def sender_rows(w):
                lo_b = act.value_load(span_row[0:1, w:w + 1], min_val=0, max_val=NEB - 1)
                hi_b = act.value_load(span_row[0:1, NWIN + w:NWIN + w + 1], min_val=1, max_val=NEB)
                with act.Fori(lo_b, hi_b) as b:
                    n = act.snap(done, min_val=0, max_val=NWIN * NEB * EC)
                    s = act.snap(slot, min_val=0, max_val=EC)
                    act.wait_ge(onehot_used, n + EC)
                    for j in range(ACT_ROWS):
                        last = nc.scalar.activation(distance[:, j, :], iota_c[:, 0:PT], ACT.Abs, scale=-1.0,
                                                    bias=sender_row[:, j, bass.DynSlice(b, 1)])
                    last.then_inc(distances_made, EC)
                    act.wait_ge(distances_made, n + EC)
                    nc.scalar.activation(rows1h[:, bass.DynSlice(s, ACT_ROWS), :], distance[:, :, :], ACT.Relu, scale=-1.0,
                                         bias=one_col[:, :]).then_inc(rows_ready, EC)
                    act.wait_ge(rows_ready, n + EC)
                    act.reg_add(done, done, EC)
                    act.reg_mod(slot, done, SLOTS)

            sender_rows(0)
            for w in range(NWIN + GW):
                if w + 1 < NWIN:
                    sender_rows(w + 1)
                if w < NWIN:
                    act.wait_ge(counted, w + 1)
                    nc.scalar.activation(CT[:, :, w * WIN:(w + 1) * WIN], ps_count[w % 2][:, :, :],
                                         ACT.Copy).then_inc(copied, 1)
                if w < GW:
                    continue
                g, k = divmod(w - GW, GW)
                if k < KD:
                    if k == 0 and g:
                        act.wait_ge(neigh_done, g * GT)
                    act.wait_ge(agg_done, g * KD + k + 1)
                    nc.scalar.activation(agg_hi[:, k, :], ps_agg[k % 2][:, 0:GT * PT], ACT.Copy).then_inc(agghi_ready, 1)
                    continue
                act.wait_ge(rdeg_ready, g + 1)
                for t in range(g * GT, (g + 1) * GT):
                    act.wait_ge(neigh_done, t + 1)
                    if t >= 2:
                        act.wait_ge(summed, t - 1)
                    nc.scalar.activation(mean[t % 2][:, :], ps_agg[t % 2][0:PT, :], ACT.Copy,
                                         scale=rdeg[:, t:t + 1]).then_inc(mean_ready, 1)




NB = 2
NE = 8
NX = NB * NE
FF = 256
KF = FF // 128
FIRST_ROWS = 256
MORE_ROWS = 128
ROUNDS = (N - FIRST_ROWS + MORE_ROWS - 1) // MORE_ROWS
MORE_FROM = NX * FIRST_ROWS
ROWS = MORE_FROM + NB * ROUNDS * MORE_ROWS
BANKS = ("sp", "fq")


class Route:
    pass


def route_tensors(nc, ctx):
    r = Route()

    def sb(name, shape, dt=F32):
        return ctx.enter_context(nc.sbuf_tensor(name, shape, dt))

    r.gate = sb("gate", [PT, NT, NB])
    r.slot = sb("slot", [PT, NT, NB], I32)
    r.token = sb("token", [PT, NT], I32)
    r.idx = sb("idx", [128, FIRST_ROWS // 128 * NX], I32)
    r.rounds = sb("rounds", [1, NB], I32)
    r.expert_of = sb("expert_of", [1, NB * NB * ROUNDS], I32)
    r.h_rows = nc.dram_tensor("h_rows", (N, D), F32).ap()
    r.y_rows = nc.dram_tensor("y_rows", (ROWS, D), F32).ap()
    r.token_of = nc.dram_tensor("token_of", (ROWS, 1), I32).ap()
    r.qk = nc.dram_tensor("qk_rows", (4, FF, N), F32).ap()
    return r


def route_and_shared_expert(nc, sems, a, X, H, hT_hi, hT_lo, ident, eps_col, stats, r):
    UNITS = [(m, c) for m in range(KF) for c in range(len(CHUNKS))]
    ST, RING = FIRST_ROWS // 128, 4
    RANKED = [(b, t) for b in range(NB) for t in range(NT)]
    sems.next_phase()
    with ExitStack() as ctx:
        def sb(name, shape, dt=F32):
            return ctx.enter_context(nc.sbuf_tensor(name, shape, dt))

        def pb(name, shape, dt=F32):
            return ctx.enter_context(nc.psum_tensor(name, shape, dt))

        def sem(name):
            return sems.new(ctx, "r_" + name)

        wr_raw = sb("wr_raw", [128, KD, NX])
        wr_hi = sb("wr_hi", [128, KD, NX], F32R)
        wr_lo = sb("wr_lo", [128, KD, NX], F32R)
        br = sb("br", [PT, NX])
        s_raw = sb("s_raw", [128, 2048])
        s_hi = sb("s_hi", [128, 2048], F32R)
        s_lo = sb("s_lo", [128, 2048], F32R)
        bs1 = sb("bs1", [128, KF])
        bs2 = sb("bs2", [PT, D])
        act1 = [sb(f"act1_{i}", [128, 512]) for i in range(2)]
        gT_hi = sb("gT_hi", [128, KF, N], F32R)
        gT_lo = sb("gT_lo", [128, KF, N], F32R)
        logit_T = sb("logit_T", [NX, N])
        logit = sb("logit", [PT, NT, NX])
        work = sb("work", [PT, NT, NX])
        prob = sb("prob", [PT, NT, NX])
        peak = sb("peak", [PT, NT * NB])
        onehot = sb("onehot", [PT, NT, NX])
        onehot16 = sb("onehot16", [PT, NT, NX], F16)
        slot_f = sb("slot_f", [PT, NT * NB])
        falling = sb("falling", [PT, NT * NB, NE])
        row0 = sb("row0", [PT, NT, NX])
        before = sb("before", [PT, NX])
        ones16 = sb("ones16", [PT, NX])
        jump = sb("jump", [PT, NX])
        zero_f = sb("zero_f", [128, D])
        upto = sb("upto", [PT, PT], F16)
        every = sb("every", [PT, PT], F16)
        zero_i = sb("zero_i", [128, ROWS // 128], I32)
        token_f = sb("token_f", [PT, NT])
        token16 = sb("token16", [PT, NT, NX], F16)
        rank = sb("rank", [PT, NT * NB])
        iota_rank = sb("iota_rank", [PT, FIRST_ROWS], F16)
        rank1h = sb("rank1h", [PT, RING, FIRST_ROWS], F16)
        zero16 = sb("zero16", [PT, 128], F16)
        more = sb("more", [PT, NX])
        ended = sb("ended", [PT, NX])
        nth_round = sb("nth_round", [1, NB, NB * ROUNDS, NE])
        had = sb("had", [1, NB, NB * ROUNDS, NE])
        had_n = sb("had_n", [1, NB, NB * ROUNDS])
        bank_more = sb("bank_more", [1, NB])
        kth = sb("kth", [PT, NX, ROUNDS])
        bounds = sb("bounds", [PT, NX, ROUNDS])
        ps_turn = [pb(f"r_turn{i}", [128, 4, 128]) for i in range(2)]
        ps_logit = pb("ps_logit", [PT, NT, NX])
        ps_rank = pb("ps_rank", [PT, 512])
        ps_up = [pb(f"ps_up{i}", [128, 512]) for i in range(2)]
        ps_down = [pb(f"ps_down{i}", [PT, D]) for i in range(2)]
        ps_logit_T = [ps_up[0], ps_up[1], ps_down[0]]
        ps_idx = ps_turn[0]

        w_loaded, b_loaded = sem("w_loaded"), sem("b_loaded")
        whi_ready, wlo_ready, slo_ready = sem("whi_ready"), sem("wlo_ready"), sem("slo_ready")
        made, saved = sem("made"), sem("saved")
        logitT_done, logitT_ready = sem("logitT_done"), sem("logitT_ready")
        logits_done, shifted, exped = sem("logits_done"), sem("shifted"), sem("exped")
        onehot_ready, ranked = sem("onehot_ready"), sem("ranked")
        rank1h_ready, rank1h_used, idx_done, cleared = sem("rank1h_ready"), sem("rank1h_used"), sem("idx_done"), sem("cleared")
        up_done, act_ready, ghi_ready, glo_ready = sem("up_done"), sem("act_ready"), sem("ghi_ready"), sem("glo_ready")
        biased, down_done, y_ready, step = sem("biased"), sem("down_done"), sem("y_ready"), sem("step")
        ln = Norm(nc, sems, ctx, "ln2", X, H, hT_hi, hT_lo, ps_turn, ident, eps_col, stats)
        block = ctx.enter_context(nc.Block())
        w1 = (s_hi[:, 0:1024].rearrange("p (k f) -> p k f", k=KD), s_lo[:, 0:1024].rearrange("p (k f) -> p k f", k=KD))
        w2 = (s_hi[:, 1024:2048].rearrange("p (k f) -> p k f", k=KF), s_lo[:, 1024:2048].rearrange("p (k f) -> p k f", k=KF))

        @block.sync
        def _(sp):
            for b, bank in enumerate(BANKS):
                sp.dma_start(wr_raw[:, :, b * NE:(b + 1) * NE],
                             a[f"L0_ffn_Wr_{bank}"].rearrange("(k p) e -> p k e", p=128)).then_inc(w_loaded, 16)
                sp.dma_start(br[:, b * NE:(b + 1) * NE], a[f"L0_ffn_br_{bank}"].partition_broadcast(PT)).then_inc(b_loaded, 16)
            sp.dma_start(s_raw[:, 0:1024].rearrange("p (k f) -> p k f", k=KD),
                         a["L0_ffn_Ws1"].rearrange("(k p) f -> p k f", p=128)).then_inc(w_loaded, 16)
            sp.dma_start(s_raw[:, 1024:2048].rearrange("p (k f) -> p k f", k=KF),
                         a["L0_ffn_Ws2"].rearrange("(k p) f -> p k f", p=128)).then_inc(w_loaded, 16)
            sp.dma_start(bs1[:, :], a["L0_ffn_bs1"]).then_inc(b_loaded, 16)
            sp.dma_start(bs2[:, :], a["L0_ffn_bs2"].partition_broadcast(PT)).then_inc(b_loaded, 16)
            sp.wait_ge(made, 4)
            sp.dma_start(r.token_of.rearrange("(p f) o -> p (f o)", p=128), zero_i[:, :]).then_inc(cleared, 16)
            sp.dma_start(r.y_rows[MORE_FROM:ROWS, :].rearrange("(p i) d -> p i d", p=128),
                         zero_f[:, :].unsqueeze(1).to_broadcast([128, (ROWS - MORE_FROM) // 128, D])).then_inc(saved, 16)
            for t in range(NT):
                sp.wait_ge(ln.h_ready, t + 1)
                sp.dma_start(r.h_rows[t * PT:(t + 1) * PT, :], H[:, t, :]).then_inc(saved, 16)
            sp.wait_ge(saved, 16 * (NT + 1))
            sp.wait_ge(cleared, 16)

        @block.gpsimd
        def _(pool):
            sems.clear(pool)
            small = dict(allow_small_or_imprecise_dtypes=True)
            nc.gpsimd.memset(every[:, :], 1.0).then_inc(made, 1)
            nc.gpsimd.memset(zero_i[:, :], 0).then_inc(made, 1)
            nc.gpsimd.memset(zero_f[:, :], 0.0).then_inc(made, 1)
            nc.gpsimd.memset(ones16[:, :], 1.0).then_inc(made, 1)
            nc.gpsimd.iota(r.token[:, :], [[PT, NT]], base=0, channel_multiplier=1).then_inc(made, 1)
            nc.gpsimd.iota(token_f[:, :], [[PT, NT]], base=0, channel_multiplier=1, **small).then_inc(made, 1)
            nc.gpsimd.iota(iota_rank[:, :], [[1, FIRST_ROWS]], base=1, channel_multiplier=0, **small).then_inc(made, 1)
            nc.gpsimd.memset(zero16[:, :], 0.0).then_inc(made, 1)
            nc.gpsimd.iota(falling[:, :, :], [[0, NT * NB], [-1, NE]], base=NE, channel_multiplier=0, **small).then_inc(made, 1)
            nc.gpsimd.iota(bounds[:, :, :], [[0, NX], [MORE_ROWS, ROUNDS]], base=FIRST_ROWS, channel_multiplier=0, **small).then_inc(made, 1)
            nc.gpsimd.iota(nth_round[:, :, :, :], [[0, NB], [1, NB * ROUNDS], [0, NE]], base=0, channel_multiplier=0, **small).then_inc(made, 1)
            nc.gpsimd.iota(row0[:, :, :], [[0, NT], [FIRST_ROWS, NX]], base=-1, channel_multiplier=0, **small).then_inc(made, 1)
            pool.wait_ge(made, 2)
            nc.gpsimd.affine_select(out=upto[:, :], in_=every[:, :], compare_op=ALU.is_ge, fill=0.0,
                                    base=0, pattern=[[1, PT]], channel_multiplier=-1).then_inc(made, 1)
            pool.wait_ge(b_loaded, 16 * (NB + 2))
            pool.wait_ge(ln.h_ready, NT)
            pool.wait_ge(whi_ready, 2)
            nc.gpsimd.tensor_tensor(s_lo[:, :], s_raw[:, :], s_hi[:, :].bitcast(F32), ALU.subtract).then_inc(slo_ready, 1)
            for t in range(NT):
                nc.gpsimd.tensor_tensor(X[:, t, :], X[:, t, :], bs2[:, :], ALU.add).then_inc(biased, 1)
            for u, (m, c) in enumerate(UNITS):
                c0, c1 = CHUNKS[c]
                pool.wait_ge(ghi_ready, u + 1)
                nc.gpsimd.tensor_tensor(gT_lo[:, m, c0:c1], act1[u % 2][:, 0:c1 - c0], gT_hi[:, m, c0:c1].bitcast(F32),
                                        ALU.subtract).then_inc(glo_ready, 1)
        @block.scalar
        def _(act):
            ln.scalar(act)
            act.wait_ge(w_loaded, 64)
            nc.scalar.activation(wr_hi[:, :, :], wr_raw[:, :, :], ACT.Copy).then_inc(whi_ready, 1)
            nc.scalar.activation(s_hi[:, :], s_raw[:, :], ACT.Copy).then_inc(whi_ready, 1)
            for c, (c0, c1) in enumerate(CHUNKS):
                act.wait_ge(logitT_done, c + 1)
                nc.scalar.activation(logit_T[:, c0:c1], ps_logit_T[c][0:NX, 0:c1 - c0], ACT.Copy).then_inc(logitT_ready, 1)
            act.wait_ge(shifted, 1)
            nc.scalar.activation(prob[:, :, :], logit[:, :, :], ACT.Exp).then_inc(exped, 1)
            act.wait_ge(b_loaded, 64)
            for u, (m, c) in enumerate(UNITS):
                c0, c1 = CHUNKS[c]
                act.wait_ge(up_done, u + 1)
                if u >= 2:
                    act.wait_ge(glo_ready, u - 1)
                nc.scalar.activation(act1[u % 2][:, 0:c1 - c0], ps_up[u % 2][:, 0:c1 - c0], ACT.Gelu,
                                     bias=bs1[:, m:m + 1]).then_inc(act_ready, 1)
                act.wait_ge(act_ready, u + 1)
                nc.scalar.activation(gT_hi[:, m, c0:c1], act1[u % 2][:, 0:c1 - c0], ACT.Copy).then_inc(ghi_ready, 1)

        @block.vector
        def _(dve):
            link = chained(dve, step)
            ln.vector(dve, link, measured=True)
            dve.wait_ge(whi_ready, 1)
            nc.vector.tensor_tensor(wr_lo[:, :, :], wr_raw[:, :, :], wr_hi[:, :, :].bitcast(F32), ALU.subtract).then_inc(wlo_ready, 1)

            def banked(t):
                return t[:, :, :].rearrange("p t (b e) -> p (t b) e", b=NB)

            def spread(t):
                return t[:, :].unsqueeze(2).to_broadcast([PT, NT * NB, NE])

            dve.wait_ge(logits_done, 1)
            dve.wait_ge(b_loaded, 64)
            dve.wait_ge(made, 13)
            link(nc.vector.tensor_tensor(logit[:, :, :], ps_logit[:, :, :],
                                         br[:, :].unsqueeze(1).to_broadcast([PT, NT, NX]), ALU.add))
            link(nc.vector.tensor_reduce(peak[:, :], banked(logit), AX.X, ALU.max))
            nc.vector.tensor_tensor(banked(logit), banked(logit), spread(peak), ALU.subtract).then_inc(shifted, 1)
            dve.wait_ge(shifted, 1)
            link(nc.vector.scalar_tensor_tensor(banked(work), banked(logit), 0.0, falling[:, :, :], ALU.is_ge, ALU.mult))
            link(nc.vector.tensor_reduce(peak[:, :], banked(work), AX.X, ALU.max))
            link(nc.vector.tensor_tensor(banked(onehot), banked(work), spread(peak), ALU.is_equal))
            nc.vector.tensor_copy(onehot16[:, :, :], onehot[:, :, :]).then_inc(onehot_ready, 1)
            dve.wait_ge(exped, 1)
            link(nc.vector.tensor_reduce(peak[:, :], banked(prob), AX.X, ALU.add))
            link(nc.vector.reciprocal(r.gate[:, :, :].rearrange("p t b -> p (t b)"), peak[:, :]))
            dve.wait_ge(ranked, 1)
            upto_now = ps_rank[:, 0:NT * NX].rearrange("p (t e) -> p t e", e=NX)
            link(nc.vector.tensor_tensor(work[:, :, :], upto_now, onehot[:, :, :], ALU.mult))
            link(nc.vector.tensor_reduce(rank[:, :], banked(work), AX.X, ALU.add))
            link(nc.vector.tensor_tensor(token16[:, :, :], onehot[:, :, :], token_f[:, :].unsqueeze(2).to_broadcast([PT, NT, NX]), ALU.mult))
            for n, (b, t) in enumerate(RANKED):
                if n >= RING:
                    dve.wait_ge(rank1h_used, n - RING + 1)
                nc.vector.tensor_scalar(rank1h[:, n % RING, :], iota_rank[:, :], rank[:, t * NB + b:t * NB + b + 1], None,
                                        ALU.is_equal).then_inc(rank1h_ready, 1)
            total = ps_rank[:, NT * NX:(NT + 1) * NX]
            link(nc.vector.tensor_tensor(kth[:, :, :], total.unsqueeze(2).to_broadcast([PT, NX, ROUNDS]), bounds[:, :, :], ALU.is_gt))
            link(nc.vector.tensor_reduce(more[:, :], kth[:, :, :], AX.X, ALU.add))
            link(nc.vector.tensor_tensor_scan(ended[:, :], ones16[:, :], more[:, :], 0.0, ALU.mult, ALU.add))
            link(nc.vector.tensor_tensor(before[:, :], ended[:, :], more[:, :], ALU.subtract))
            link(nc.vector.tensor_scalar(before[:, :], before[:, :], float(MORE_ROWS), float(MORE_FROM - FIRST_ROWS - 1),
                                         ALU.mult, ALU.add))
            link(nc.vector.tensor_tensor(jump[:, :], before[:, :], row0[:, 0, :], ALU.subtract))
            link(nc.vector.tensor_scalar(work[:, :, :], upto_now, float(FIRST_ROWS), None, ALU.is_gt))
            link(nc.vector.tensor_tensor(work[:, :, :], work[:, :, :], jump[:, :].unsqueeze(1).to_broadcast([PT, NT, NX]), ALU.mult))
            link(nc.vector.tensor_tensor(work[:, :, :], work[:, :, :], upto_now, ALU.add))
            link(nc.vector.tensor_tensor(work[:, :, :], work[:, :, :], row0[:, :, :], ALU.add))
            link(nc.vector.tensor_tensor(work[:, :, :], work[:, :, :], onehot[:, :, :], ALU.mult))
            link(nc.vector.tensor_reduce(slot_f[:, :], banked(work), AX.X, ALU.add))
            nc.vector.tensor_copy(r.slot[:, :, :].rearrange("p t b -> p (t b)"), slot_f[:, :])
            link(nc.vector.tensor_tensor(had[:, :, :, :], ended[0:1, :].rearrange("o (b e) -> o b e", b=NB).unsqueeze(2).to_broadcast([1, NB, NB * ROUNDS, NE]),
                                         nth_round[:, :, :, :], ALU.is_le))
            link(nc.vector.tensor_reduce(had_n[:, :, :], had[:, :, :, :], AX.X, ALU.add))
            nc.vector.tensor_copy(r.expert_of[:, :], had_n[:, :, :].rearrange("o b n -> o (b n)"))
            link(nc.vector.tensor_reduce(bank_more[:, :], more[0:1, :].rearrange("o (b e) -> o b e", b=NB), AX.X, ALU.add))
            link(nc.vector.tensor_copy(r.rounds[:, :], bank_more[:, :]))
            dve.wait_ge(idx_done, 1)
            nc.vector.tensor_copy(r.idx[:, :], ps_idx[:, 0, 0:ST * NX])
            for t in range(NT):
                dve.wait_ge(down_done, t + 1)
                if t == 0:
                    dve.wait_ge(biased, NT)
                nc.vector.tensor_tensor(X[:, t, :], X[:, t, :], ps_down[t % 2][:, :], ALU.add).then_inc(y_ready, 1)

        @block.tensor
        def _(pe):
            ln.tensor(pe)
            pe.wait_ge(wlo_ready, 1)
            pe.wait_ge(ln.lo_ready, NT)
            for c, (c0, c1) in enumerate(CHUNKS):
                for k in range(KD):
                    last = three(nc, ps_logit_T[c][0:NX, 0:c1 - c0], wr_hi[:, k, :], wr_lo[:, k, :], hT_hi[:, k, c0:c1], hT_lo[:, k, c0:c1],
                                 k == 0, k == KD - 1)
                last.then_inc(logitT_done, 1)
            pe.wait_ge(logitT_ready, len(CHUNKS))
            for t in range(NT):
                last = nc.tensor.transpose(ps_logit[:, t, :], logit_T[:, t * PT:(t + 1) * PT], ident[0:NX, 0:NX])
            last.then_inc(logits_done, 1)
            for u, (m, c) in enumerate(UNITS):
                c0, c1 = CHUNKS[c]
                if u == 0:
                    pe.wait_ge(slo_ready, 1)
                if u >= 2:
                    pe.wait_ge(act_ready, u - 1)
                for k in range(KD):
                    ms = slice(m * 128, (m + 1) * 128)
                    last = three(nc, ps_up[u % 2][:, 0:c1 - c0], w1[0][:, k, ms], w1[1][:, k, ms],
                                 hT_hi[:, k, c0:c1], hT_lo[:, k, c0:c1], k == 0, k == KD - 1)
                last.then_inc(up_done, 1)
                if u == 1:
                    pe.wait_ge(onehot_ready, 1)
                    pe.wait_ge(made, 13)
                    for t in range(NT + 1):
                        for q in range(min(t + 1, NT)):
                            lhs = upto if q == t else every
                            last = nc.tensor.matmul(ps_rank[:, t * NX:(t + 1) * NX], lhs[:, :], onehot16[:, q, :],
                                                    start=(q == 0), stop=(q == min(t, NT - 1)))
                    last.then_inc(ranked, 1)
                if u == 3:
                    nc.tensor.matmul(ps_idx[:, 0, 0:ST * NX], zero16[:, :], zero16[:, 0:ST * NX], start=True, stop=False,
                                     skip_group_check=True)
                    for n, (b, t) in enumerate(RANKED):
                        pe.wait_ge(rank1h_ready, n + 1)
                        for h in range(ST):
                            cols = slice(h * NX + b * NE, h * NX + (b + 1) * NE)
                            last = nc.tensor.matmul(ps_idx[:, 0, cols], rank1h[:, n % RING, h * 128:(h + 1) * 128],
                                                    token16[:, t, b * NE:(b + 1) * NE], start=False, stop=False, skip_group_check=True)
                        last.then_inc(rank1h_used, 1)
                    nc.tensor.matmul(ps_idx[:, 0, 0:ST * NX], zero16[:, :], zero16[:, 0:ST * NX], start=False, stop=True,
                                     skip_group_check=True).then_inc(idx_done, 1)
            pe.wait_ge(glo_ready, len(UNITS))
            for t in range(NT):
                tok = slice(t * PT, (t + 1) * PT)
                if t >= 2:
                    pe.wait_ge(y_ready, t - 1)
                for k in range(KF):
                    last = three(nc, ps_down[t % 2][:, :], gT_hi[:, k, tok], gT_lo[:, k, tok], w2[0][:, k, :], w2[1][:, k, :],
                                 k == 0, k == KF - 1)
                last.then_inc(down_done, 1)


def expert_weights(a, x):
    bank, e = BANKS[x // NE], x % NE
    return (a[f"L0_ffn_W1_{bank}"][e].rearrange("(k p) f -> p k f", p=128),
            a[f"L0_ffn_W2_{bank}"][e].rearrange("(k p) f -> p k f", p=128), a[f"L0_ffn_b2_{bank}"][e])


def routed_experts(nc, sems, a, ident, r):
    ST = FIRST_ROWS // 128
    sems.next_phase()
    with ExitStack() as ctx:
        def sb(name, shape, dt=F32):
            return ctx.enter_context(nc.sbuf_tensor(name, shape, dt))

        def pb(name, shape, dt=F32):
            return ctx.enter_context(nc.psum_tensor(name, shape, dt))

        def sem(name):
            return sems.new(ctx, "e_" + name)

        UP, DOWN = 0, 1
        raw = [[sb(f"e_raw{m}{i}", [128, 1024]) for i in range(2)] for m in (UP, DOWN)]
        whi = [[sb(f"e_whi{m}{i}", [128, 1024], F32R) for i in range(2)] for m in (UP, DOWN)]
        wlo = [[sb(f"e_wlo{m}{i}", [128, 1024], F32R) for i in range(2)] for m in (UP, DOWN)]
        b1 = sb("e_b1", [128, NX, KF])
        b2 = [sb(f"e_b2_{i}", [128, D]) for i in range(2)]
        rows = [sb(f"e_rows{i}", [128, ST, D]) for i in range(2)]
        xT_hi = [sb(f"e_xT_hi{i}", [128, KD, FIRST_ROWS], F32R) for i in range(2)]
        xT_lo = [sb(f"e_xT_lo{i}", [128, KD, FIRST_ROWS], F32R) for i in range(2)]
        g = sb("e_g", [128, KF, FIRST_ROWS])
        g_hi = [sb(f"e_g_hi{i}", [128, KF, FIRST_ROWS], F32R) for i in range(2)]
        g_lo = [sb(f"e_g_lo{i}", [128, KF, FIRST_ROWS], F32R) for i in range(2)]
        y = [sb(f"e_y{i}", [128, D]) for i in range(ST)]
        ps_turn = [pb(f"e_turn{s}", [128, KD, 128]) for s in range(ST)]
        ps_up = [pb(f"e_up{i}", [128, KF, FIRST_ROWS]) for i in range(2)]
        ps_down = [pb(f"e_down{s}", [128, D]) for s in range(ST)]
        b1_loaded, scattered = sem("b1_loaded"), sem("scattered")
        w_loaded = [[sem(f"w_loaded{m}{i}") for i in range(2)] for m in (UP, DOWN)]
        b2_loaded = [sem(f"b2_loaded{i}") for i in range(2)]
        gathered = [sem(f"gathered{i}") for i in range(2 * ST)]
        whi_ready, wlo_ready = ([sem(f"{n}{m}") for m in (UP, DOWN)] for n in ("whi_ready", "wlo_ready"))
        turned, xhi_ready, xlo_ready = sem("turned"), sem("xhi_ready"), sem("xlo_ready")
        up_done, g_ready, ghi_ready, glo_ready = sem("up_done"), sem("g_ready"), sem("ghi_ready"), sem("glo_ready")
        down_done, y_ready = sem("down_done"), sem("y_ready")
        y_stored = [sem(f"y_stored{s}") for s in range(ST)]
        block = ctx.enter_context(nc.Block())

        def as_lhs(t, m, i):
            return t[m][i][:, :].rearrange("p (k f) -> p k f", k=(KD, KF)[m])


        @block.sync
        def _(sp):
            def load_w(x, m):
                if x >= NX:
                    return
                if x >= 2:
                    sp.wait_ge(whi_ready[m], x - 1)
                    sp.wait_ge(wlo_ready[m], x - 1)
                sp.dma_start(as_lhs(raw, m, x % 2), expert_weights(a, x)[m]).then_inc(w_loaded[m][x % 2], 16)

            def load_b2(x):
                if x >= NX:
                    return
                if x >= 2:
                    sp.wait_ge(y_ready, ST * (x - 1))
                sp.dma_start(b2[x % 2][:, :], expert_weights(a, x)[2].partition_broadcast(128)).then_inc(b2_loaded[x % 2], 16)

            load_w(0, UP)
            load_w(1, UP)
            load_w(0, DOWN)
            for b, bank in enumerate(BANKS):
                sp.dma_start(b1[:, b * NE:(b + 1) * NE, :], a[f"L0_ffn_b1_{bank}"]).then_inc(b1_loaded, 16)
            load_w(1, DOWN)
            load_b2(0)
            load_b2(1)
            load_w(2, UP)
            for x in range(NX):
                load_w(x + 3, UP)
                load_w(x + 2, DOWN)
                for s in range(ST):
                    sp.wait_ge(y_ready, x * ST + s + 1)
                    row = x * FIRST_ROWS + s * 128
                    sp.dma_start(r.y_rows[row:row + 128, :], y[s][:, :]).then_inc(y_stored[s], 16)
                load_b2(x + 2)
            for s in range(ST):
                sp.wait_ge(y_stored[s], 16 * NX)

        @block.gpsimd
        def _(pool):
            for x in range(NX):
                for s in range(ST):
                    if x >= 2:
                        pool.wait_ge(turned, ST * (x - 2) + s + 1)
                    nc.gpsimd.indirect_dma_start(
                        out=rows[x % 2][:, s, :], out_offset=None, in_=r.h_rows,
                        in_offset=bass.IndirectOffsetOnAxis(ap=r.idx[:, s * NX + x:s * NX + x + 1], axis=0)).then_inc(gathered[(x % 2) * ST + s], 16)
                if x == 1:
                    sems.clear(pool)
                if 2 < x < NT + 3:
                    t = x - 3
                    for b in range(NB):
                        nc.gpsimd.indirect_dma_start(
                            out=r.token_of, out_offset=bass.IndirectOffsetOnAxis(ap=r.slot[:, t, b:b + 1], axis=0),
                            in_=r.token[:, t:t + 1], in_offset=None).then_inc(scattered, 16)
            pool.wait_ge(scattered, 16 * NT * NB)

        @block.scalar
        def _(act):
            def split_w(x, m):
                act.wait_ge(w_loaded[m][x % 2], 16 * (x // 2 + 1))
                if x >= 2 and m == UP:
                    act.wait_ge(up_done, x - 1)
                elif x >= 2:
                    act.wait_ge(down_done, ST * (x - 1))
                nc.scalar.activation(whi[m][x % 2][:, :], raw[m][x % 2][:, :], ACT.Copy).then_inc(whi_ready[m], 1)

            def split_x(x):
                if x >= 2:
                    act.wait_ge(up_done, x - 1)
                for s in range(ST):
                    act.wait_ge(turned, ST * x + s + 1)
                    nc.scalar.activation(xT_hi[x % 2][:, :, s * 128:(s + 1) * 128], ps_turn[s][:, :, :], ACT.Copy).then_inc(xhi_ready, 1)

            def activate(x):
                act.wait_ge(up_done, x + 1)
                if x:
                    act.wait_ge(glo_ready, x)
                for m in range(KF):
                    nc.scalar.activation(g[:, m, :], ps_up[x % 2][:, m, :], ACT.Gelu, bias=b1[:, x, m:m + 1]).then_inc(g_ready, 1)
                act.wait_ge(g_ready, KF * (x + 1))
                if x >= 2:
                    act.wait_ge(down_done, ST * (x - 1))
                nc.scalar.activation(g_hi[x % 2][:, :, :], g[:, :, :], ACT.Copy).then_inc(ghi_ready, 1)

            split_w(0, UP)
            act.wait_ge(b1_loaded, 16 * NB)
            for x in range(-2, NX):
                if x + 2 < NX:
                    split_x(x + 2)
                    if x + 2 > 0:
                        split_w(x + 2, UP)
                if 0 <= x + 1 < NX:
                    split_w(x + 1, DOWN)
                    activate(x + 1)

        @block.vector
        def _(dve):
            def split_w(x, m):
                dve.wait_ge(whi_ready[m], x + 1)
                nc.vector.tensor_tensor(wlo[m][x % 2][:, :], raw[m][x % 2][:, :], whi[m][x % 2][:, :].bitcast(F32),
                                        ALU.subtract).then_inc(wlo_ready[m], 1)

            def split_x(x):
                for s in range(ST):
                    dve.wait_ge(xhi_ready, ST * x + s + 1)
                    cols = slice(s * 128, (s + 1) * 128)
                    nc.vector.tensor_tensor(xT_lo[x % 2][:, :, cols], ps_turn[s][:, :, :], xT_hi[x % 2][:, :, cols].bitcast(F32),
                                            ALU.subtract).then_inc(xlo_ready, 1)

            split_w(0, UP)
            for x in range(-2, NX):
                if x + 2 < NX:
                    split_x(x + 2)
                    if x + 2 > 0:
                        split_w(x + 2, UP)
                if 0 <= x + 1 < NX:
                    split_w(x + 1, DOWN)
                    dve.wait_ge(ghi_ready, x + 2)
                    i = (x + 1) % 2
                    nc.vector.tensor_tensor(g_lo[i][:, :, :], g[:, :, :], g_hi[i][:, :, :].bitcast(F32), ALU.subtract).then_inc(glo_ready, 1)
                if x >= 0:
                    dve.wait_ge(b2_loaded[x % 2], 16 * (x // 2 + 1))
                    for s in range(ST):
                        dve.wait_ge(down_done, ST * x + s + 1)
                        if x:
                            dve.wait_ge(y_stored[s], 16 * x)
                        nc.vector.tensor_tensor(y[s][:, :], ps_down[s][:, :], b2[x % 2][:, :], ALU.add).then_inc(y_ready, 1)

        @block.tensor
        def _(pe):
            def turn(x):
                for s in range(ST):
                    pe.wait_ge(gathered[(x % 2) * ST + s], 16 * (x // 2 + 1))
                    if x:
                        pe.wait_ge(xlo_ready, ST * (x - 1) + s + 1)
                    for k in range(KD):
                        last = nc.tensor.transpose(ps_turn[s][:, k, :], rows[x % 2][:, s, k * 128:(k + 1) * 128], ident[:, :])
                    last.then_inc(turned, 1)

            def up(x):
                u_hi, u_lo, i = as_lhs(whi, UP, x % 2), as_lhs(wlo, UP, x % 2), x % 2
                pe.wait_ge(xlo_ready, ST * (x + 1))
                pe.wait_ge(wlo_ready[UP], x + 1)
                if x >= 2:
                    pe.wait_ge(g_ready, KF * (x - 1))
                for m in range(KF):
                    ms = slice(m * 128, (m + 1) * 128)
                    for k in range(KD):
                        last = three(nc, ps_up[i][:, m, :], u_hi[:, k, ms], u_lo[:, k, ms], xT_hi[i][:, k, :], xT_lo[i][:, k, :],
                                     k == 0, k == KD - 1)
                last.then_inc(up_done, 1)

            def down(x):
                d_hi, d_lo, i = as_lhs(whi, DOWN, x % 2), as_lhs(wlo, DOWN, x % 2), x % 2
                pe.wait_ge(glo_ready, x + 1)
                pe.wait_ge(wlo_ready[DOWN], x + 1)
                for s in range(ST):
                    if x:
                        pe.wait_ge(y_ready, ST * (x - 1) + s + 1)
                    for k in range(KF):
                        cols = slice(s * 128, (s + 1) * 128)
                        last = three(nc, ps_down[s][:, :], g_hi[i][:, k, cols], g_lo[i][:, k, cols], d_hi[:, k, :], d_lo[:, k, :],
                                     k == 0, k == KF - 1)
                    last.then_inc(down_done, 1)

            for x in range(-2, NX):
                if x + 2 < NX:
                    turn(x + 2)
                if 0 <= x + 1 < NX:
                    up(x + 1)
                if x >= 0:
                    down(x)


def overfull_experts(nc, sems, a, ident, r):
    sems.next_phase()
    with ExitStack() as ctx:
        def sb(name, shape, dt=F32):
            return ctx.enter_context(nc.sbuf_tensor(name, shape, dt))

        def pb(name, shape, dt=F32):
            return ctx.enter_context(nc.psum_tensor(name, shape, dt))

        def sem(name):
            return sems.new(ctx, "o_" + name)

        raw = sb("o_raw", [128, 2048])
        whi = sb("o_whi", [128, 2048], F32R)
        wlo = sb("o_wlo", [128, 2048], F32R)
        b1 = sb("o_b1", [128, KF])
        b2 = sb("o_b2", [128, D])
        idx = sb("o_idx", [128, 1], I32)
        rows = sb("o_rows", [128, D])
        xT_hi = sb("o_xT_hi", [128, KD, MORE_ROWS], F32R)
        xT_lo = sb("o_xT_lo", [128, KD, MORE_ROWS], F32R)
        g = sb("o_g", [128, KF, MORE_ROWS])
        g_hi = sb("o_g_hi", [128, KF, MORE_ROWS], F32R)
        g_lo = sb("o_g_lo", [128, KF, MORE_ROWS], F32R)
        y = sb("o_y", [128, D])
        ps_turn = pb("o_turn", [128, KD, 128])
        ps_up = pb("o_up", [128, KF, 256])
        ps_down = pb("o_down", [128, D])
        w_loaded, whi_ready, w_ready = sem("w_loaded"), sem("whi_ready"), sem("w_ready")
        begun = sem("begun")
        idx_loaded, gathered, turned = sem("idx_loaded"), sem("gathered"), sem("turned")
        xhi_ready, x_ready, up_done, g_made = sem("xhi_ready"), sem("x_ready"), sem("up_done"), sem("g_made")
        ghi_ready, g_ready, down_done, y_ready, y_stored, round_over = (
            sem("ghi_ready"), sem("g_ready"), sem("down_done"), sem("y_ready"), sem("y_stored"), sem("round_over"))
        block = ctx.enter_context(nc.Block())
        up_hi, down_hi = (whi[:, 0:1024].rearrange("p (k f) -> p k f", k=KD), whi[:, 1024:2048].rearrange("p (k f) -> p k f", k=KF))
        up_lo, down_lo = (wlo[:, 0:1024].rearrange("p (k f) -> p k f", k=KD), wlo[:, 1024:2048].rearrange("p (k f) -> p k f", k=KF))

        def overfull(eng, tag, at_round):
            rounds = eng.alloc_register(f"{tag}_rounds")
            eng.reg_mov(rounds, 1)
            for b in range(NB):
                count = eng.value_load(r.rounds[0:1, b:b + 1], min_val=0, max_val=ROUNDS)
                with eng.If(count > 0):
                    with eng.Fori(0, count):
                        at_round(eng.snap(rounds, min_val=1, max_val=NB * ROUNDS), b)
                        eng.reg_add(rounds, rounds, 1)

        @block.sync
        def _(sp):
            sp.sem_inc(round_over, 1)

            def at_round(nth, b):
                bank, row = BANKS[b], nth * MORE_ROWS + (MORE_FROM - MORE_ROWS)
                e = sp.value_load(r.expert_of[0:1, bass.DynSlice(nth + (b * NB * ROUNDS - 1), 1)], min_val=0, max_val=NE - 1)
                one = bass.DynSlice(e, 1)
                sp.wait_ge(round_over, nth)
                sp.dma_start(idx[:, :], r.token_of[bass.DynSlice(row, MORE_ROWS), :]).then_inc(idx_loaded, 16)
                sp.dma_start(raw[:, 0:1024].rearrange("p (k f) -> p k f", k=KD),
                             a[f"L0_ffn_W1_{bank}"][one].rearrange("o (k p) f -> p (o k) f", p=128)).then_inc(w_loaded, 16)
                sp.dma_start(raw[:, 1024:2048].rearrange("p (k f) -> p k f", k=KF),
                             a[f"L0_ffn_W2_{bank}"][one].rearrange("o (k p) f -> p (o k) f", p=128)).then_inc(w_loaded, 16)
                sp.dma_start(b1[:, :], a[f"L0_ffn_b1_{bank}"][:, one, :].rearrange("p o m -> p (o m)")).then_inc(w_loaded, 16)
                sp.dma_start(b2[:, :], a[f"L0_ffn_b2_{bank}"][one].rearrange("o d -> (o d)").partition_broadcast(128)).then_inc(w_loaded, 16)
                sp.wait_ge(y_ready, nth)
                sp.dma_start(r.y_rows[bass.DynSlice(row, MORE_ROWS), :], y[:, :]).then_inc(y_stored, 16)
                sp.wait_ge(y_stored, nth * 16)
                sp.sem_inc(round_over, 1)

            overfull(sp, "sp", at_round)

        @block.gpsimd
        def _(pool):
            def at_round(nth, b):
                pool.wait_ge(idx_loaded, nth * 16)
                pool.sem_inc(begun, 1)
                nc.gpsimd.indirect_dma_start(out=rows[:, :], out_offset=None, in_=r.h_rows,
                                             in_offset=bass.IndirectOffsetOnAxis(ap=idx[:, 0:1], axis=0)).then_inc(gathered, 16)

            overfull(pool, "pool", at_round)
            sems.clear(pool)

        @block.scalar
        def _(act):
            def at_round(nth, b):
                act.wait_ge(w_loaded, nth * 64)
                nc.scalar.activation(whi[:, :], raw[:, :], ACT.Copy).then_inc(whi_ready, 1)
                act.wait_ge(turned, nth)
                nc.scalar.activation(xT_hi[:, :, :], ps_turn[:, :, :], ACT.Copy).then_inc(xhi_ready, 1)
                act.wait_ge(up_done, nth)
                for m in range(KF):
                    last = nc.scalar.activation(g[:, m, :], ps_up[:, m, 0:MORE_ROWS], ACT.Gelu, bias=b1[:, m:m + 1])
                last.then_inc(g_made, 1)
                act.wait_ge(g_made, nth)
                nc.scalar.activation(g_hi[:, :, :], g[:, :, :], ACT.Copy).then_inc(ghi_ready, 1)

            overfull(act, "act", at_round)

        @block.vector
        def _(dve):
            def at_round(nth, b):
                dve.wait_ge(whi_ready, nth)
                nc.vector.tensor_tensor(wlo[:, :], raw[:, :], whi[:, :].bitcast(F32), ALU.subtract).then_inc(w_ready, 1)
                dve.wait_ge(xhi_ready, nth)
                nc.vector.tensor_tensor(xT_lo[:, :, :], ps_turn[:, :, :], xT_hi[:, :, :].bitcast(F32), ALU.subtract).then_inc(x_ready, 1)
                dve.wait_ge(ghi_ready, nth)
                nc.vector.tensor_tensor(g_lo[:, :, :], g[:, :, :], g_hi[:, :, :].bitcast(F32), ALU.subtract).then_inc(g_ready, 1)
                dve.wait_ge(down_done, nth)
                nc.vector.tensor_tensor(y[:, :], ps_down[:, :], b2[:, :], ALU.add).then_inc(y_ready, 1)

            overfull(dve, "dve", at_round)

        @block.tensor
        def _(pe):
            def at_round(nth, b):
                pe.wait_ge(gathered, nth * 16)
                pe.sem_inc(begun, 1)
                for k in range(KD):
                    last = nc.tensor.transpose(ps_turn[:, k, :], rows[:, k * 128:(k + 1) * 128], ident[:, :])
                last.then_inc(turned, 1)
                pe.wait_ge(w_ready, nth)
                pe.wait_ge(x_ready, nth)
                for m in range(KF):
                    for k in range(KD):
                        ms = slice(m * 128, (m + 1) * 128)
                        last = three(nc, ps_up[:, m, 0:MORE_ROWS], up_hi[:, k, ms], up_lo[:, k, ms],
                                     xT_hi[:, k, :], xT_lo[:, k, :], k == 0, k == KD - 1)
                last.then_inc(up_done, 1)
                pe.wait_ge(g_ready, nth)
                for k in range(KF):
                    last = three(nc, ps_down[:, :], g_hi[:, k, :], g_lo[:, k, :], down_hi[:, k, :], down_lo[:, k, :],
                                 k == 0, k == KF - 1)
                last.then_inc(down_done, 1)

            overfull(pe, "pe", at_round)


def combine(nc, sems, X, CT, ident, stats, r):
    NR = 6
    swaps = [(i, j, min(j + 4, NT)) for i in range(NT) for j in range(i + 1, NT, 4)]
    diagonal = [(j, min(j + 4, NT)) for j in range(0, NT, 4)]
    sems.next_phase()
    with ExitStack() as ctx:
        rows = [ctx.enter_context(nc.sbuf_tensor(f"c_rows{i}", [PT, D], F32)) for i in range(NR)]
        gathered = [sems.new(ctx, f"c_gathered{i}") for i in range(NR)]
        added = sems.new(ctx, "c_added")
        turned = sems.new(ctx, "c_turned")
        swapped = sems.new(ctx, "c_swapped")
        ps = [[ctx.enter_context(nc.psum_tensor(f"c_ps{n}{half}", [PT, 4, 128], F32)) for half in range(2)] for n in range(2)]
        block = ctx.enter_context(nc.Block())
        pairs = [(t, b) for t in range(NT) for b in range(NB)]

        @block.gpsimd
        def _(pool):
            for n, (t, b) in enumerate(pairs):
                if n == NR:
                    sems.clear(pool)
                if n >= NR:
                    pool.wait_ge(added, n - NR + 1)
                nc.gpsimd.indirect_dma_start(out=rows[n % NR][:, :], out_offset=None, in_=r.y_rows,
                                             in_offset=bass.IndirectOffsetOnAxis(ap=r.slot[:, t, b:b + 1], axis=0)).then_inc(gathered[n % NR], 16)

        @block.vector
        def _(dve):
            for n, (t, b) in enumerate(pairs):
                dve.wait_ge(gathered[n % NR], 16 * (n // NR + 1))
                if b:
                    dve.wait_ge(added, n)
                nc.vector.scalar_tensor_tensor(X[:, t, :], rows[n % NR][:, :], r.gate[:, t, b:b + 1], X[:, t, :],
                                               ALU.mult, ALU.add).then_inc(added, 1)
                if b == NB - 1:
                    dve.wait_ge(added, n + 1)
                    nc.vector.bn_stats(stats[:, t, :], X[:, t, :])

        def block_of(i, j):
            return CT[:, i, j * PT:(j + 1) * PT]

        @block.tensor
        def _(pe):
            for n, (i, j0, j1) in enumerate(swaps):
                if n >= 2:
                    pe.wait_ge(swapped, n - 1)
                for j in range(j0, j1):
                    nc.tensor.transpose(ps[n % 2][0][:, j - j0, 0:PT], block_of(i, j), ident[0:PT, 0:PT])
                for j in range(j0, j1):
                    last = nc.tensor.transpose(ps[n % 2][1][:, j - j0, 0:PT], block_of(j, i), ident[0:PT, 0:PT])
                last.then_inc(turned, 1)
            for m, (j0, j1) in enumerate(diagonal):
                n = len(swaps) + m
                pe.wait_ge(swapped, n - 1)
                for j in range(j0, j1):
                    last = nc.tensor.transpose(ps[n % 2][0][:, j - j0, 0:PT], block_of(j, j), ident[0:PT, 0:PT])
                last.then_inc(turned, 1)

        @block.scalar
        def _(act):
            for n, (i, j0, j1) in enumerate(swaps):
                act.wait_ge(turned, n + 1)
                nc.scalar.activation(CT[:, j0:j1, i * PT:(i + 1) * PT], ps[n % 2][0][:, 0:j1 - j0, 0:PT], ACT.Copy)
                nc.scalar.activation(CT[:, i, j0 * PT:j1 * PT].rearrange("p (j q) -> p j q", q=PT), ps[n % 2][1][:, 0:j1 - j0, 0:PT],
                                     ACT.Copy).then_inc(swapped, 1)
            for m, (j0, j1) in enumerate(diagonal):
                n = len(swaps) + m
                act.wait_ge(turned, n + 1)
                for j in range(j0, j1):
                    last = nc.scalar.activation(block_of(j, j), ps[n % 2][0][:, j - j0, 0:PT], ACT.Copy)
                last.then_inc(swapped, 1)


HEADS = 8
DH = FF // HEADS
TINY = 1.1754944e-38
HUGE = 3.4028235e38


def project_qkv(nc, sems, a, X, H, hT_hi, hT_lo, ident, eps_col, stats, V, r):
    sems.next_phase()
    with ExitStack() as ctx:
        def sb(name, shape, dt=F32):
            return ctx.enter_context(nc.sbuf_tensor(name, shape, dt))

        def pb(name, shape, dt=F32):
            return ctx.enter_context(nc.psum_tensor(name, shape, dt))

        def sem(name):
            return sems.new(ctx, "q_" + name)

        raw = [sb(f"q_raw{i}", [128, KD, FF]) for i in range(2)]
        whi = [sb(f"q_whi{i}", [128, KD, FF], F32R) for i in range(3)]
        wlo = [sb(f"q_wlo{i}", [128, KD, FF], F32R) for i in range(3)]
        bqk = sb("bqk", [128, 2, KF])
        bv = sb("bv", [PT, FF])
        full = sb("q_full", [128, N])
        hi = [sb(f"q_hi{i}", [128, N], F32R) for i in range(2)]
        lo = [sb(f"q_lo{i}", [128, N], F32R) for i in range(2)]
        ps_qk = [pb(f"ps_qk{i}", [128, 3, 512]) for i in range(2)]
        ps_turn = [pb(f"q_turn{i}", [128, 4, 128]) for i in range(2)]
        w_loaded, b_loaded = sem("w_loaded"), sem("b_loaded")
        whi_ready, wlo_ready, ones_made = sem("whi_ready"), sem("wlo_ready"), sem("ones_made")
        v_done, v_ready, qk_done, full_ready = sem("v_done"), sem("v_ready"), sem("qk_done"), sem("full_ready")
        hi_ready, lo_ready, stored, step = sem("hi_ready"), sem("lo_ready"), [sem(f"stored{i}") for i in range(2)], sem("step")
        ln = Norm(nc, sems, ctx, "ln3", X, H, hT_hi, hT_lo, ps_turn, ident, eps_col, stats)
        block = ctx.enter_context(nc.Block())

        @block.sync
        def _(sp):
            for i, name in enumerate("vqk"):
                if i >= 2:
                    sp.wait_ge(wlo_ready, i - 1)
                sp.dma_start(raw[i % 2][:, :, :], a[f"L1_gnn_W{name}"].rearrange("(k p) f -> p k f", p=128)).then_inc(w_loaded, 16)
                if i < 2:
                    sp.dma_start(bqk[:, i, :], a[f"L1_gnn_b{'qk'[i]}"]).then_inc(b_loaded, 16)
                sp.wait_ge(w_loaded, 16 * (i + 1))
            sp.dma_start(bv[:, :], a["L1_gnn_bv"].partition_broadcast(PT)).then_inc(b_loaded, 16)
            for u in range(2 * KF):
                q, m = u // KF, u % KF
                sp.wait_ge(hi_ready, u + 1)
                sp.dma_start(r.qk[2 * q, m * 128:(m + 1) * 128, :], hi[u % 2][:, :].bitcast(F32)).then_inc(stored[u % 2], 16)
                sp.wait_ge(lo_ready, u + 1)
                sp.dma_start(r.qk[2 * q + 1, m * 128:(m + 1) * 128, :], lo[u % 2][:, :].bitcast(F32)).then_inc(stored[u % 2], 16)
            for i in range(2):
                sp.wait_ge(stored[i], 32 * KF)

        @block.gpsimd
        def _(pool):
            sems.clear(pool)
            nc.gpsimd.memset(V[:, :, :, DH:64], 1.0).then_inc(ones_made, 1)
            pool.wait_ge(ones_made, 1)

        @block.scalar
        def _(act):
            ln.scalar(act)
            for i in range(3):
                act.wait_ge(w_loaded, 16 * (i + 1))
                nc.scalar.activation(whi[i][:, :, :], raw[i % 2][:, :, :], ACT.Copy).then_inc(whi_ready, 1)
            act.wait_ge(b_loaded, 48)
            for u in range(2 * KF):
                act.wait_ge(qk_done, u + 1)
                if u:
                    act.wait_ge(lo_ready, u)
                for c, (c0, c1) in enumerate(CHUNKS):
                    last = nc.scalar.activation(full[:, c0:c1], ps_qk[u % 2][:, c, 0:c1 - c0], ACT.Identity,
                                                bias=bqk[:, u // KF, u % KF:u % KF + 1])
                last.then_inc(full_ready, 1)

        @block.vector
        def _(dve):
            link = chained(dve, step)
            ln.vector(dve, link, measured=True)
            for i in range(3):
                dve.wait_ge(whi_ready, i + 1)
                nc.vector.tensor_tensor(wlo[i][:, :, :], raw[i % 2][:, :, :], whi[i][:, :, :].bitcast(F32), ALU.subtract).then_inc(wlo_ready, 1)
            for t in range(NT):
                last = nc.vector.tensor_tensor(X[:, t, :], X[:, t, :], H[:, t, :], ALU.add)
            link(last)
            dve.wait_ge(b_loaded, 48)
            for t in range(NT):
                dve.wait_ge(v_done, t + 1)
                nc.vector.tensor_tensor(V[:, t, :, 0:DH], ps_turn[t % 2][0:PT, 0:2, :].rearrange("p a (h d) -> p (a h) d", d=DH),
                                        bv[:, :].rearrange("p (h d) -> p h d", d=DH), ALU.add).then_inc(v_ready, 1)
            for u in range(2 * KF):
                dve.wait_ge(full_ready, u + 1)
                if u >= 2:
                    dve.wait_ge(stored[u % 2], 32)
                i = u % 2
                nc.vector.tensor_copy(hi[i][:, :], full[:, :]).then_inc(hi_ready, 1)
                dve.wait_ge(hi_ready, u + 1)
                nc.vector.tensor_tensor(lo[i][:, :], full[:, :], hi[i][:, :].bitcast(F32), ALU.subtract).then_inc(lo_ready, 1)

        @block.tensor
        def _(pe):
            ln.tensor(pe)
            pe.wait_ge(ln.lo_ready, NT)
            pe.wait_ge(wlo_ready, 1)
            for t in range(NT):
                tok = slice(t * PT, (t + 1) * PT)
                if t >= 2:
                    pe.wait_ge(v_ready, t - 1)
                out = ps_turn[t % 2][0:PT, 0:2, :].rearrange("p a f -> p (a f)")
                for k in range(KD):
                    last = three(nc, out, hT_hi[:, k, tok], hT_lo[:, k, tok], whi[0][:, k, :], wlo[0][:, k, :], k == 0, k == KD - 1)
                last.then_inc(v_done, 1)
            for u in range(2 * KF):
                q, m = u // KF, u % KF
                pe.wait_ge(wlo_ready, q + 2)
                if u >= 2:
                    pe.wait_ge(full_ready, u - 1)
                for c, (c0, c1) in enumerate(CHUNKS):
                    for k in range(KD):
                        ms = slice(m * 128, (m + 1) * 128)
                        last = three(nc, ps_qk[u % 2][:, c, 0:c1 - c0], whi[q + 1][:, k, ms], wlo[q + 1][:, k, ms],
                                     hT_hi[:, k, c0:c1], hT_lo[:, k, c0:c1], k == 0, k == KD - 1)
                last.then_inc(qk_done, 1)


def attention(nc, sems, oT_hi, oT_lo, CT, V, r):
    WIDTH = 418
    STARTS = (0, 418, N - 418)
    SKIP = (0, 0, 3 * 418 - N)
    units = [(h, s, c) for h in range(HEADS) for s in range(NT) for c in range(3)]
    NS, NP, LAG = 5, 4, 4
    PIECES = [(i * N // 5, (i + 1) * N // 5) for i in range(5)]
    HG = 128 // DH
    sems.next_phase()
    with ExitStack() as ctx:
        def sb(name, shape, dt=F32):
            return ctx.enter_context(nc.sbuf_tensor(name, shape, dt))

        def pb(name, shape, dt=F32):
            return ctx.enter_context(nc.psum_tensor(name, shape, dt))

        def sem(name):
            return sems.new(ctx, "a_" + name)

        q = [sb(f"a_q{i}", [3 * DH, N], F32R) for i in range(2)]
        k = [sb(f"a_k{i}", [3 * DH, N], F32R) for i in range(2)]
        e = [sb(f"a_e{i}", [PT, WIDTH]) for i in range(NP)]
        p = [sb(f"a_p{i}", [PT, WIDTH]) for i in range(NP)]
        num = sb("a_num", [128, N])
        den = sb("a_den", [128, N])
        ps_s = [pb(f"a_s{i}", [PT, 512]) for i in range(NS)]
        ps_o = [pb(f"a_o{i}", [64, 512]) for i in range(3)]
        loaded = [sem(f"loaded{i}") for i in range(2)]
        scored, exped, weighed = sem("scored"), sem("exped"), sem("weighed")
        summed_units = sem("summed_units")
        num_taken, den_taken, ratio_ready = sem("num_taken"), sem("den_taken"), sem("ratio_ready")
        step = sem("step")
        block = ctx.enter_context(nc.Block())

        @block.sync
        def _(sp):
            for h in range(HEADS):
                if h >= 2:
                    sp.wait_ge(scored, 3 * NT * (h - 1))
                rows = slice(h * DH, (h + 1) * DH)
                for j, (kq, kk) in enumerate(((0, 2), (1, 2), (0, 3))):
                    sp.dma_start(q[h % 2][j * DH:(j + 1) * DH, :].bitcast(F32), r.qk[kq, rows, :]).then_inc(loaded[h % 2], 16)
                    sp.dma_start(k[h % 2][j * DH:(j + 1) * DH, :].bitcast(F32), r.qk[kk, rows, :]).then_inc(loaded[h % 2], 16)

        @block.gpsimd
        def _(pool):
            sems.clear(pool)

        @block.scalar
        def _(act):
            def take_num(h, c):
                act.wait_ge(summed_units, (NT * (h + 1) - 1) * 3 + c + 1)
                if h == HG:
                    act.wait_ge(ratio_ready, len(PIECES))
                part = slice((h % HG) * DH, (h % HG + 1) * DH)
                nc.scalar.activation(num[part, STARTS[c] + SKIP[c]:STARTS[c] + WIDTH], ps_o[c][0:DH, SKIP[c]:WIDTH], ACT.Relu).then_inc(num_taken, 1)

            for u, (h, s, c) in enumerate(units):
                act.wait_ge(scored, u + 1)
                if u >= NP:
                    act.wait_ge(weighed, u - NP + 1)
                nc.scalar.activation(e[u % NP][:, :], ps_s[u % NS][:, 0:WIDTH], ACT.Exp, scale=DH ** -0.5).then_inc(exped, 1)
                if h and s == 0:
                    take_num(h - 1, c)
            for c in range(3):
                take_num(HEADS - 1, c)

        @block.vector
        def _(dve):
            link = chained(dve, step)

            def take_den(h, c):
                dve.wait_ge(summed_units, (NT * (h + 1) - 1) * 3 + c + 1)
                part = slice((h % HG) * DH, (h % HG + 1) * DH)
                nc.vector.tensor_scalar(den[part, STARTS[c] + SKIP[c]:STARTS[c] + WIDTH], ps_o[c][DH:2 * DH, SKIP[c]:WIDTH], TINY, None,
                                        ALU.max).then_inc(den_taken, 1)

            def divide(g, i):
                cols = slice(*PIECES[i])
                if i == 0:
                    dve.wait_ge(den_taken, 3 * HG * (g + 1))
                    dve.wait_ge(num_taken, 3 * HG * (g + 1))
                link(nc.vector.reciprocal(den[:, cols], den[:, cols]))
                link(nc.vector.tensor_tensor(num[:, cols], num[:, cols], den[:, cols], ALU.mult))
                link(nc.vector.tensor_copy(oT_hi[:, g, cols], num[:, cols]))
                nc.vector.tensor_tensor(oT_lo[:, g, cols], num[:, cols], oT_hi[:, g, cols].bitcast(F32), ALU.subtract).then_inc(ratio_ready, 1)

            for u, (h, s, c) in enumerate(units):
                dve.wait_ge(exped, u + 1)
                if u >= NP:
                    dve.wait_ge(summed_units, u - NP + 1)
                nc.vector.scalar_tensor_tensor(p[u % NP][:, :], e[u % NP][:, :], HUGE, CT[:, s, STARTS[c]:STARTS[c] + WIDTH],
                                               ALU.min, ALU.mult).then_inc(weighed, 1)
                if h and s == 0:
                    if h - 1 == HG:
                        dve.wait_ge(ratio_ready, len(PIECES))
                    take_den(h - 1, c)
                if h == HG and 1 <= s <= len(PIECES) and c == 0:
                    divide(0, s - 1)
            for c in range(3):
                take_den(HEADS - 1, c)
            for i in range(len(PIECES)):
                divide(1, i)
            dve.wait_ge(ratio_ready, 2 * len(PIECES))

        @block.tensor
        def _(pe):
            for v in range(len(units) + LAG):
                if v < len(units):
                    h, s, c = units[v]
                    if s == 0 and c == 0:
                        pe.wait_ge(loaded[h % 2], 96 * (h // 2 + 1))
                    if v >= NS:
                        pe.wait_ge(exped, v - NS + 1)
                    nc.tensor.matmul(ps_s[v % NS][:, 0:WIDTH], k[h % 2][:, s * PT:(s + 1) * PT],
                                     q[h % 2][:, STARTS[c]:STARTS[c] + WIDTH], start=True, stop=True).then_inc(scored, 1)
                if v >= LAG:
                    u = v - LAG
                    h, s, c = units[u]
                    pe.wait_ge(weighed, u + 1)
                    if h and s == 0:
                        pe.wait_ge(num_taken, 3 * (h - 1) + c + 1)
                        pe.wait_ge(den_taken, 3 * (h - 1) + c + 1)
                    nc.tensor.matmul(ps_o[c][:, 0:WIDTH], V[:, s, h, :], p[u % NP][:, :], start=(s == 0),
                                     stop=(s == NT - 1)).then_inc(summed_units, 1)


def attention_out(nc, sems, a, X, oT_hi, oT_lo, stats):
    UNITS = [(m, c) for m in range(KD) for c in range(len(CHUNKS))]
    sems.next_phase()
    with ExitStack() as ctx:
        def sb(name, shape, dt=F32):
            return ctx.enter_context(nc.sbuf_tensor(name, shape, dt))

        def pb(name, shape, dt=F32):
            return ctx.enter_context(nc.psum_tensor(name, shape, dt))

        def sem(name):
            return sems.new(ctx, "w_" + name)

        shapes = ([128, KF, D], [128, KD, D])
        raw = [sb(f"o2_raw{i}", shapes[i]) for i in range(2)]
        whi = [sb(f"o2_whi{i}", shapes[i], F32R) for i in range(2)]
        wlo = [sb(f"o2_wlo{i}", shapes[i], F32R) for i in range(2)]
        ba = sb("ba", [128, KD])
        bf = sb("bf", [PT, D])
        full = [sb(f"w_full{i}", [128, 512]) for i in range(2)]
        f_hi = sb("w_f_hi", [128, KD, N], F32R)
        f_lo = sb("w_f_lo", [128, KD, N], F32R)
        y = [sb(f"w_y{i}", [PT, D]) for i in range(2)]
        ps_f = [pb(f"w_f{i}", [128, 512]) for i in range(2)]
        ps_y = [pb(f"w_psy{i}", [PT, D]) for i in range(2)]
        w_loaded, b_loaded = [sem(f"w_loaded{i}") for i in range(2)], sem("b_loaded")
        whi_ready, wlo_ready = sem("whi_ready"), sem("wlo_ready")
        f_done, full_ready, fhi_ready, flo_ready = sem("f_done"), sem("full_ready"), sem("fhi_ready"), sem("flo_ready")
        y_done, y_ready, step = sem("y_done"), sem("y_ready"), sem("step")
        block = ctx.enter_context(nc.Block())

        @block.sync
        def _(sp):
            for i, name in enumerate("af"):
                sp.dma_start(raw[i][:, :, :], a[f"L1_gnn_W{name}"].rearrange("(k p) f -> p k f", p=128)).then_inc(w_loaded[i], 16)
            sp.dma_start(ba[:, :], a["L1_gnn_ba"]).then_inc(b_loaded, 16)
            sp.dma_start(bf[:, :], a["L1_gnn_bf"].partition_broadcast(PT)).then_inc(b_loaded, 16)

        @block.gpsimd
        def _(pool):
            sems.clear(pool)

        @block.scalar
        def _(act):
            for i in range(2):
                act.wait_ge(w_loaded[i], 16)
                nc.scalar.activation(whi[i][:, :, :], raw[i][:, :, :], ACT.Copy).then_inc(whi_ready, 1)
            act.wait_ge(b_loaded, 32)
            for u, (m, c) in enumerate(UNITS):
                w = CHUNKS[c][1] - CHUNKS[c][0]
                act.wait_ge(f_done, u + 1)
                if u >= 2:
                    act.wait_ge(flo_ready, u - 1)
                nc.scalar.activation(full[u % 2][:, 0:w], ps_f[u % 2][:, 0:w], ACT.Relu, bias=ba[:, m:m + 1]).then_inc(full_ready, 1)
                act.wait_ge(full_ready, u + 1)
                nc.scalar.activation(f_hi[:, m, CHUNKS[c][0]:CHUNKS[c][1]], full[u % 2][:, 0:w], ACT.Copy).then_inc(fhi_ready, 1)

        @block.vector
        def _(dve):
            link = chained(dve, step)
            for i in range(2):
                dve.wait_ge(whi_ready, i + 1)
                nc.vector.tensor_tensor(wlo[i][:, :, :], raw[i][:, :, :], whi[i][:, :, :].bitcast(F32), ALU.subtract).then_inc(wlo_ready, 1)
            for u, (m, c) in enumerate(UNITS):
                c0, c1 = CHUNKS[c]
                dve.wait_ge(fhi_ready, u + 1)
                nc.vector.tensor_tensor(f_lo[:, m, c0:c1], full[u % 2][:, 0:c1 - c0], f_hi[:, m, c0:c1].bitcast(F32),
                                        ALU.subtract).then_inc(flo_ready, 1)
            for t in range(NT):
                dve.wait_ge(y_done, t + 1)
                nc.vector.tensor_tensor(y[t % 2][:, :], ps_y[t % 2][:, :], bf[:, :], ALU.add).then_inc(y_ready, 1)
                dve.wait_ge(y_ready, t + 1)
                link(nc.vector.scalar_tensor_tensor(X[:, t, :], y[t % 2][:, :], 0.0, X[:, t, :], ALU.max, ALU.add))
                nc.vector.bn_stats(stats[:, t, :], X[:, t, :])

        @block.tensor
        def _(pe):
            pe.wait_ge(wlo_ready, 1)
            for u, (m, c) in enumerate(UNITS):
                c0, c1 = CHUNKS[c]
                if u >= 2:
                    pe.wait_ge(full_ready, u - 1)
                for k in range(KF):
                    ms = slice(m * 128, (m + 1) * 128)
                    last = three(nc, ps_f[u % 2][:, 0:c1 - c0], whi[0][:, k, ms], wlo[0][:, k, ms], oT_hi[:, k, c0:c1], oT_lo[:, k, c0:c1],
                                 k == 0, k == KF - 1)
                last.then_inc(f_done, 1)
            pe.wait_ge(wlo_ready, 2)
            pe.wait_ge(flo_ready, len(UNITS))
            for t in range(NT):
                tok = slice(t * PT, (t + 1) * PT)
                if t >= 2:
                    pe.wait_ge(y_ready, t - 1)
                for k in range(KD):
                    last = three(nc, ps_y[t % 2][:, :], f_hi[:, k, tok], f_lo[:, k, tok], whi[1][:, k, :], wlo[1][:, k, :],
                                 k == 0, k == KD - 1)
                last.then_inc(y_done, 1)


MAX_THRESHOLD = 0.25


def gated_experts(nc, sems, a, X, H, hT_hi, hT_lo, ident, eps_col, stats, out):
    NG = NE + 2
    NY = 4
    sems.next_phase()
    with ExitStack() as ctx:
        def sb(name, shape, dt=F32):
            return ctx.enter_context(nc.sbuf_tensor(name, shape, dt))

        def pb(name, shape, dt=F32):
            return ctx.enter_context(nc.psum_tensor(name, shape, dt))

        def sem(name):
            return sems.new(ctx, "f_" + name)

        wg_raw = sb("wg_raw", [128, KD, NG])
        wg_hi = sb("wg_hi", [128, KD, NG], F32R)
        wg_lo = sb("wg_lo", [128, KD, NG], F32R)
        wt_raw = sb("wt_raw", [128, KD])
        bg = sb("bg", [PT, NG])
        be = sb("be", [NE, D])
        raw = [sb(f"f_raw{i}", [128, KD, D]) for i in range(2)]
        whi = [sb(f"f_whi{i}", [128, KD, D], F32R) for i in range(2)]
        wlo = [sb(f"f_wlo{i}", [128, KD, D], F32R) for i in range(2)]
        logit_T = sb("f_logit_T", [NG, N])
        logit = sb("f_logit", [PT, NT, NG])
        prob = sb("f_prob", [PT, NT, NE])
        peak = sb("f_peak", [PT, NT])
        total = sb("f_total", [PT, NT])
        thr = sb("f_thr", [PT, NT])
        weight = sb("f_weight", [PT, NT, NE])
        weight_T = sb("f_weight_T", [NE, NT, PT])
        ps_turn = [pb(f"f_turn{i}", [128, 4, 128]) for i in range(2)]
        ps_logit = pb("f_ps_logit", [PT, NT, NG])
        ps_y = [pb(f"f_y{i}", [PT, D]) for i in range(NY)]
        g_loaded, thr_loaded = sem("g_loaded"), sem("thr_loaded")
        w_loaded = [sem(f"w_loaded{i}") for i in range(2)]
        pad_made, ghi_ready, glo_ready = sem("pad_made"), sem("ghi_ready"), sem("glo_ready")
        whi_ready, wlo_ready = sem("whi_ready"), sem("wlo_ready")
        logitT_done, logitT_ready = sem("logitT_done"), sem("logitT_ready")
        logits_done, shifted, exped = sem("logits_done"), sem("shifted"), sem("exped")
        weights_ready, wt_turned, wt_ready = sem("weights_ready"), sem("wt_turned"), sem("wt_ready")
        y_done, y_added, stored, step = sem("y_done"), sem("y_added"), sem("stored"), sem("step")
        ln = Norm(nc, sems, ctx, "ln4", X, H, hT_hi, hT_lo, ps_turn, ident, eps_col, stats)
        block = ctx.enter_context(nc.Block())

        @block.sync
        def _(sp):
            sp.dma_start(wg_raw[:, :, 0:NE], a["L1_ffn_W_gate"].rearrange("(k p) e -> p k e", p=128)).then_inc(g_loaded, 16)
            sp.dma_start(wt_raw[:, :], a["L1_ffn_W_thr"]).then_inc(thr_loaded, 16)
            sp.dma_start(bg[:, 0:NE], a["L1_ffn_b_gate"].partition_broadcast(PT)).then_inc(g_loaded, 16)
            sp.dma_start(bg[:, NE:NE + 1], a["L1_ffn_b_thr"].partition_broadcast(PT)).then_inc(g_loaded, 16)
            sp.dma_start(be[:, :], a["L1_ffn_b_exp"]).then_inc(g_loaded, 16)
            for x in range(NE):
                if x >= 2:
                    sp.wait_ge(wlo_ready, x - 1)
                sp.dma_start(raw[x % 2][:, :, :], a["L1_ffn_W_exp"][x].rearrange("(k p) f -> p k f", p=128)).then_inc(w_loaded[x % 2], 16)
            for t in range(NT):
                sp.wait_ge(y_added, NT * NE + t + 1)
                sp.dma_start(out[t * PT:(t + 1) * PT, :], X[:, t, :]).then_inc(stored, 16)
            sp.wait_ge(stored, 16 * NT)

        @block.gpsimd
        def _(pool):
            sems.clear(pool)
            nc.gpsimd.memset(wg_raw[:, :, NE + 1:NG], 0.0).then_inc(pad_made, 1)
            nc.gpsimd.memset(bg[:, NE + 1:NG], 0.0).then_inc(pad_made, 1)
            pool.wait_ge(thr_loaded, 16)
            nc.gpsimd.tensor_copy(wg_raw[:, :, NE], wt_raw[:, :]).then_inc(pad_made, 1)

        @block.scalar
        def _(act):
            ln.scalar(act)
            act.wait_ge(g_loaded, 64)
            act.wait_ge(pad_made, 3)
            nc.scalar.activation(wg_hi[:, :, :], wg_raw[:, :, :], ACT.Copy).then_inc(ghi_ready, 1)

            def split_w(x):
                act.wait_ge(w_loaded[x % 2], 16 * (x // 2 + 1))
                if x >= 2:
                    act.wait_ge(y_done, NT * x)
                nc.scalar.activation(whi[x % 2][:, :, :], raw[x % 2][:, :, :], ACT.Copy).then_inc(whi_ready, 1)

            for c, (c0, c1) in enumerate(CHUNKS):
                act.wait_ge(logitT_done, c + 1)
                nc.scalar.activation(logit_T[:, c0:c1], ps_y[c][0:NG, 0:c1 - c0], ACT.Copy).then_inc(logitT_ready, 1)
            split_w(0)
            act.wait_ge(shifted, 1)
            nc.scalar.activation(prob[:, :, :], logit[:, :, 0:NE], ACT.Exp).then_inc(exped, 1)
            nc.scalar.activation(thr[:, :], logit[:, :, NE], ACT.Exp, scale=-1.0).then_inc(exped, 1)
            for t in range(NT):
                act.wait_ge(wt_turned, t + 1)
                nc.scalar.activation(weight_T[:, t, :], ps_turn[t % 2][0:NE, 0, 0:PT], ACT.Copy).then_inc(wt_ready, 1)
            for x in range(1, NE):
                split_w(x)

        @block.vector
        def _(dve):
            link = chained(dve, step)
            ln.vector(dve, link, measured=True)
            dve.wait_ge(ghi_ready, 1)
            nc.vector.tensor_tensor(wg_lo[:, :, :], wg_raw[:, :, :], wg_hi[:, :, :].bitcast(F32), ALU.subtract).then_inc(glo_ready, 1)

            def split_w(x):
                dve.wait_ge(whi_ready, x + 1)
                nc.vector.tensor_tensor(wlo[x % 2][:, :, :], raw[x % 2][:, :, :], whi[x % 2][:, :, :].bitcast(F32), ALU.subtract).then_inc(wlo_ready, 1)

            def spread(t):
                return t[:, :].unsqueeze(2).to_broadcast([PT, NT, NE])

            split_w(0)
            dve.wait_ge(logits_done, 1)
            link(nc.vector.tensor_tensor(logit[:, :, :], ps_logit[:, :, :], bg[:, :].unsqueeze(1).to_broadcast([PT, NT, NG]), ALU.add))
            link(nc.vector.tensor_reduce(peak[:, :], logit[:, :, 0:NE], AX.X, ALU.max))
            nc.vector.tensor_tensor(logit[:, :, 0:NE], logit[:, :, 0:NE], spread(peak), ALU.subtract).then_inc(shifted, 1)
            dve.wait_ge(exped, 2)
            link(nc.vector.tensor_reduce(total[:, :], prob[:, :, :], AX.X, ALU.add))
            link(nc.vector.reciprocal(total[:, :], total[:, :]))
            link(nc.vector.tensor_tensor(prob[:, :, :], prob[:, :, :], spread(total), ALU.mult))
            link(nc.vector.tensor_scalar(thr[:, :], thr[:, :], 1.0, None, ALU.add))
            link(nc.vector.reciprocal(thr[:, :], thr[:, :]))
            link(nc.vector.tensor_scalar(thr[:, :], thr[:, :], MAX_THRESHOLD, None, ALU.mult))
            link(nc.vector.tensor_tensor(weight[:, :, :], prob[:, :, :], spread(thr), ALU.subtract))
            link(nc.vector.tensor_scalar(weight[:, :, :], weight[:, :, :], 0.0, None, ALU.max))
            link(nc.vector.tensor_reduce(total[:, :], weight[:, :, :], AX.X, ALU.add))
            link(nc.vector.scalar_tensor_tensor(total[:, :], total[:, :], 0.0, total[:, :], ALU.is_equal, ALU.add))
            link(nc.vector.reciprocal(total[:, :], total[:, :]))
            nc.vector.tensor_tensor(weight[:, :, :], weight[:, :, :], spread(total), ALU.mult).then_inc(weights_ready, 1)
            split_w(1)
            for t in range(NT):
                dve.wait_ge(y_done, t + 1)
                nc.vector.tensor_tensor(X[:, t, :], X[:, t, :], ps_y[t % NY][:, :], ALU.add).then_inc(y_added, 1)
            dve.wait_ge(weights_ready, 1)
            for x in range(NE):
                if 1 <= x and x + 1 < NE:
                    split_w(x + 1)
                for t in range(NT):
                    n = NT * (x + 1) + t
                    dve.wait_ge(y_done, n + 1)
                    dve.wait_ge(y_added, n - NT + 1)
                    nc.vector.scalar_tensor_tensor(X[:, t, :], ps_y[n % NY][:, :], weight[:, t, x:x + 1], X[:, t, :],
                                                   ALU.mult, ALU.add).then_inc(y_added, 1)

        @block.tensor
        def _(pe):
            ln.tensor(pe)
            pe.wait_ge(ln.lo_ready, NT)
            pe.wait_ge(glo_ready, 1)
            for c, (c0, c1) in enumerate(CHUNKS):
                for k in range(KD):
                    last = three(nc, ps_y[c][0:NG, 0:c1 - c0], wg_hi[:, k, :], wg_lo[:, k, :], hT_hi[:, k, c0:c1], hT_lo[:, k, c0:c1],
                                 k == 0, k == KD - 1)
                last.then_inc(logitT_done, 1)
            pe.wait_ge(logitT_ready, len(CHUNKS))
            for t in range(NT):
                last = nc.tensor.transpose(ps_logit[:, t, :], logit_T[:, t * PT:(t + 1) * PT], ident[0:NG, 0:NG])
            last.then_inc(logits_done, 1)
            pe.wait_ge(weights_ready, 1)
            for t in range(NT):
                if t >= 2:
                    pe.wait_ge(wt_ready, t - 1)
                nc.tensor.transpose(ps_turn[t % 2][0:NE, 0, 0:PT], weight[:, t, :], ident[0:PT, 0:PT]).then_inc(wt_turned, 1)
            for t in range(NT):
                pe.wait_ge(wt_ready, t + 1)
                if t >= NY:
                    pe.wait_ge(y_added, t - NY + 1)
                nc.tensor.matmul(ps_y[t % NY][:, :], weight_T[:, t, :], be[:, :], start=True, stop=True).then_inc(y_done, 1)
            for x in range(NE):
                pe.wait_ge(wlo_ready, x + 1)
                for t in range(NT):
                    n = NT * (x + 1) + t
                    tok = slice(t * PT, (t + 1) * PT)
                    pe.wait_ge(y_added, n - NY + 1)
                    for k in range(KD):
                        last = three(nc, ps_y[n % NY][:, :], hT_hi[:, k, tok], hT_lo[:, k, tok], whi[x % 2][:, k, :], wlo[x % 2][:, k, :],
                                     k == 0, k == KD - 1)
                    last.then_inc(y_done, 1)


def build(nc, a, outs):
    with ExitStack() as ctx:
        def sb(name, shape, dt=F32):
            return ctx.enter_context(nc.sbuf_tensor(name, shape, dt))

        X = sb("X", [PT, NT, D])
        hT_hi = sb("hT_hi", [128, KD, N], F32R)
        hT_lo = sb("hT_lo", [128, KD, N], F32R)
        ident = sb("ident", [128, 128])
        eps_col = sb("eps_col", [128, 1])
        stats = sb("stats", [PT, NT, 6])
        r = route_tensors(nc, ctx)
        sems = Semaphores(nc)
        with nc.sbuf_tensor("CT", [PT, NT, N], F32) as CT:
            with nc.sbuf_tensor("H1", [PT, NT, D], F32) as H:
                neighbour_mean_layer(nc, sems, a, X, H, hT_hi, hT_lo, ident, eps_col, stats, CT)
            with nc.sbuf_tensor("H2", [PT, NT, D], F32) as H:
                route_and_shared_expert(nc, sems, a, X, H, hT_hi, hT_lo, ident, eps_col, stats, r)
            routed_experts(nc, sems, a, ident, r)
            overfull_experts(nc, sems, a, ident, r)
            combine(nc, sems, X, CT, ident, stats, r)
            with nc.sbuf_tensor("V", [PT, NT, HEADS, 64], F32) as V:
                with nc.sbuf_tensor("H3", [PT, NT, D], F32) as H:
                    project_qkv(nc, sems, a, X, H, hT_hi, hT_lo, ident, eps_col, stats, V, r)
                attention(nc, sems, hT_hi, hT_lo, CT, V, r)
        attention_out(nc, sems, a, X, hT_hi, hT_lo, stats)
        with nc.sbuf_tensor("H4", [PT, NT, D], F32) as H:
            gated_experts(nc, sems, a, X, H, hT_hi, hT_lo, ident, eps_col, stats, outs["out"])


def kernel(**inputs):
    import numpy as _np
    import concourse.bacc as _bacc
    from concourse import mybir as _mybir
    from concourse.bass_utils import run_bass_kernel_spmd as _run

    nc = _bacc.Bacc("TRN2", target_bir_lowering=False, num_devices=1)
    arrays, a = {}, {}
    for name in inputs:
        v = _np.asarray(inputs[name])
        if name in ("L0_gnn_W_self", "L0_gnn_W_neigh"):
            v = v.T
        if name in ("L0_ffn_bs1", "L1_gnn_bq", "L1_gnn_bk", "L1_gnn_ba", "L1_ffn_W_thr"):
            v = v.reshape(-1, 128).T
        if name in ("L0_ffn_b1_sp", "L0_ffn_b1_fq"):
            v = v.reshape(8, 2, 128).transpose(2, 0, 1)
        v = _np.ascontiguousarray(v)
        arrays[f"in_{name}"] = v
        a[name] = nc.dram_tensor(f"in_{name}", v.shape, _mybir.dt.from_np(v.dtype), kind="ExternalInput").ap()
    outs = {"out": nc.dram_tensor("out_0", (N, D), F32, kind="ExternalOutput").ap()}
    build(nc, a, outs)
    r = _run(nc, [arrays], core_ids=[0])
    return r.results[0]["out_0"]
```
